# Optimizing a Trainium2 kernel written in Bass

```python
import numpy as np
import jax
import jax.numpy as jnp

def _softmax(x, axis=-1):
    return jax.nn.softmax(x, axis=axis)

def _gelu(x):
    return jax.nn.gelu(x, approximate=True)

def _silu(x):
    return jax.nn.silu(x)

def _sigmoid(x):
    return jax.nn.sigmoid(x)

def _layernorm(x, axis=-1, eps=1e-05):
    m = jnp.mean(x, axis=axis, keepdims=True)
    v = jnp.var(x, axis=axis, keepdims=True)
    return (x - m) / jnp.sqrt(v + eps)

def _scatter_add(tgt, idx, src, axis=0):
    return tgt.at[idx].add(src)

def _segment_sum(src, seg, n):
    return jax.ops.segment_sum(src, seg, n)
kernel_name = 'mk_seq_preln_d2_jaxref_r8_174791'

def setup_inputs(seed: int=0):
    np.random.seed(seed)
    _w = jnp.asarray

    def _L0_attn_setup():
        import jax, jax.numpy as jnp
        import numpy as np
        D_MODEL = 128
        N_HEADS = 16
        HEAD_DIM = D_MODEL // N_HEADS
        D_LATENT = 32
        LAMBDA_DECAY = 0.01
        TIME_STEP = 0.01
        CLAMP = 10000.0

        def _reference_tuple_inner(x, Wq, Wk, Wv, Wo, W_down_kv, W_up_k, W_up_v):
            B, S, _ = x.shape
            q = x @ Wq
            k = x @ Wk
            v = x @ Wv
            latent_kv = (k + v) @ W_down_kv
            k_rec = latent_kv @ W_up_k
            v_rec = latent_kv @ W_up_v

            def heads(t):
                return t.reshape(B, S, N_HEADS, HEAD_DIM).transpose(0, 2, 1, 3)
            qh, kh, vh = (heads(q), heads(k_rec), heads(v_rec))
            scale = 1.0 / (jnp.sqrt(jnp.float32(D_MODEL)) + 1e-08)
            scores = jnp.einsum('bhqd,bhkd->bhqk', qh, kh) * scale
            scores = jnp.clip(jnp.nan_to_num(scores, nan=-1000000000.0), -CLAMP, CLAMP)
            idx = jnp.arange(S, dtype=jnp.float32)
            decay = jnp.exp(-LAMBDA_DECAY * TIME_STEP * jnp.abs(idx[:, None] - idx[None, :]))
            scores = scores * decay[None, None, :, :]
            scores = jnp.clip(jnp.nan_to_num(scores, nan=-1000000000.0), -CLAMP, CLAMP)
            attn = jax.nn.softmax(scores, axis=-1)
            out = jnp.einsum('bhqk,bhkd->bhqd', attn, vh)
            out = out.transpose(0, 2, 1, 3).reshape(B, S, D_MODEL)
            return (out @ Wo, latent_kv)
        key = jax.random.key(seed)
        ks = jax.random.split(key, 8)
        B, S = (2, 256)

        def w(k, i, o):
            return jax.random.normal(k, (i, o), dtype=jnp.float32) * 0.02
        return {'x': jax.random.normal(ks[0], (B, S, D_MODEL), dtype=jnp.float32), 'Wq': w(ks[1], D_MODEL, D_MODEL), 'Wk': w(ks[2], D_MODEL, D_MODEL), 'Wv': w(ks[3], D_MODEL, D_MODEL), 'Wo': w(ks[4], D_MODEL, D_MODEL), 'W_down_kv': w(ks[5], D_MODEL, D_LATENT), 'W_up_k': w(ks[6], D_LATENT, D_MODEL), 'W_up_v': w(ks[7], D_LATENT, D_MODEL)}
    _L0_attn_in = _L0_attn_setup()

    def _L0_ffn_setup():
        import jax, jax.numpy as jnp
        import numpy as np
        NUM_EXPERTS = 160
        TOP_K = 8
        ROUTED_SCALE = 2.5
        HIDDEN = 128
        INTER = 64
        key = jax.random.key(seed)
        ks = jax.random.split(key, 7)
        B, S = (1, 256)
        return {'hidden_states': jax.random.normal(ks[0], (B, S, HIDDEN), dtype=jnp.float32), 'router_w': jax.random.normal(ks[1], (NUM_EXPERTS, HIDDEN), dtype=jnp.float32) * 0.02, 'expert_bias': jnp.zeros((NUM_EXPERTS,), dtype=jnp.float32), 'w_gate': jax.random.normal(ks[2], (NUM_EXPERTS, INTER, HIDDEN), dtype=jnp.float32) * 0.02, 'w_down': jax.random.normal(ks[3], (NUM_EXPERTS, HIDDEN, INTER), dtype=jnp.float32) * 0.02, 'w_gate_shared': jax.random.normal(ks[4], (INTER, HIDDEN), dtype=jnp.float32) * 0.02, 'w_down_shared': jax.random.normal(ks[5], (HIDDEN, INTER), dtype=jnp.float32) * 0.02}
    _L0_ffn_in = _L0_ffn_setup()

    def _L1_attn_setup():
        import jax, jax.numpy as jnp
        import numpy as np
        B, S, D = (4, 512, 128)
        CHUNK = 64
        MAX_LR = 0.2
        MIN_DECAY = 0.5
        MAX_NORM = 30.0
        NORM_EPS = 1e-05

        def _forward(x, M_init, eta_w, eta_b, alpha_w, alpha_b, gate_w, gate_b, vg_w1, vg_w2):
            b, s, d = x.shape
            n_ch = s // CHUNK

            def value_gen(y):
                h = jax.nn.silu(y @ vg_w1.T) @ vg_w2.T
                return h + y
            x_chunks = x.reshape(b, n_ch, CHUNK, d).transpose(1, 0, 2, 3)
            M0 = jnp.broadcast_to(M_init, (b, d, d))

            def step(M, chunk):
                eta_tok = jax.nn.sigmoid(chunk @ eta_w + eta_b[0]) * MAX_LR
                alpha_tok = MIN_DECAY + jax.nn.sigmoid(chunk @ alpha_w + alpha_b[0]) * (1.0 - MIN_DECAY)
                eta = eta_tok.mean(axis=1)[:, None, None]
                alpha = alpha_tok.mean(axis=1)[:, None, None]
                outputs = jnp.einsum('bci,boi->bco', chunk, M)
                nrm = jnp.sqrt(jnp.sum(chunk * chunk, axis=-1, keepdims=True))
                keys = chunk / jnp.maximum(nrm, NORM_EPS)
                k_mean = keys.mean(axis=1)
                v_target = value_gen(outputs).mean(axis=1)
                Mk = jnp.einsum('boi,bi->bo', M, k_mean)
                err = v_target - Mk
                update = err[:, :, None] * k_mean[:, None, :]
                M_new = alpha * M + eta * update
                gate = jax.nn.sigmoid(k_mean @ gate_w + gate_b[0])[:, None, None]
                M_new = gate * M_new + (1.0 - gate) * M
                M_norm = jnp.sqrt(jnp.sum(M_new * M_new, axis=(-2, -1), keepdims=True))
                scale = jnp.minimum(MAX_NORM / (M_norm + 1e-06), 1.0)
                return (M_new * scale, outputs)
            M_final, outs = jax.lax.scan(step, M0, x_chunks)
            outs = outs.transpose(1, 0, 2, 3).reshape(b, s, d)
            final_out = value_gen(outs)
            return (final_out, M_final)

        def _reference_tuple_inner(x, M_init, eta_w, eta_b, alpha_w, alpha_b, gate_w, gate_b, vg_w1, vg_w2):
            return _forward(x, M_init, eta_w, eta_b, alpha_w, alpha_b, gate_w, gate_b, vg_w1, vg_w2)
        key = jax.random.key(seed)
        ks = jax.random.split(key, 10)
        return {'x': jax.random.normal(ks[0], (B, S, D), jnp.float32), 'M_init': jax.random.normal(ks[1], (D, D), jnp.float32) * 0.02, 'eta_w': jax.random.normal(ks[2], (D,), jnp.float32) * 0.02, 'eta_b': jax.random.normal(ks[3], (1,), jnp.float32), 'alpha_w': jax.random.normal(ks[4], (D,), jnp.float32) * 0.02, 'alpha_b': jax.random.normal(ks[5], (1,), jnp.float32), 'gate_w': jax.random.normal(ks[6], (D,), jnp.float32) * 0.02, 'gate_b': jax.random.normal(ks[7], (1,), jnp.float32), 'vg_w1': jax.random.normal(ks[8], (D, D), jnp.float32) * 0.02, 'vg_w2': jax.random.normal(ks[9], (D, D), jnp.float32) * 0.02}
    _L1_attn_in = _L1_attn_setup()

    def _L1_ffn_setup():
        import jax, jax.numpy as jnp
        import numpy as np
        N_EXPERTS = 8
        N_GROUP = 4
        TOPK_GROUP = 2
        TOP_K = 2
        HIDDEN = 128
        INTER = 256
        B, S = (1, 128)

        def _grouped_topk(scores):
            T, E = scores.shape
            per_group = E // N_GROUP
            group_scores = scores.reshape(T, N_GROUP, per_group).max(-1)
            _, gidx = jax.lax.top_k(group_scores, TOPK_GROUP)
            gmask = jnp.zeros((T, N_GROUP), scores.dtype).at[jnp.arange(T)[:, None], gidx].set(1.0)
            smask = jnp.repeat(gmask, per_group, axis=1)
            masked = jnp.where(smask > 0, scores, 0.0)
            topk_w, topk_ids = jax.lax.top_k(masked, TOP_K)
            topk_w = topk_w / topk_w.sum(-1, keepdims=True)
            return (topk_ids, topk_w)
        key = jax.random.key(seed)
        k1, k2, k3, k4 = jax.random.split(key, 4)
        return {'hidden_states': jax.random.normal(k1, (B, S, HIDDEN), jnp.float32), 'gate_w': jax.random.normal(k2, (N_EXPERTS, HIDDEN), jnp.float32) * 0.02, 'w13_weight': jax.random.normal(k3, (N_EXPERTS, 2 * INTER, HIDDEN), jnp.float32) * 0.02, 'w2_weight': jax.random.normal(k4, (N_EXPERTS, HIDDEN, INTER), jnp.float32) * 0.02}
    _L1_ffn_in = _L1_ffn_setup()
    _d = {'L0_attn_x': _L0_attn_in['x'], 'L0_attn_Wq': _L0_attn_in['Wq'], 'L0_attn_Wk': _L0_attn_in['Wk'], 'L0_attn_Wv': _L0_attn_in['Wv'], 'L0_attn_Wo': _L0_attn_in['Wo'], 'L0_attn_W_down_kv': _L0_attn_in['W_down_kv'], 'L0_attn_W_up_k': _L0_attn_in['W_up_k'], 'L0_attn_W_up_v': _L0_attn_in['W_up_v'], 'L0_ffn_router_w': _L0_ffn_in['router_w'], 'L0_ffn_expert_bias': _L0_ffn_in['expert_bias'], 'L0_ffn_w_gate': _L0_ffn_in['w_gate'], 'L0_ffn_w_down': _L0_ffn_in['w_down'], 'L0_ffn_w_gate_shared': _L0_ffn_in['w_gate_shared'], 'L0_ffn_w_down_shared': _L0_ffn_in['w_down_shared'], 'L1_attn_M_init': _L1_attn_in['M_init'], 'L1_attn_eta_w': _L1_attn_in['eta_w'], 'L1_attn_eta_b': _L1_attn_in['eta_b'], 'L1_attn_alpha_w': _L1_attn_in['alpha_w'], 'L1_attn_alpha_b': _L1_attn_in['alpha_b'], 'L1_attn_gate_w': _L1_attn_in['gate_w'], 'L1_attn_gate_b': _L1_attn_in['gate_b'], 'L1_attn_vg_w1': _L1_attn_in['vg_w1'], 'L1_attn_vg_w2': _L1_attn_in['vg_w2'], 'L1_ffn_gate_w': _L1_ffn_in['gate_w'], 'L1_ffn_w13_weight': _L1_ffn_in['w13_weight'], 'L1_ffn_w2_weight': _L1_ffn_in['w2_weight']}
    _x0 = _d['L0_attn_x']
    _d['L0_attn_x'] = jax.random.normal(jax.random.fold_in(jax.random.key(seed), 1), (2, 1024, 128), dtype=_x0.dtype)
    del _x0
    return _d

def reference(L0_attn_x, L0_attn_Wq, L0_attn_Wk, L0_attn_Wv, L0_attn_Wo, L0_attn_W_down_kv, L0_attn_W_up_k, L0_attn_W_up_v, L0_ffn_router_w, L0_ffn_expert_bias, L0_ffn_w_gate, L0_ffn_w_down, L0_ffn_w_gate_shared, L0_ffn_w_down_shared, L1_attn_M_init, L1_attn_eta_w, L1_attn_eta_b, L1_attn_alpha_w, L1_attn_alpha_b, L1_attn_gate_w, L1_attn_gate_b, L1_attn_vg_w1, L1_attn_vg_w2, L1_ffn_gate_w, L1_ffn_w13_weight, L1_ffn_w2_weight):

    def _L0_attn_ref(x, Wq, Wk, Wv, Wo, W_down_kv, W_up_k, W_up_v):
        import jax, jax.numpy as jnp
        import numpy as np
        D_MODEL = 128
        N_HEADS = 16
        HEAD_DIM = D_MODEL // N_HEADS
        D_LATENT = 32
        LAMBDA_DECAY = 0.01
        TIME_STEP = 0.01
        CLAMP = 10000.0

        def _reference_tuple_inner(x, Wq, Wk, Wv, Wo, W_down_kv, W_up_k, W_up_v):
            B, S, _ = x.shape
            q = x @ Wq
            k = x @ Wk
            v = x @ Wv
            latent_kv = (k + v) @ W_down_kv
            k_rec = latent_kv @ W_up_k
            v_rec = latent_kv @ W_up_v

            def heads(t):
                return t.reshape(B, S, N_HEADS, HEAD_DIM).transpose(0, 2, 1, 3)
            qh, kh, vh = (heads(q), heads(k_rec), heads(v_rec))
            scale = 1.0 / (jnp.sqrt(jnp.float32(D_MODEL)) + 1e-08)
            scores = jnp.einsum('bhqd,bhkd->bhqk', qh, kh) * scale
            scores = jnp.clip(jnp.nan_to_num(scores, nan=-1000000000.0), -CLAMP, CLAMP)
            idx = jnp.arange(S, dtype=jnp.float32)
            decay = jnp.exp(-LAMBDA_DECAY * TIME_STEP * jnp.abs(idx[:, None] - idx[None, :]))
            scores = scores * decay[None, None, :, :]
            scores = jnp.clip(jnp.nan_to_num(scores, nan=-1000000000.0), -CLAMP, CLAMP)
            attn = jax.nn.softmax(scores, axis=-1)
            out = jnp.einsum('bhqk,bhkd->bhqd', attn, vh)
            out = out.transpose(0, 2, 1, 3).reshape(B, S, D_MODEL)
            return (out @ Wo, latent_kv)
        return _reference_tuple_inner(x, Wq, Wk, Wv, Wo, W_down_kv, W_up_k, W_up_v)[0]

    def _L0_ffn_ref(hidden_states, router_w, expert_bias, w_gate, w_down, w_gate_shared, w_down_shared):
        import jax, jax.numpy as jnp
        import numpy as np
        NUM_EXPERTS = 160
        TOP_K = 8
        ROUTED_SCALE = 2.5
        HIDDEN = 128
        INTER = 64
        B, S, H = hidden_states.shape
        x = hidden_states.reshape(-1, H)
        T = x.shape[0]
        logits = x @ router_w.T + expert_bias[None, :]
        probs = jax.nn.sigmoid(logits)
        top_w, top_idx = jax.lax.top_k(probs, TOP_K)
        top_w = top_w / (jnp.sum(top_w, axis=-1, keepdims=True) + 1e-09)
        top_w = top_w * ROUTED_SCALE
        combine = jnp.zeros((T, NUM_EXPERTS), dtype=x.dtype)
        combine = combine.at[jnp.arange(T)[:, None], top_idx].set(top_w)
        h1 = jax.nn.silu(jnp.einsum('th,eih->eti', x, w_gate))
        h1w = h1 * combine.T[:, :, None]
        routed = jnp.einsum('eti,ehi->th', h1w, w_down)
        shared = jax.nn.silu(x @ w_gate_shared.T) @ w_down_shared.T
        return (routed + shared).reshape(B, S, H)

    def _L1_attn_ref(x, M_init, eta_w, eta_b, alpha_w, alpha_b, gate_w, gate_b, vg_w1, vg_w2):
        import jax, jax.numpy as jnp
        import numpy as np
        B, S, D = (4, 512, 128)
        CHUNK = 64
        MAX_LR = 0.2
        MIN_DECAY = 0.5
        MAX_NORM = 30.0
        NORM_EPS = 1e-05

        def _forward(x, M_init, eta_w, eta_b, alpha_w, alpha_b, gate_w, gate_b, vg_w1, vg_w2):
            b, s, d = x.shape
            n_ch = s // CHUNK

            def value_gen(y):
                h = jax.nn.silu(y @ vg_w1.T) @ vg_w2.T
                return h + y
            x_chunks = x.reshape(b, n_ch, CHUNK, d).transpose(1, 0, 2, 3)
            M0 = jnp.broadcast_to(M_init, (b, d, d))

            def step(M, chunk):
                eta_tok = jax.nn.sigmoid(chunk @ eta_w + eta_b[0]) * MAX_LR
                alpha_tok = MIN_DECAY + jax.nn.sigmoid(chunk @ alpha_w + alpha_b[0]) * (1.0 - MIN_DECAY)
                eta = eta_tok.mean(axis=1)[:, None, None]
                alpha = alpha_tok.mean(axis=1)[:, None, None]
                outputs = jnp.einsum('bci,boi->bco', chunk, M)
                nrm = jnp.sqrt(jnp.sum(chunk * chunk, axis=-1, keepdims=True))
                keys = chunk / jnp.maximum(nrm, NORM_EPS)
                k_mean = keys.mean(axis=1)
                v_target = value_gen(outputs).mean(axis=1)
                Mk = jnp.einsum('boi,bi->bo', M, k_mean)
                err = v_target - Mk
                update = err[:, :, None] * k_mean[:, None, :]
                M_new = alpha * M + eta * update
                gate = jax.nn.sigmoid(k_mean @ gate_w + gate_b[0])[:, None, None]
                M_new = gate * M_new + (1.0 - gate) * M
                M_norm = jnp.sqrt(jnp.sum(M_new * M_new, axis=(-2, -1), keepdims=True))
                scale = jnp.minimum(MAX_NORM / (M_norm + 1e-06), 1.0)
                return (M_new * scale, outputs)
            M_final, outs = jax.lax.scan(step, M0, x_chunks)
            outs = outs.transpose(1, 0, 2, 3).reshape(b, s, d)
            final_out = value_gen(outs)
            return (final_out, M_final)

        def _reference_tuple_inner(x, M_init, eta_w, eta_b, alpha_w, alpha_b, gate_w, gate_b, vg_w1, vg_w2):
            return _forward(x, M_init, eta_w, eta_b, alpha_w, alpha_b, gate_w, gate_b, vg_w1, vg_w2)
        return _reference_tuple_inner(x, M_init, eta_w, eta_b, alpha_w, alpha_b, gate_w, gate_b, vg_w1, vg_w2)[0]

    def _L1_ffn_ref(hidden_states, gate_w, w13_weight, w2_weight):
        import jax, jax.numpy as jnp
        import numpy as np
        N_EXPERTS = 8
        N_GROUP = 4
        TOPK_GROUP = 2
        TOP_K = 2
        HIDDEN = 128
        INTER = 256
        B, S = (1, 128)

        def _grouped_topk(scores):
            T, E = scores.shape
            per_group = E // N_GROUP
            group_scores = scores.reshape(T, N_GROUP, per_group).max(-1)
            _, gidx = jax.lax.top_k(group_scores, TOPK_GROUP)
            gmask = jnp.zeros((T, N_GROUP), scores.dtype).at[jnp.arange(T)[:, None], gidx].set(1.0)
            smask = jnp.repeat(gmask, per_group, axis=1)
            masked = jnp.where(smask > 0, scores, 0.0)
            topk_w, topk_ids = jax.lax.top_k(masked, TOP_K)
            topk_w = topk_w / topk_w.sum(-1, keepdims=True)
            return (topk_ids, topk_w)
        Bm, Sm, H = hidden_states.shape
        x = hidden_states.reshape(-1, H)
        T = x.shape[0]
        scores = jax.nn.softmax(x @ gate_w.T, axis=-1)
        topk_ids, topk_w = _grouped_topk(scores)
        combine = jnp.zeros((T, N_EXPERTS), x.dtype).at[jnp.arange(T)[:, None], topk_ids].add(topk_w)
        gu = jnp.einsum('th,eih->tei', x, w13_weight)
        gate, up = (gu[..., :INTER], gu[..., INTER:])
        act = jax.nn.silu(gate) * up
        act = act * combine[:, :, None]
        out = jnp.einsum('tei,ehi->th', act, w2_weight)
        return out.reshape(Bm, Sm, H)
    x = L0_attn_x
    x = x + _L0_attn_ref(_layernorm(x, axis=-1), L0_attn_Wq, L0_attn_Wk, L0_attn_Wv, L0_attn_Wo, L0_attn_W_down_kv, L0_attn_W_up_k, L0_attn_W_up_v)
    x = x + _L0_ffn_ref(_layernorm(x, axis=-1), L0_ffn_router_w, L0_ffn_expert_bias, L0_ffn_w_gate, L0_ffn_w_down, L0_ffn_w_gate_shared, L0_ffn_w_down_shared)
    x = x + _L1_attn_ref(_layernorm(x, axis=-1), L1_attn_M_init, L1_attn_eta_w, L1_attn_eta_b, L1_attn_alpha_w, L1_attn_alpha_b, L1_attn_gate_w, L1_attn_gate_b, L1_attn_vg_w1, L1_attn_vg_w2)
    x = x + _L1_ffn_ref(_layernorm(x, axis=-1), L1_ffn_gate_w, L1_ffn_w13_weight, L1_ffn_w2_weight)
    return x

_drawn_inputs = setup_inputs


def setup_inputs(seed=0):
    import zlib

    import numpy as np

    out = dict(_drawn_inputs(seed))
    spreads = {'L0_ffn_expert_bias': (0.0, 0.573)}
    factors = {'L0_attn_Wq': 8.0,
     'L0_attn_Wk': 8.0,
     'L0_attn_Wv': 8.0,
     'L0_attn_Wo': 8.0,
     'L0_attn_W_down_kv': 8.0,
     'L0_attn_W_up_k': 8.0,
     'L0_attn_W_up_v': 8.0,
     'L0_ffn_router_w': 3.647,
     'L0_ffn_w_gate': 3.483,
     'L0_ffn_w_down': 3.468,
     'L0_ffn_w_gate_shared': 3.083,
     'L0_ffn_w_down_shared': 3.042,
     'L1_attn_eta_w': 64.0,
     'L1_attn_alpha_w': 8.0,
     'L1_attn_gate_w': 64.0,
     'L1_attn_vg_w1': 8.0,
     'L1_attn_vg_w2': 8.0,
     'L1_ffn_gate_w': 8.0,
     'L1_ffn_w13_weight': 8.0,
     'L1_ffn_w2_weight': 8.0}
    for name, (base, spread) in spreads.items():
        noise = np.random.default_rng([zlib.crc32(name.encode()), seed]).standard_normal(out[name].shape)
        drawn = base * np.exp(spread * noise) if base else spread * noise
        out[name] = jnp.asarray(drawn.astype(out[name].dtype))
    for name, factor in factors.items():
        out[name] = (out[name] * factor).astype(out[name].dtype)
    return out
```

```python
from contextlib import ExitStack

import concourse.bass as bass
import numpy as np
from concourse import mybir

F32 = mybir.dt.float32
BF16 = mybir.dt.bfloat16
I32 = mybir.dt.int32
ALU = mybir.AluOpType
ACT = mybir.ActivationFunctionType
AX = mybir.AxisListType

P = 128
B, S, D = 2, 1024, 128
T = B * S
NT = T // P
G = 4
GW = T // G
TPG = NT // G
H, HD = 16, 8
NH = B * H
QT = S // P
LAT = 32
PAIRS = 9
CLAMP = 10000.0
DECAY = 0.01 * 0.01
SCALE = 1.0 / (float(np.sqrt(np.float32(D))) + 1e-8)
EPS = 1e-5
NE, EI, TOPK = 160, 64, 8
MT_N = NE * EI // P
ROUTED = 2.5
CH = 64
NCH = S // CH
MAX_LR, MIN_DECAY, MAX_NORM, NORM_EPS = 0.2, 0.5, 30.0, 1e-5
NE2, FI2 = 8, 256
FT_N = NE2 * FI2 // P
TW = 2 * S - P
CREDIT = 2


class Link:

    def __init__(self, eng, sem):
        self.eng, self.sem, self.n, self.turn = eng, sem, 0, 0

    def sign(self, ins):
        ins.then_inc(self.sem, 1)
        self.n += 1
        return ins

    def wait(self):
        self.eng.wait_ge(self.sem, self.n + self.turn)

    def __call__(self, ins):
        self.sign(ins)
        self.wait()
        return ins

    def end_loop(self, turns, per_turn):
        self.n, self.turn = self.n + (turns - 1) * per_turn, 0


def build(nc, a, out):
    with ExitStack() as ctx:
        def sb(name, shape, dt=F32):
            return ctx.enter_context(nc.sbuf_tensor(name, shape, dt))

        def sem(name):
            return ctx.enter_context(nc.semaphore(name))

        def dram(name, shape, dt):
            return nc.dram_tensor(name, shape, dt, kind="Internal").ap()

        bank01 = ctx.enter_context(nc.psum_tensor("bank01", [P, 1024], F32))
        bank23 = ctx.enter_context(nc.psum_tensor("bank23", [P, 1024], F32))
        bank45 = ctx.enter_context(nc.psum_tensor("bank45", [P, 1024], F32))
        bank67 = ctx.enter_context(nc.psum_tensor("bank67", [P, 1024], F32))
        wide = [bank01, bank23, bank45, bank67]

        def bank(n):
            return wide[n // 2][:, (n % 2) * 512:(n % 2) * 512 + 512]

        x = sb("x", [P, NT, D])
        xn = sb("xn", [P, NT, D])
        xnT = sb("xnT", [P, T])
        stats = sb("stats", [P, NT, 6])
        mv = sb("mv", [P, NT, 2])
        rstd = sb("rstd", [P, NT])
        ident = sb("ident", [P, P])
        half = sb("half", [P, NT])
        wq = sb("wq", [P, D])
        wk = sb("wk", [P, D])
        wv = sb("wv", [P, D])
        wo = sb("wo", [P, D])
        w_down = sb("w_down", [P, LAT])
        w_up = sb("w_up", [LAT, 2 * D])
        big = sb("big", [P, 4 * T])
        kvT = big[:, 0:512]
        latT = big[0:LAT, 512:1024]
        qk_f = big[:, 1024:2048].rearrange("p (w t) -> p w t", w=2)
        qk_r = big[:, 2048:3072].rearrange("p (w t) -> p w t", w=2)
        qk_part = sb("qk_part", [P, 2, 3, GW], BF16)
        v_heads = sb("v_heads", [P, NH, QT, HD])
        o_heads = sb("o_heads", [P, NH, QT, HD])
        q_stack = [sb(f"q_stack{u}", [P, S], BF16) for u in range(2)]
        k_stack = [sb(f"k_stack{u}", [P, S], BF16) for u in range(2)]
        v_cur = [sb(f"v_cur{u}", [P, QT * HD]) for u in range(2)]
        decay = sb("decay", [P, TW])
        sc = [sb(f"sc{u}", [P, S]) for u in range(2)]
        pr = [sb(f"pr{u}", [P, S]) for u in range(2)]
        prT = [sb(f"prT{u}", [P, S]) for u in range(2)]
        row = sb("row", [P, 2, 4])
        oT = big[:, 0:T]

        o_tok = big[:, T:2 * T].rearrange("p (t d) -> p t d", t=NT)
        v_flat = v_heads[:, :, :, :].rearrange("p n t d -> p (n t d)")
        o_flat = o_heads[:, :, :, :].rearrange("p n t d -> p (n t d)")
        distance = big[:, 2 * T:2 * T + TW].bitcast(I32)

        w_router = sb("w_router", [P, NE])
        b_router = sb("b_router", [P, NE])
        w_shared = sb("w_shared", [P, EI])
        wd_shared = sb("wd_shared", [EI, D])
        gates = big[:, 2 * T:2 * T + NT * NE].rearrange("p (t e) -> p t e", t=NT)
        rest = sb("rest", [P, TPG, NE])
        top = sb("top", [P, NT, 8])
        top_sum = sb("top_sum", [P, NT])
        top_inv = sb("top_inv", [P, NT])
        cT = big[:, 0:2 * T].rearrange("p (a t) -> p a t", a=2)
        c_part = sb("c_part", [P, 2, 3, GW], BF16)
        c_dram = dram("c_parts", [NE * 3, T], BF16)
        spread = sb("spread", [P, P], BF16)
        c_rows = [sb(f"c_rows{u}", [P, T], BF16) for u in range(2)]
        w_exp = [sb(f"w_exp{u}", [P, 2 * D]) for u in range(2)]
        act_out = [sb(f"act_out{u}", [P, GW]) for u in range(2)]
        hid = [sb(f"hid{u}", [P, GW]) for u in range(2)]
        accT = big[:, 0:T]

        w_tok = sb("w_tok", [P, 3])
        b_tok = sb("b_tok", [1, 3])
        m0 = sb("m0", [P, D])
        vg1T = sb("vg1T", [P, D])
        vg2 = sb("vg2", [P, D])
        vg2T = sb("vg2T", [P, D])
        ones = sb("ones", [P, P])
        root = sb("root", [P, NT])
        state = [sb(f"state{b}", [P, 2 * D]) for b in range(B)]
        kept = [sb(f"kept{b}", [P, 2 * D]) for b in range(B)]
        vg2_cat = sb("vg2_cat", [P, 2 * D])
        tok = big[0:1, 0:2 * T]
        squares = big[:, 2 * T:3 * T]
        inv_norm = sb("inv_norm", [P, NT])
        by_half = sb("by_half", [P, NT, 2])
        x_mean = sb("x_mean", [P, B * NCH])
        k_mean = sb("k_mean", [P, B * NCH])
        one_row = sb("one_row", [1, 6 * B * NCH])
        steps = sb("steps", [P, NCH, B, 3])
        steps_flat = steps[:, :, :, :].rearrange("p n b c -> p (n b c)")
        step = [sb(f"step{u}", [P, B * 3]) for u in range(2)]
        silu_z = [sb(f"silu_z{b}", [P, CH]) for b in range(B)]
        h_sum = [sb(f"h_sum{b}", [P, 1]) for b in range(B)]
        m_sq = sb("m_sq", [P, B, D])
        m_norm = sb("m_norm", [P, 4, B])
        memT = big[:, 3 * T:4 * T]

        def across(ap, n):
            return bass.AP(ap.tensor, ap.offset, [list(ap.ap[0]), [0, n]])

        w_gate2 = sb("w_gate2", [P, NE2])
        r_max = sb("r_max", [P, NT])
        r_sum = sb("r_sum", [P, NT])
        soft = sb("soft", [P, NT, NE2])
        padded = sb("padded", [P, 2, NT, 16])
        best = sb("best", [P, 2, NT, 8])
        taken = sb("taken", [P, 2, NT, 8])
        marked = sb("marked", [P, 2, NT, 16])
        combine2 = sb("combine2", [P, NT, NE2])
        c2T = big[0:NE2, 0:T]
        c2_dram = dram("c2_parts", [NE2 * 3, T], BF16)
        spread2 = sb("spread2", [P, P], BF16)
        w_ffn = [sb(f"w_ffn{u}", [P, 3 * D]) for u in range(2)]
        gated = [sb(f"gated{u}", [P, GW]) for u in range(2)]

        q_dram = dram("q_parts", [3, NH * HD, S], BF16)
        k_dram = dram("k_parts", [3, NH * HD, S], BF16)

        x_loaded = sem("x_loaded")
        w_loaded = sem("w_loaded")
        consts = sem("consts")
        table = sem("table")
        dve_link = sem("dve_link")
        act_link = sem("act_link")
        pool_link = sem("pool_link")
        var_ready = sem("var_ready")
        rstd_ready = sem("rstd_ready")
        xn_ready = sem("xn_ready")
        xnT_psum = sem("xnT_psum")
        xnT_ready = sem("xnT_ready")
        stored = sem("stored")
        q_psum = sem("q_psum")
        kv_psum = sem("kv_psum")
        kv_ready = sem("kv_ready")
        lat_psum = sem("lat_psum")
        lat_ready = sem("lat_ready")
        k_psum = sem("k_psum")
        v_psum = sem("v_psum")
        q_ready = sem("q_ready")
        k_ready = sem("k_ready")
        v_ready = sem("v_ready")
        parts_ready = sem("parts_ready")
        parts_saved = sem("parts_saved")
        stacks_zero = sem("stacks_zero")
        stacks_loaded = [sem(f"stacks_loaded{u}") for u in range(2)]
        s_psum = sem("s_psum")
        s_clamped = sem("s_clamped")
        max_ready = sem("max_ready")
        exp_ready = sem("exp_ready")
        prT_psum = sem("prT_psum")
        prT_ready = sem("prT_ready")
        o_psum = sem("o_psum")
        o_ready = sem("o_ready")
        o_all = sem("o_all")
        oT_psum = sem("oT_psum")
        oT_ready = sem("oT_ready")
        y_psum = sem("y_psum")
        x_ready = sem("x_ready")
        w3_loaded = sem("w3_loaded")
        logit2_psum = sem("logit2_psum")
        shifted = sem("shifted")
        exp2_ready = sem("exp2_ready")
        combine2_ready = sem("combine2_ready")
        c2T_psum = sem("c2T_psum")
        c2T_ready = sem("c2T_ready")
        c2_split = sem("c2_split")
        c2_saved = sem("c2_saved")
        ffn_zero = sem("ffn_zero")
        ffn_loaded = [sem(f"ffn_loaded{u}") for u in range(2)]
        gate_z = sem("gate_z")
        up_z = sem("up_z")
        c2_psum = sem("c2_psum")
        silu2_ready = sem("silu2_ready")
        gated_ready = sem("gated_ready")
        hid2_ready = sem("hid2_ready")
        down2_done = sem("down2_done")
        acc2_done = sem("acc2_done")
        accT2_ready = sem("accT2_ready")
        acc2_psum = sem("acc2_psum")
        w2_loaded = sem("w2_loaded")
        tok_psum = sem("tok_psum")
        tok_ready = sem("tok_ready")
        sq_ready = sem("sq_ready")
        root_ready = sem("root_ready")
        by_half_ready = sem("by_half_ready")
        km_psum = sem("km_psum")
        km_ready = sem("km_ready")
        gate_psum = sem("gate_psum")
        gate_row = sem("gate_row")
        scalars_ready = sem("scalars_ready")
        scalars_psum = sem("scalars_psum")
        steps_ready = sem("steps_ready")
        fold_psum = sem("fold_psum")
        fold_ready = sem("fold_ready")
        step_ready = sem("step_ready")
        state_ready = [sem(f"state_ready{b}") for b in range(B)]
        mz_psum = [sem(f"mz_psum{b}") for b in range(B)]
        mz_silu = [sem(f"mz_silu{b}") for b in range(B)]
        err_psum = [sem(f"err_psum{b}") for b in range(B)]
        out_psum = [sem(f"out_psum{b}") for b in range(B)]
        out_taken = [sem(f"out_taken{b}") for b in range(B)]
        rows_ready = sem("rows_ready")
        norm_psum = sem("norm_psum")
        norm_sq = sem("norm_sq")
        norm_ready = sem("norm_ready")
        mem_psum = sem("mem_psum")
        w1_loaded = sem("w1_loaded")
        shared_psum = sem("shared_psum")
        shared_act = sem("shared_act")
        shared_down = sem("shared_down")
        logit_psum = sem("logit_psum")
        logit_ready = sem("logit_ready")
        gate_ready = sem("gate_ready")
        combine_ready = sem("combine_ready")
        cT_psum = sem("cT_psum")
        cT_ready = sem("cT_ready")
        c_split = sem("c_split")
        c_split_b = sem("c_split_b")
        c_saved = sem("c_saved")
        moe_zero = sem("moe_zero")
        exp_loaded = [sem(f"exp_loaded{u}") for u in range(2)]
        z_psum = sem("z_psum")
        silu_ready = sem("silu_ready")
        cb_psum = sem("cb_psum")
        hid_ready = sem("hid_ready")
        down_done = sem("down_done")
        acc_done = sem("acc_done")
        accT_ready = sem("accT_ready")
        acc_psum = sem("acc_psum")

        def x_dram(t):
            return t.rearrange("b (t p) d -> p (b t) d", p=P)

        def ready(eng, s, n):
            eng.wait_ge(s, n + (1 + CREDIT))

        def free(eng, s, n, buffers=2):
            eng.wait_ge(s, n + (1 + CREDIT - buffers))

        block = ctx.enter_context(nc.Block())

        @block.sync
        def _(sp):
            for g in range(G):
                ts = slice(g * TPG, (g + 1) * TPG)
                sp.dma_start(x[:, ts, :], x_dram(a["x"])[:, ts, :]).then_inc(x_loaded, 16)
            for dst, src in ((wq[:], "wq"), (wk[:], "wk"), (wv[:], "wv"), (wo[:], "wo"), (w_down[:], "w_down"),
                             (w_up[:, 0:D], "w_up_k"), (w_up[:, D:2 * D], "w_up_v")):
                sp.dma_start(dst, a[src]).then_inc(w_loaded, 16)
            for dst, src in ((w_router[:], a["w_router"]), (w_shared[:], a["w_shared"]), (wd_shared[:], a["wd_shared"]),
                             (b_router[:], bass.AP(a["b_router"].tensor, 0, [[0, P], [1, NE]]))):
                sp.dma_start(dst, src).then_inc(w1_loaded, 16)
            for dst, src in ((w_tok[:], "w_tok"), (b_tok[:], "b_tok"), (m0[:], "m0"), (state[0][:, 0:D], "m0T"),
                             (state[1][:, 0:D], "m0T"), (vg1T[:], "vg1T"), (vg2[:], "vg2"), (vg2T[:], "vg2T")):
                sp.dma_start(dst, a[src]).then_inc(w2_loaded, 16)
            sp.dma_start(w_gate2[:], a["w_gate2"]).then_inc(w3_loaded, 16)
            for g in range(G):
                b, o = g // 2, (g % 2) * GW
                sp.wait_ge(parts_ready, g + 1)
                for w, dst in enumerate((q_dram, k_dram)):
                    sp.dma_start(dst[:, b * P:(b + 1) * P, o:o + GW].rearrange("i r t -> r i t"),
                                 qk_part[:, w, :, :]).then_inc(parts_saved, 16)
            sp.wait_ge(parts_saved, G * 32)
            sp.wait_ge(stacks_zero, 1)
            sp.wait_ge(v_ready, G)

            def load_stacks(n, u):
                part = NH * HD * S
                for r in range(3):
                    rows = slice(r * 3 * HD, (r + 1) * 3 * HD)
                    sp.dma_start(q_stack[u][rows, :], bass.AP(q_dram.tensor, n * (HD * S) + r * part,
                                                              [[0, 3], [S, HD], [1, S]])).then_inc(stacks_loaded[u], 16)
                    sp.dma_start(k_stack[u][rows, :], bass.AP(k_dram.tensor, n * (HD * S),
                                                              [[part, 3], [S, HD], [1, S]])).then_inc(stacks_loaded[u], 16)
                sp.dma_start(v_cur[u][:], v_flat[:, bass.ds(n * (QT * HD), QT * HD)]).then_inc(stacks_loaded[u], 16)

            load_stacks(0, 0)
            load_stacks(1, 1)
            with sp.Fori(0, NH // 2 - 1) as i:
                for u in range(2):
                    ready(sp, o_psum, i * (2 * QT) + ((u + 1) * QT - 1))
                    load_stacks(i * 2 + (2 + u), u)

            for g in range(G):
                cols = slice(g * GW, (g + 1) * GW)
                sp.wait_ge(c_split, g + 1)
                sp.dma_start(bass.AP(c_dram.tensor, g * GW, [[3 * T, P], [T, 3], [1, GW]]), c_part[:, 0, :, :])\
                    .then_inc(c_saved, 16)
                sp.wait_ge(c_split_b, g + 1)
                sp.dma_start(bass.AP(c_dram.tensor, P * 3 * T + g * GW, [[3 * T, NE - P], [T, 3], [1, GW]]),
                             c_part[0:NE - P, 1, :, :]).then_inc(c_saved, 16)
            sp.wait_ge(c_saved, G * 32)
            sp.wait_ge(moe_zero, 1)

            def load_experts(m, u):
                sp.dma_start(w_exp[u][:], a["w_exp"][bass.ds(m, 1), :, :].rearrange("m p n -> p (m n)")).then_inc(exp_loaded[u], 16)
                sp.dma_start(c_rows[u][0:6, :], c_dram[bass.ds(m * 6, 6), :]).then_inc(exp_loaded[u], 16)

            load_experts(0, 0)
            sp.wait_ge(down_done, 1 + CREDIT)
            load_experts(1, 1)
            with sp.Fori(0, MT_N // 2 - 1) as i:
                for u in range(2):
                    sp.wait_ge(down_done, i * 8 + (4 * (2 + u) - 3 + CREDIT))
                    load_experts(i * 2 + (2 + u), u)
            for g in range(G):
                sp.wait_ge(c2_split, g + 1)
                sp.dma_start(bass.AP(c2_dram.tensor, g * GW, [[3 * T, NE2], [T, 3], [1, GW]]), c_part[0:NE2, 0, :, :])\
                    .then_inc(c2_saved, 16)
            sp.wait_ge(c2_saved, G * 16)
            sp.wait_ge(ffn_zero, 1)

            def load_ffn(m, e, u):
                sp.dma_start(w_ffn[u][:], a["w_ffn"][bass.ds(m, 1), :, :].rearrange("m p n -> p (m n)")).then_inc(ffn_loaded[u], 16)
                sp.dma_start(c_rows[u][0:3, :], c2_dram[bass.ds(e * 3, 3), :]).then_inc(ffn_loaded[u], 16)

            load_ffn(0, 0, 0)
            sp.wait_ge(down2_done, 1 + CREDIT)
            load_ffn(1, 0, 1)
            with sp.Fori(0, NE2 - 1) as i:
                for u in range(2):
                    sp.wait_ge(down2_done, i * 8 + (4 * (2 + u) - 3 + CREDIT))
                    load_ffn(i * 2 + (2 + u), i + 1, u)
            for g in range(G):
                ts = slice(g * TPG, (g + 1) * TPG)
                sp.wait_ge(x_ready, G * 3 + g + 1)
                sp.dma_start(x_dram(out)[:, ts, :], x[:, ts, :]).then_inc(stored, 16)
            sp.wait_ge(stored, 16 * G)

        @block.gpsimd
        def _(pool):
            link = Link(pool, pool_link)
            link(pool.memset(ident[:], 0.0))
            pool.affine_select(out=ident[:], in_=ident[:], compare_op=ALU.not_equal, fill=1.0, base=0,
                               pattern=[[-1, P]], channel_multiplier=1).then_inc(consts, 1)
            link(pool.memset(half[:], -0.5))
            link(pool.memset(root[:], 0.5))
            link(pool.memset(ones[:], 1.0))
            link(pool.memset(by_half[:], 0.0))
            pool.iota(distance, [[1, TW]], base=-(S - P), channel_multiplier=-1).then_inc(table, 1)
            for u in range(2):
                link.sign(pool.memset(q_stack[u][:], 0.0))
                link.sign(pool.memset(k_stack[u][:], 0.0))
            link.wait()
            pool.sem_inc(stacks_zero, 1)

            def norm(k):
                for g in range(G):
                    ts = slice(g * TPG, (g + 1) * TPG)
                    pool.wait_ge(var_ready, G * k + g + 1)
                    link(pool.tensor_scalar(rstd[:, ts], mv[:, ts, 1], EPS, None, ALU.add))
                    pool.tensor_tensor(rstd[:, ts], rstd[:, ts], half[:, ts], ALU.pow).then_inc(rstd_ready, 1)

            norm(0)

            for e in range(2):
                half_cols = spread[:, e * EI:(e + 1) * EI]
                link(pool.memset(half_cols, 1.0))
                link(pool.affine_select(out=half_cols, in_=half_cols, compare_op=ALU.is_ge, fill=0.0, base=-3 * e,
                                        pattern=[[0, EI]], channel_multiplier=1))
                link(pool.affine_select(out=half_cols, in_=half_cols, compare_op=ALU.is_ge, fill=0.0, base=3 * e + 2,
                                        pattern=[[0, EI]], channel_multiplier=-1))
            for u in range(2):
                link.sign(pool.memset(c_rows[u][:], 0.0))
            link.sign(pool.memset(w_exp[1][:, D:2 * D], 0.0))
            link.sign(pool.memset(hid[1][:], 0.0))
            link.wait()
            pool.sem_inc(moe_zero, 1)
            norm(1)
            for g in range(G):
                v = cT[0:NE - P, 1, g * GW:(g + 1) * GW]
                parts = c_part[0:NE - P, 1]
                pool.wait_ge(cT_ready, 2 * g + 2)
                if g:
                    pool.wait_ge(c_saved, 32 * g)
                link(pool.tensor_copy(parts[:, 0, :], v))
                link(pool.tensor_tensor(v, v, parts[:, 0, :], ALU.subtract))
                link(pool.tensor_copy(parts[:, 1, :], v))
                link(pool.tensor_tensor(v, v, parts[:, 1, :], ALU.subtract))
                pool.tensor_copy(parts[:, 2, :], v).then_inc(c_split_b, 1)

            norm(2)
            pool.wait_ge(sq_ready, 1)
            pool.tensor_tensor(inv_norm[:], inv_norm[:], root[:], ALU.pow).then_inc(root_ready, 1)
            pool.wait_ge(steps_ready, 1)
            pool.sem_inc(step_ready, CREDIT)
            pool.sem_inc(norm_ready, CREDIT)
            with pool.Fori(0, NCH // 2) as i:
                for u in range(2):
                    n = i * 2 + u
                    free(pool, norm_psum, n)
                    pool.tensor_copy(step[u][:], steps_flat[:, bass.ds(i * (2 * B * 3) + u * (B * 3), B * 3)])\
                        .then_inc(step_ready, 1)
                    ready(pool, norm_sq, n)
                    pool.tensor_tensor(m_norm[:, 2, :], m_norm[:, 1, :], root[:, 0:B], ALU.pow).then_inc(norm_ready, 1)

            link(pool.memset(spread2[:], 1.0))
            link(pool.affine_select(out=spread2[:], in_=spread2[:], compare_op=ALU.is_ge, fill=0.0, base=2,
                                    pattern=[[0, P]], channel_multiplier=-1))
            link.sign(pool.memset(padded[:], -1.0))
            link.sign(pool.memset(taken[:], -1.0))
            link.sign(pool.memset(w_ffn[1][:, 2 * D:3 * D], 0.0))
            pool.wait_ge(acc_done, 1)
            link.sign(pool.memset(hid[1][:], 0.0))
            link.wait()
            pool.sem_inc(ffn_zero, 1)
            norm(3)

        @block.scalar
        def _(act):
            link = Link(act, act_link)
            act.wait_ge(table, 1)
            link(act.activation(decay[:], distance, ACT.Abs))
            act.activation(decay[:], decay[:], ACT.Exp, scale=-DECAY).then_inc(table, 1)

            def norm(k):
                for g in range(G):
                    n = G * k + g
                    act.wait_ge(xnT_psum, n + 1)
                    act.activation(xnT[:, g * GW:(g + 1) * GW], bank(n % 2), ACT.Copy).then_inc(xnT_ready, 1)

            norm(0)
            for g in range(G):
                act.wait_ge(kv_psum, g + 1)
                act.activation(kvT, bank(3), ACT.Copy).then_inc(kv_ready, 1)
                act.wait_ge(q_psum, g + 1)
                if g:
                    act.wait_ge(parts_ready, g)
                act.activation(qk_f[:, 0, :], bank(2), ACT.Copy, scale=SCALE).then_inc(q_ready, 1)
                act.wait_ge(lat_psum, g + 1)
                act.activation(latT, bank(4)[0:LAT, :], ACT.Copy).then_inc(lat_ready, 1)
                act.wait_ge(k_psum, g + 1)
                act.activation(qk_f[:, 1, :], bank(5), ACT.Copy).then_inc(k_ready, 1)
                act.wait_ge(v_psum, g + 1)
                b, t0 = g // 2, (g % 2) * TPG
                for t in range(TPG):
                    ins = act.activation(v_heads[:, b * H:(b + 1) * H, t0 + t, :],
                                         bank(6)[:, t * P:(t + 1) * P].rearrange("p (h d) -> p h d", h=H), ACT.Copy)
                ins.then_inc(v_ready, 1)

            act.sem_inc(exp_ready, CREDIT)
            act.sem_inc(prT_ready, CREDIT)
            with act.Fori(0, NH // 2) as i:
                for c in range(2 * QT + 1):
                    if c < 2 * QT:
                        n = i * (2 * QT) + c
                        ready(act, max_ready, n)
                        free(act, prT_psum, n)
                        free(act, o_ready, n)
                        act.activation(pr[c % 2][:], sc[c % 2][:], ACT.Exp, bias=row[:, c % 2, 1:2],
                                       accum_out=row[:, c % 2, 2:3]).then_inc(exp_ready, 1)
                    if c >= 1:
                        n = i * (2 * QT) + (c - 1)
                        ready(act, prT_psum, n)
                        free(act, o_psum, n)
                        act.activation(prT[(c - 1) % 2][:], wide[2][:], ACT.Copy).then_inc(prT_ready, 1)
            for g in range(G):
                act.wait_ge(oT_psum, g + 1)
                act.activation(oT[:, g * GW:(g + 1) * GW], bank(g % 2), ACT.Copy).then_inc(oT_ready, 1)

            norm(1)
            for g in range(G):
                act.wait_ge(shared_psum, g + 1)
                if g >= 2:
                    act.wait_ge(shared_down, g - 1)
                act.activation(act_out[g % 2][0:EI, :], bank(4 + g % 2)[0:EI, :], ACT.Silu).then_inc(shared_act, 1)
            for t in range(NT):
                act.wait_ge(logit_ready, t + 1)
                act.activation(gates[:, t, :], gates[:, t, :], ACT.Sigmoid).then_inc(gate_ready, 1)
            for g in range(G):
                cols = slice(g * GW, (g + 1) * GW)
                act.wait_ge(cT_psum, g + 1)
                act.activation(cT[:, 0, cols], bank(4), ACT.Copy).then_inc(cT_ready, 1)
                act.activation(cT[0:NE - P, 1, cols], bank(5)[0:NE - P, :], ACT.Copy).then_inc(cT_ready, 1)
            act.sem_inc(silu_ready, CREDIT)
            with act.Fori(0, MT_N // 2) as i:
                for c in range(2 * G):
                    n = i * (2 * G) + c
                    ready(act, z_psum, n)
                    free(act, hid_ready, n)
                    act.activation(act_out[c % 2][:], bank(4 + c % 2), ACT.Silu).then_inc(silu_ready, 1)
            for g in range(G):
                act.wait_ge(acc_done, 1)
                act.activation(accT[:, g * GW:(g + 1) * GW], bank(g), ACT.Copy).then_inc(accT_ready, 1)

            norm(2)
            act.wait_ge(w2_loaded, 8 * 16)
            for g in range(G):
                for k in range(2):
                    act.wait_ge(tok_psum, 2 * g + k + 1)
                    act.activation(tok[:, k * T + g * GW:k * T + (g + 1) * GW], bank(2 + k)[0:1, :], ACT.Sigmoid,
                                   bias=b_tok[:, k:k + 1]).then_inc(tok_ready, 1)
            act.wait_ge(gate_psum, 1)
            act.activation(one_row[:, 0:B * NCH], bank(5)[0:1, 0:B * NCH], ACT.Sigmoid, bias=b_tok[:, 2:3]).then_inc(gate_row, 1)
            act.wait_ge(fold_psum, 1)
            link(act.activation(vg2_cat[:, 0:D], vg2T[:], ACT.Copy, scale=1.0 / CH))
            act.activation(vg2_cat[:, D:2 * D], bank(7)[:, 0:D], ACT.Copy, scale=1.0 / CH).then_inc(fold_ready, 1)
            for b in range(B):
                act.activation(state[b][:, D:2 * D], bank(7)[:, D:2 * D], ACT.Copy).then_inc(fold_ready, 1)
            for b in range(B):
                act.sem_inc(mz_silu[b], CREDIT)
                act.sem_inc(out_taken[b], CREDIT)
            with act.Fori(0, NCH // 2) as i:
                for u in range(2):
                    n = i * 2 + u
                    for b in range(B):
                        ready(act, mz_psum[b], n)
                        act.activation(silu_z[b][:], bank(b)[:, 0:CH], ACT.Silu, accum_out=h_sum[b][:]).then_inc(mz_silu[b], 1)
                    for b in range(B):
                        ready(act, out_psum[b], n)
                        act.activation(memT[:, bass.ds(i * (2 * CH) + (b * S + u * CH), CH)], bank(4 + b)[:, 0:CH],
                                       ACT.Copy).then_inc(out_taken[b], 1)

            norm(3)
            act.wait_ge(shifted, 1)
            act.activation(soft[:], soft[:], ACT.Exp).then_inc(exp2_ready, 1)
            for g in range(G):
                act.wait_ge(c2T_psum, g + 1)
                act.activation(c2T[:, g * GW:(g + 1) * GW], bank(g)[0:NE2, :], ACT.Copy).then_inc(c2T_ready, 1)
            act.sem_inc(silu2_ready, CREDIT)
            with act.Fori(0, NE2) as i:
                for c in range(2 * G):
                    n = i * (2 * G) + c
                    ready(act, gate_z, n)
                    free(act, gated_ready, n)
                    act.activation(act_out[c % 2][:], bank(4), ACT.Silu).then_inc(silu2_ready, 1)
            for g in range(G):
                act.wait_ge(acc2_done, 1)
                act.activation(accT[:, g * GW:(g + 1) * GW], bank(g), ACT.Copy).then_inc(accT2_ready, 1)

        @block.tensor
        def _(pe):
            pe.wait_ge(consts, 1)

            def norm(k):
                for g in range(G):
                    n = G * k + g
                    pe.wait_ge(xn_ready, n + 1)
                    if g >= 2:
                        pe.wait_ge(xnT_ready, n - 1)
                    for t in range(TPG):
                        ins = pe.transpose(bank(n % 2)[:, t * P:(t + 1) * P], xn[:, g * TPG + t, :], ident[:])
                    ins.then_inc(xnT_psum, 1)

            norm(0)
            pe.wait_ge(w_loaded, 7 * 16)
            for g in range(G):
                cols = xnT[:, g * GW:(g + 1) * GW]
                pe.wait_ge(xnT_ready, g + 1)
                if g:
                    pe.wait_ge(kv_ready, g)
                pe.matmul(bank(3), wk[:], cols, start=True, stop=False)
                pe.matmul(bank(3), wv[:], cols, start=False, stop=True).then_inc(kv_psum, 1)
                if g:
                    pe.wait_ge(q_ready, g)
                pe.matmul(bank(2), wq[:], cols, start=True, stop=True).then_inc(q_psum, 1)
                pe.wait_ge(kv_ready, g + 1)
                if g:
                    pe.wait_ge(lat_ready, g)
                pe.matmul(bank(4)[0:LAT, :], w_down[:], kvT, start=True, stop=True).then_inc(lat_psum, 1)
                pe.wait_ge(lat_ready, g + 1)
                if g:
                    pe.wait_ge(k_ready, g)
                pe.matmul(bank(5), w_up[:, 0:D], latT, start=True, stop=True).then_inc(k_psum, 1)
                if g:
                    pe.wait_ge(v_ready, g)
                for t in range(TPG):
                    ins = pe.matmul(bank(6)[:, t * P:(t + 1) * P], latT[:, t * P:(t + 1) * P], w_up[:, D:2 * D],
                                    start=True, stop=True)
                ins.then_inc(v_psum, 1)

            pe.wait_ge(k_ready, G)
            pe.wait_ge(v_ready, G)
            pe.sem_inc(s_psum, CREDIT)
            pe.sem_inc(prT_psum, CREDIT)
            pe.sem_inc(o_psum, CREDIT)
            with pe.Fori(0, NH // 2) as i:
                for c in range(2 * QT + 2):
                    if c < 2 * QT:
                        n, u, q = i * (2 * QT) + c, c // QT, c % QT
                        if q == 0:
                            pe.wait_ge(stacks_loaded[u], i * (7 * 16) + 7 * 16)
                        free(pe, s_clamped, n)
                        for k in range(S // 512):
                            ins = pe.matmul(wide[c % 2][:, k * 512:(k + 1) * 512], q_stack[u][:, q * P:(q + 1) * P],
                                            k_stack[u][:, k * 512:(k + 1) * 512], start=True, stop=True)
                        ins.then_inc(s_psum, 1)
                    if 1 <= c < 2 * QT + 1:
                        n = i * (2 * QT) + (c - 1)
                        ready(pe, exp_ready, n)
                        free(pe, prT_ready, n, 1)
                        for k in range(QT):
                            ins = pe.transpose(wide[2][:, k * P:(k + 1) * P], pr[(c - 1) % 2][:, k * P:(k + 1) * P], ident[:])
                        ins.then_inc(prT_psum, 1)
                    if c >= 2:
                        n, u = i * (2 * QT) + (c - 2), (c - 2) // QT
                        ready(pe, prT_ready, n)
                        free(pe, o_ready, n)
                        for k in range(QT):
                            ins = pe.matmul(bank(6 + c % 2)[:, 0:HD], prT[c % 2][:, k * P:(k + 1) * P],
                                            v_cur[u][:, k * HD:(k + 1) * HD], start=(k == 0), stop=(k == QT - 1))
                        ins.then_inc(o_psum, 1)
            pe.wait_ge(o_all, 1)
            for g in range(G):
                b, t0 = g // 2, (g % 2) * TPG
                if g >= 2:
                    pe.wait_ge(oT_ready, g - 1)
                for t in range(TPG):
                    ins = pe.transpose(bank(g % 2)[:, t * P:(t + 1) * P], o_tok[:, g * TPG + t, :], ident[:])
                ins.then_inc(oT_psum, 1)
            for g in range(G):
                pe.wait_ge(oT_ready, g + 1)
                if g >= 2:
                    pe.wait_ge(x_ready, g - 1)
                for t in range(TPG):
                    ins = pe.matmul(bank(2 + g % 2)[:, t * P:(t + 1) * P], oT[:, g * GW + t * P:g * GW + (t + 1) * P], wo[:],
                                    start=True, stop=True)
                ins.then_inc(y_psum, 1)

            norm(1)
            pe.wait_ge(w1_loaded, 4 * 16)
            pe.wait_ge(xnT_ready, 2 * G)
            for g in range(G):
                if g >= 2:
                    pe.wait_ge(shared_act, g - 1)
                pe.matmul(bank(4 + g % 2)[0:EI, :], w_shared[:], xnT[:, g * GW:(g + 1) * GW], start=True, stop=True)\
                    .then_inc(shared_psum, 1)
                pe.wait_ge(shared_act, g + 1)
                pe.matmul(bank(g), wd_shared[:], act_out[g % 2][0:EI, :], start=True, stop=False, skip_group_check=True)\
                    .then_inc(shared_down, 1)
            for t in range(NT):
                if t >= 2:
                    pe.wait_ge(logit_ready, t - 1)
                pe.matmul(bank(6 + t % 2)[:, 0:NE], xnT[:, t * P:(t + 1) * P], w_router[:], start=True, stop=True)\
                    .then_inc(logit_psum, 1)
            for g in range(G):
                pe.wait_ge(combine_ready, g + 1)
                if g:
                    pe.wait_ge(cT_ready, 2 * g)
                for t in range(TPG):
                    pe.transpose(bank(4)[:, t * P:(t + 1) * P], rest[:, t, 0:P], ident[:])
                    ins = pe.transpose(bank(5)[0:NE - P, t * P:(t + 1) * P], rest[:, t, P:NE], ident[:])
                ins.then_inc(cT_psum, 1)
            pe.wait_ge(moe_zero, 1)
            pe.wait_ge(cT_ready, 2 * G)
            for s_ in (z_psum, cb_psum, down_done):
                pe.sem_inc(s_, CREDIT)

            def down(u, c):
                return pe.matmul(bank(c % G), w_exp[u][:, D:2 * D], hid[c % 2][:], start=False, stop=False,
                                 skip_group_check=True)

            with pe.Fori(0, MT_N // 2) as i:
                for c in range(2 * G):
                    n, u, g = i * (2 * G) + c, c // G, c % G
                    cols = slice(g * GW, (g + 1) * GW)
                    if g == 0:
                        pe.wait_ge(exp_loaded[u], i * 32 + 32)
                    free(pe, silu_ready, n)
                    pe.matmul(bank(4 + c % 2), w_exp[u][:, 0:D], xnT[:, cols], start=True, stop=True).then_inc(z_psum, 1)
                    free(pe, hid_ready, n)
                    pe.matmul(bank(6 + c % 2), spread[:], c_rows[u][:, cols], start=True, stop=True).then_inc(cb_psum, 1)
                    ready(pe, hid_ready, n - 1)
                    down((c - 1) // G % 2, (c - 1) % (2 * G)).then_inc(down_done, 1)
            ready(pe, hid_ready, MT_N * G - 1)
            down(1, 2 * G - 1).then_inc(acc_done, 1)
            for g in range(G):
                pe.wait_ge(accT_ready, g + 1)
                for t in range(TPG):
                    ins = pe.transpose(bank(4 + g)[:, t * P:(t + 1) * P], accT[:, g * GW + t * P:g * GW + (t + 1) * P], ident[:])
                ins.then_inc(acc_psum, 1)

            norm(2)
            pe.wait_ge(w2_loaded, 8 * 16)
            pe.wait_ge(xnT_ready, 3 * G)
            pe.matmul(bank(7)[:, 0:D], vg2[:], vg1T[:], start=True, stop=True)
            pe.matmul(bank(7)[:, D:2 * D], m0[:], vg1T[:], start=True, stop=True).then_inc(fold_psum, 1)
            for g in range(G):
                for k in range(2):
                    if g:
                        pe.wait_ge(tok_ready, 2 * g + k - 1)
                    pe.matmul(bank(2 + k)[0:1, :], w_tok[:, k:k + 1], xnT[:, g * GW:(g + 1) * GW], start=True, stop=True)\
                        .then_inc(tok_psum, 1)
            pe.wait_ge(by_half_ready, 1)
            for t in range(NT):
                ins = pe.matmul(bank(4)[:, 2 * t:2 * t + 2], xn[:, t, :], by_half[:, t, :], start=True, stop=True)
            ins.then_inc(km_psum, 1)
            pe.wait_ge(km_ready, 1)
            pe.matmul(bank(5)[0:1, 0:B * NCH], w_tok[:, 2:3], k_mean[:], start=True, stop=True).then_inc(gate_psum, 1)
            pe.wait_ge(scalars_ready, 1)
            pe.matmul(bank(6)[:, 0:2 * B * NCH], ones[0:1, :], one_row[:, 4 * B * NCH:6 * B * NCH], start=True, stop=True)\
                .then_inc(scalars_psum, 1)
            pe.wait_ge(steps_ready, 1)
            pe.wait_ge(fold_ready, 1 + B)
            for b in range(B):
                pe.sem_inc(mz_psum[b], CREDIT)
                pe.sem_inc(err_psum[b], CREDIT)
                pe.sem_inc(out_psum[b], CREDIT)
            pe.sem_inc(norm_psum, CREDIT)
            with pe.Fori(0, NCH // 2) as i:
                for u in range(2):
                    n = i * 2 + u
                    for b in range(B):
                        chunk = xnT[:, bass.ds(i * (2 * CH) + (b * S + u * CH), CH)]
                        free(pe, state_ready[b], n, 1)
                        pe.matmul(bank(b)[:, 0:CH], state[b][:, D:2 * D], chunk, start=True, stop=True).then_inc(mz_psum[b], 1)
                        ready(pe, step_ready, n)
                        pe.matmul(bank(2 + b)[:, 0:2 * D], across(step[u][:, 3 * b + 2:3 * b + 3], P), state[b][:],
                                  start=True, stop=False)
                        free(pe, out_taken[b], n, 1)
                        pe.matmul(bank(4 + b)[:, 0:CH], state[b][:, 0:D], chunk, start=True, stop=False)
                    for b in range(B):
                        ready(pe, mz_silu[b], n)
                        pe.matmul(bank(2 + b)[:, 0:2 * D], across(h_sum[b][:], P), vg2_cat[:], start=False, stop=True)\
                            .then_inc(err_psum[b], 1)
                        pe.matmul(bank(4 + b)[:, 0:CH], vg2T[:], silu_z[b][:], start=False, stop=True).then_inc(out_psum[b], 1)
                    ready(pe, rows_ready, n)
                    pe.matmul(bank(6)[:, 0:B], ones[:], m_norm[:, 0, :], start=True, stop=True).then_inc(norm_psum, 1)
            for b in range(B):
                ready(pe, out_taken[b], NCH - 1)
            for g in range(G):
                for t in range(TPG):
                    ins = pe.transpose(bank(g)[:, t * P:(t + 1) * P], memT[:, g * GW + t * P:g * GW + (t + 1) * P], ident[:])
                ins.then_inc(mem_psum, 1)

            norm(3)
            pe.wait_ge(w3_loaded, 16)
            pe.wait_ge(xnT_ready, 4 * G)
            for t in range(NT):
                ins = pe.matmul(bank(4)[:, t * NE2:(t + 1) * NE2], xnT[:, t * P:(t + 1) * P], w_gate2[:], start=True, stop=True)
            ins.then_inc(logit2_psum, 1)
            pe.wait_ge(combine2_ready, 1)
            for g in range(G):
                for t in range(TPG):
                    ins = pe.transpose(bank(g)[0:NE2, t * P:(t + 1) * P], combine2[:, g * TPG + t, :], ident[:])
                ins.then_inc(c2T_psum, 1)
            pe.wait_ge(ffn_zero, 1)
            pe.wait_ge(c2T_ready, G)
            for s_ in (gate_z, up_z, c2_psum, down2_done):
                pe.sem_inc(s_, CREDIT)
            for g in range(G):
                pe.matmul(bank(g), w_ffn[1][:, 2 * D:3 * D], hid[1][:], start=True, stop=False, skip_group_check=True)

            def down2(u, c):
                return pe.matmul(bank(c % G), w_ffn[u][:, 2 * D:3 * D], hid[c % 2][:], start=False, stop=False,
                                 skip_group_check=True)

            with pe.Fori(0, NE2) as i:
                for c in range(2 * G):
                    n, u, g = i * (2 * G) + c, c // G, c % G
                    cols = slice(g * GW, (g + 1) * GW)
                    if g == 0:
                        pe.wait_ge(ffn_loaded[u], i * 32 + 32)
                    free(pe, silu2_ready, n, 1)
                    pe.matmul(bank(4), w_ffn[u][:, 0:D], xnT[:, cols], start=True, stop=True).then_inc(gate_z, 1)
                    free(pe, gated_ready, n, 1)
                    pe.matmul(bank(5), w_ffn[u][:, D:2 * D], xnT[:, cols], start=True, stop=True).then_inc(up_z, 1)
                    free(pe, hid2_ready, n, 1)
                    pe.matmul(bank(6), spread2[:], c_rows[u][:, cols], start=True, stop=True).then_inc(c2_psum, 1)
                    ready(pe, hid2_ready, n - 1)
                    down2((c - 1) // G % 2, (c - 1) % (2 * G)).then_inc(down2_done, 1)
            ready(pe, hid2_ready, FT_N * G - 1)
            down2(1, 2 * G - 1).then_inc(acc2_done, 1)
            for g in range(G):
                pe.wait_ge(accT2_ready, g + 1)
                for t in range(TPG):
                    ins = pe.transpose(bank(4 + g)[:, t * P:(t + 1) * P], accT[:, g * GW + t * P:g * GW + (t + 1) * P], ident[:])
                ins.then_inc(acc2_psum, 1)

        @block.vector
        def _(dve):
            link = Link(dve, dve_link)

            def norm(k):
                for g in range(G):
                    n = G * k + g
                    tiles = range(g * TPG, (g + 1) * TPG)
                    if k == 0:
                        dve.wait_ge(x_loaded, 16 * G)
                    else:
                        dve.wait_ge(x_ready, G * (k - 1) + g + 1)
                    for t in tiles:
                        link.sign(dve.bn_stats(stats[:, t, :], x[:, t, :]))
                    link.wait()
                    for t in tiles:
                        ins = dve.bn_aggr(mv[:, t, :], stats[:, t, :])
                        if t < tiles[-1]:
                            link.sign(ins)
                    link.wait()
                    ins.then_inc(var_ready, 1)
                    dve.wait_ge(rstd_ready, n + 1)
                    for t in tiles:
                        ins = dve.tensor_scalar(xn[:, t, :], x[:, t, :], mv[:, t, 0:1], rstd[:, t:t + 1], ALU.subtract, ALU.mult)
                        if t < tiles[-1]:
                            link.sign(ins)
                    link.wait()
                    ins.then_inc(xn_ready, 1)

            norm(0)
            for g in range(G):
                if g:
                    dve.wait_ge(parts_saved, 32 * g)
                for w, src in ((0, q_ready), (1, k_ready)):
                    dve.wait_ge(src, g + 1)
                    link(dve.tensor_copy(qk_part[:, w, 0, :], qk_f[:, w, :]))
                    link(dve.tensor_tensor(qk_r[:, w, :], qk_f[:, w, :], qk_part[:, w, 0, :], ALU.subtract))
                    link(dve.tensor_copy(qk_part[:, w, 1, :], qk_r[:, w, :]))
                    link(dve.tensor_tensor(qk_r[:, w, :], qk_r[:, w, :], qk_part[:, w, 1, :], ALU.subtract))
                    ins = dve.tensor_copy(qk_part[:, w, 2, :], qk_r[:, w, :])
                    if w == 0:
                        link(ins)
                ins.then_inc(parts_ready, 1)

            dve.wait_ge(table, 2)
            dve.sem_inc(s_clamped, CREDIT)
            dve.sem_inc(max_ready, CREDIT)
            dve.sem_inc(o_ready, CREDIT)
            first, link_n = link.n, 0
            with dve.Fori(0, NH // 2) as i:
                per_turn = 2 * QT * 2
                link.turn = i * per_turn
                for c in range(2 * QT + 2):
                    if c < 2 * QT:
                        n, q = i * (2 * QT) + c, c % QT
                        ready(dve, s_psum, n)
                        free(dve, exp_ready, n)
                        dve.tensor_scalar(sc[c % 2][:], wide[c % 2][:], -CLAMP, CLAMP, ALU.max, ALU.min).then_inc(s_clamped, 1)
                        dve.wait_ge(table, 2)
                        ready(dve, s_clamped, n)
                        at = S - P - q * P
                        link(dve.tensor_tensor_reduce(sc[c % 2][:], sc[c % 2][:], decay[:, at:at + S], 1.0, -3.0e38,
                                                      ALU.mult, ALU.max, row[:, c % 2, 0:1]))
                        dve.tensor_scalar(row[:, c % 2, 1:2], row[:, c % 2, 0:1], -1.0, None, ALU.mult).then_inc(max_ready, 1)
                    if c >= 2:
                        n, u, q = i * (2 * QT) + (c - 2), (c - 2) // QT, (c - 2) % QT
                        ready(dve, exp_ready, n)
                        link(dve.reciprocal(row[:, c % 2, 3:4], row[:, c % 2, 2:3]))
                        ready(dve, o_psum, n)
                        dve.tensor_scalar(o_flat[:, bass.ds((i * 2 + u) * (QT * HD) + q * HD, HD)], bank(6 + c % 2)[:, 0:HD],
                                          row[:, c % 2, 3:4], None, ALU.mult).then_inc(o_ready, 1)
                assert link.n - first == per_turn
            link.end_loop(NH // 2, per_turn)
            ready(dve, o_ready, NH * QT - 1)
            for b in range(B):
                for q in range(QT):
                    ins = dve.tensor_copy(o_tok[:, b * QT + q, :].rearrange("p (h d) -> p h d", h=H),
                                          o_heads[:, b * H:(b + 1) * H, q, :])
                    if b * QT + q < NT - 1:
                        link.sign(ins)
            link.wait()
            ins.then_inc(o_all, 1)
            for g in range(G):
                ts = slice(g * TPG, (g + 1) * TPG)
                dve.wait_ge(y_psum, g + 1)
                dve.tensor_tensor(x[:, ts, :], x[:, ts, :], bank(2 + g % 2).rearrange("p (t d) -> p t d", t=TPG), ALU.add)\
                    .then_inc(x_ready, 1)

            norm(1)
            dve.wait_ge(w1_loaded, 4 * 16)
            for t in range(NT):
                dve.wait_ge(logit_psum, t + 1)
                dve.tensor_tensor(gates[:, t, :], bank(6 + t % 2)[:, 0:NE], b_router[:], ALU.add).then_inc(logit_ready, 1)
            for g in range(G):
                tiles = range(g * TPG, (g + 1) * TPG)
                ts = slice(g * TPG, (g + 1) * TPG)
                dve.wait_ge(gate_ready, (g + 1) * TPG)
                for t in tiles:
                    link.sign(dve.max(top[:, t, :], gates[:, t, :]))
                link.wait()
                if g:
                    dve.wait_ge(cT_psum, g)
                for t in tiles:
                    link.sign(dve.match_replace(rest[:, t % TPG, :], top[:, t, :], gates[:, t, :], -1.0))
                link(dve.tensor_reduce(top_sum[:, ts], top[:, ts, :], AX.X, ALU.add))
                link(dve.tensor_scalar(top_sum[:, ts], top_sum[:, ts], 1e-9, None, ALU.add))
                link(dve.reciprocal(top_inv[:, ts], top_sum[:, ts]))
                for t in tiles:
                    link.sign(dve.scalar_tensor_tensor(rest[:, t % TPG, :], rest[:, t % TPG, :], 0.0, gates[:, t, :],
                                                       ALU.max, ALU.subtract))
                link.wait()
                for t in tiles:
                    ins = dve.tensor_scalar(rest[:, t % TPG, :], rest[:, t % TPG, :], top_inv[:, t:t + 1], -ROUTED,
                                            ALU.mult, ALU.mult)
                    if t < tiles[-1]:
                        link.sign(ins)
                link.wait()
                ins.then_inc(combine_ready, 1)
            for g in range(G):
                v = cT[:, 0, g * GW:(g + 1) * GW]
                dve.wait_ge(cT_ready, 2 * g + 1)
                if g:
                    dve.wait_ge(c_saved, 32 * g)
                link(dve.tensor_copy(c_part[:, 0, 0, :], v))
                link(dve.tensor_tensor(v, v, c_part[:, 0, 0, :], ALU.subtract))
                link(dve.tensor_copy(c_part[:, 0, 1, :], v))
                link(dve.tensor_tensor(v, v, c_part[:, 0, 1, :], ALU.subtract))
                dve.tensor_copy(c_part[:, 0, 2, :], v).then_inc(c_split, 1)
            dve.sem_inc(hid_ready, CREDIT)
            with dve.Fori(0, MT_N // 2) as i:
                for c in range(2 * G):
                    n = i * (2 * G) + c
                    ready(dve, silu_ready, n)
                    ready(dve, cb_psum, n)
                    dve.wait_ge(down_done, n + CREDIT)
                    dve.tensor_tensor(hid[c % 2][:], act_out[c % 2][:], bank(6 + c % 2), ALU.mult).then_inc(hid_ready, 1)
            for g in range(G):
                ts = slice(g * TPG, (g + 1) * TPG)
                dve.wait_ge(acc_psum, g + 1)
                dve.tensor_tensor(x[:, ts, :], x[:, ts, :], bank(4 + g).rearrange("p (t d) -> p t d", t=TPG), ALU.add)\
                    .then_inc(x_ready, 1)

            norm(2)
            C2 = B * NCH
            dve.wait_ge(xn_ready, 3 * G)
            link(dve.tensor_tensor(squares, xn[:, :, :].rearrange("p t d -> p (t d)"), xn[:, :, :].rearrange("p t d -> p (t d)"),
                                   ALU.mult))
            dve.tensor_reduce(inv_norm[:], squares.rearrange("p (t d) -> p t d", t=NT), AX.X, ALU.add).then_inc(sq_ready, 1)
            dve.wait_ge(xnT_ready, 3 * G)
            link(dve.tensor_reduce(x_mean[:], xnT[:, :].rearrange("p (c t) -> p c t", t=CH), AX.X, ALU.add))
            dve.wait_ge(root_ready, 1)
            link(dve.tensor_scalar(inv_norm[:], inv_norm[:], NORM_EPS, float(CH), ALU.max, ALU.mult))
            link(dve.reciprocal(inv_norm[:], inv_norm[:]))
            link(dve.tensor_copy(by_half[0:CH, :, 0], inv_norm[0:CH, :]))
            dve.tensor_copy(by_half[CH:P, :, 1], inv_norm[CH:P, :]).then_inc(by_half_ready, 1)
            dve.wait_ge(km_psum, 1)
            dve.tensor_copy(k_mean[:], bank(4)[:, 0:C2]).then_inc(km_ready, 1)
            dve.wait_ge(km_ready, 1)
            by_step = [steps[:, :, :, k].rearrange("p n b -> p b n") for k in range(3)]
            by_batch = lambda ap: ap.rearrange("p (b n) -> p b n", b=B)
            link(dve.scalar_tensor_tensor(by_step[2], by_batch(x_mean[:]), 1.0 / CH, by_batch(k_mean[:]), ALU.mult, ALU.subtract))
            dve.wait_ge(tok_ready, 2 * G)
            rows = [one_row[:, k * C2:(k + 1) * C2] for k in range(6)]
            link(dve.tensor_reduce(one_row[:, C2:3 * C2], tok.rearrange("p (c t) -> p c t", t=CH), AX.X, ALU.add))
            link(dve.tensor_scalar(rows[3], rows[2], -(1.0 - MIN_DECAY) / CH, 1.0 - MIN_DECAY, ALU.mult, ALU.add))
            dve.wait_ge(gate_row, 1)
            link(dve.tensor_tensor(rows[3], rows[3], rows[0], ALU.mult))
            link(dve.tensor_scalar(rows[4], rows[3], -1.0, 1.0, ALU.mult, ALU.add))
            dve.scalar_tensor_tensor(rows[5], rows[1], MAX_LR / CH, rows[0], ALU.mult, ALU.mult).then_inc(scalars_ready, 1)
            dve.wait_ge(scalars_psum, 1)
            link(dve.tensor_copy(by_step[0], by_batch(bank(6)[:, 0:C2])))
            dve.tensor_tensor(by_step[1], by_batch(k_mean[:]), by_batch(bank(6)[:, C2:2 * C2]), ALU.mult).then_inc(steps_ready, 1)
            for b in range(B):
                dve.sem_inc(state_ready[b], CREDIT)
            dve.sem_inc(rows_ready, CREDIT)
            dve.sem_inc(norm_sq, CREDIT)
            dve.wait_ge(fold_ready, 1 + B)
            first, per_turn = link.n, 2 * (2 * B + 1 + 3)
            with dve.Fori(0, NCH // 2) as i:
                link.turn = i * per_turn
                for u in range(2):
                    n = i * 2 + u
                    ready(dve, step_ready, n)
                    for b in range(B):
                        free(dve, state_ready[b], n, 1)
                        link.sign(dve.tensor_scalar(kept[b][:], state[b][:], step[u][:, 3 * b:3 * b + 1], None, ALU.mult))
                    link.wait()
                    for b in range(B):
                        ready(dve, err_psum[b], n)
                        link(dve.scalar_tensor_tensor(state[b][:], bank(2 + b)[:, 0:2 * D], step[u][:, 3 * b + 1:3 * b + 2],
                                                      kept[b][:], ALU.mult, ALU.add))
                        ins = dve.tensor_tensor_reduce(m_sq[:, b, :], state[b][:, 0:D], state[b][:, 0:D], 1.0, 0.0,
                                                       ALU.mult, ALU.add, m_norm[:, 0, b:b + 1])
                        if b == 0:
                            link.sign(ins)
                    ins.then_inc(rows_ready, 1)
                    ready(dve, norm_psum, n)
                    dve.tensor_copy(m_norm[:, 1, :], bank(6)[:, 0:B]).then_inc(norm_sq, 1)
                    ready(dve, norm_ready, n)
                    link(dve.tensor_scalar(m_norm[:, 3, :], m_norm[:, 2, :], 1e-6, None, ALU.add))
                    link(dve.reciprocal(m_norm[:, 3, :], m_norm[:, 3, :]))
                    link(dve.tensor_scalar(m_norm[:, 3, :], m_norm[:, 3, :], MAX_NORM, 1.0, ALU.mult, ALU.min))
                    for b in range(B):
                        dve.tensor_scalar(state[b][:], state[b][:], m_norm[:, 3, b:b + 1], None, ALU.mult)\
                            .then_inc(state_ready[b], 1)
                assert link.n - first == per_turn, (link.n - first, per_turn)
            link.end_loop(NCH // 2, per_turn)
            for g in range(G):
                ts = slice(g * TPG, (g + 1) * TPG)
                dve.wait_ge(mem_psum, g + 1)
                dve.tensor_tensor(x[:, ts, :], x[:, ts, :], bank(g).rearrange("p (t d) -> p t d", t=TPG), ALU.add)\
                    .then_inc(x_ready, 1)

            norm(3)

            def by_row(ap, n):
                return bass.AP(ap.tensor, ap.offset, [list(ap.ap[0]), list(ap.ap[1]), [0, n]])

            logits = bank(4)[:, 0:NT * NE2].rearrange("p (t e) -> p t e", t=NT)
            dve.wait_ge(logit2_psum, 1)
            link(dve.tensor_reduce(r_max[:], logits, AX.X, ALU.max))
            dve.tensor_tensor(soft[:], logits, by_row(r_max[:], NE2), ALU.subtract).then_inc(shifted, 1)
            dve.wait_ge(exp2_ready, 1)
            link(dve.tensor_reduce(r_sum[:], soft[:], AX.X, ALU.add))
            link(dve.reciprocal(r_sum[:], r_sum[:]))
            link(dve.tensor_tensor(soft[:], soft[:], by_row(r_sum[:], NE2), ALU.mult))
            dve.wait_ge(ffn_zero, 1)
            pairs = soft[:].rearrange("p t (g k) -> p t g k", k=2)
            link(dve.tensor_reduce(padded[:, 0, :, 0:4], pairs, AX.X, ALU.max))

            def mark_two(k):
                for t in range(NT):
                    link.sign(dve.max(best[:, k, t, :], padded[:, k, t, :]))
                link.wait()
                link(dve.tensor_copy(taken[:, k, :, 0:2], best[:, k, :, 0:2]))
                for t in range(NT):
                    link.sign(dve.match_replace(marked[:, k, t, :], taken[:, k, t, :], padded[:, k, t, :], -2.0))
                link.wait()

            mark_two(0)
            link(dve.tensor_scalar(marked[:, 0, :, :], marked[:, 0, :, :], -2.0, None, ALU.is_equal))
            for k in range(2):
                link.sign(dve.tensor_tensor(padded[:, 1, :, k:8:2], soft[:, :, k:8:2], marked[:, 0, :, 0:4], ALU.mult))
            link.wait()
            mark_two(1)
            link(dve.tensor_scalar(marked[:, 1, :, :], marked[:, 1, :, :], -2.0, None, ALU.is_equal))
            link(dve.tensor_tensor(combine2[:], padded[:, 1, :, 0:8], marked[:, 1, :, 0:8], ALU.mult))
            link(dve.tensor_reduce(r_sum[:], best[:, 1, :, 0:2], AX.X, ALU.add))
            link(dve.reciprocal(r_sum[:], r_sum[:]))
            dve.tensor_tensor(combine2[:], combine2[:], by_row(r_sum[:], NE2), ALU.mult).then_inc(combine2_ready, 1)
            for g in range(G):
                v = c2T[:, g * GW:(g + 1) * GW]
                parts = c_part[0:NE2, 0]
                dve.wait_ge(c2T_ready, g + 1)
                if g:
                    dve.wait_ge(c2_saved, 16 * g)
                link(dve.tensor_copy(parts[:, 0, :], v))
                link(dve.tensor_tensor(v, v, parts[:, 0, :], ALU.subtract))
                link(dve.tensor_copy(parts[:, 1, :], v))
                link(dve.tensor_tensor(v, v, parts[:, 1, :], ALU.subtract))
                dve.tensor_copy(parts[:, 2, :], v).then_inc(c2_split, 1)
            dve.sem_inc(gated_ready, CREDIT)
            dve.sem_inc(hid2_ready, CREDIT)
            with dve.Fori(0, NE2) as i:
                for c in range(2 * G):
                    n = i * (2 * G) + c
                    ready(dve, silu2_ready, n)
                    ready(dve, up_z, n)
                    free(dve, hid2_ready, n)
                    dve.tensor_tensor(gated[c % 2][:], act_out[c % 2][:], bank(5), ALU.mult).then_inc(gated_ready, 1)
                    ready(dve, gated_ready, n)
                    ready(dve, c2_psum, n)
                    dve.wait_ge(down2_done, n + CREDIT)
                    dve.tensor_tensor(hid[c % 2][:], gated[c % 2][:], bank(6), ALU.mult).then_inc(hid2_ready, 1)
            for g in range(G):
                ts = slice(g * TPG, (g + 1) * TPG)
                dve.wait_ge(acc2_psum, g + 1)
                dve.tensor_tensor(x[:, ts, :], x[:, ts, :], bank(4 + g).rearrange("p (t d) -> p t d", t=TPG), ALU.add)\
                    .then_inc(x_ready, 1)


def kernel(**inputs):
    import concourse.bacc as bacc
    from concourse.bass_utils import run_bass_kernel_spmd as run

    w = {k: np.asarray(v) for k, v in inputs.items()}
    arrays = {
        "x": w["L0_attn_x"], "wq": w["L0_attn_Wq"], "wk": w["L0_attn_Wk"], "wv": w["L0_attn_Wv"], "wo": w["L0_attn_Wo"],
        "w_down": w["L0_attn_W_down_kv"], "w_up_k": w["L0_attn_W_up_k"], "w_up_v": w["L0_attn_W_up_v"],
        "w_router": w["L0_ffn_router_w"].T, "b_router": w["L0_ffn_expert_bias"],
        "w_shared": w["L0_ffn_w_gate_shared"].T, "wd_shared": w["L0_ffn_w_down_shared"].T,
        "w_exp": np.concatenate([w["L0_ffn_w_gate"].reshape(MT_N, P, D).transpose(0, 2, 1),
                                 w["L0_ffn_w_down"].transpose(0, 2, 1).reshape(MT_N, P, D)], axis=2),
        "w_tok": np.stack([w["L1_attn_eta_w"], w["L1_attn_alpha_w"], w["L1_attn_gate_w"]], axis=1),
        "b_tok": np.stack([w["L1_attn_eta_b"], w["L1_attn_alpha_b"], w["L1_attn_gate_b"]], axis=1),
        "m0": w["L1_attn_M_init"], "m0T": w["L1_attn_M_init"].T, "vg1T": w["L1_attn_vg_w1"].T,
        "vg2": w["L1_attn_vg_w2"], "vg2T": w["L1_attn_vg_w2"].T,
        "w_gate2": w["L1_ffn_gate_w"].T,
        "w_ffn": np.concatenate([w["L1_ffn_w13_weight"].reshape(NE2, 2, FI2 // P, P, D)[:, 0].reshape(FT_N, P, D).transpose(0, 2, 1),
                                 w["L1_ffn_w13_weight"].reshape(NE2, 2, FI2 // P, P, D)[:, 1].reshape(FT_N, P, D).transpose(0, 2, 1),
                                 w["L1_ffn_w2_weight"].transpose(0, 2, 1).reshape(FT_N, P, D)], axis=2),
    }
    arrays = {"in_" + k: np.ascontiguousarray(v) for k, v in arrays.items()}
    nc = bacc.Bacc("TRN2", target_bir_lowering=False, num_devices=1)
    a = {k[3:]: nc.dram_tensor(k, v.shape, mybir.dt.from_np(v.dtype), kind="ExternalInput").ap() for k, v in arrays.items()}
    out = nc.dram_tensor("out", (B, S, D), F32, kind="ExternalOutput").ap()
    build(nc, a, out)
    return run(nc, [arrays], core_ids=[0]).results[0]["out"]
```

```python
from contextlib import ExitStack

import concourse.bass as bass
import numpy as np
from concourse import mybir

F32 = mybir.dt.float32
BF16 = mybir.dt.bfloat16
I32 = mybir.dt.int32
ALU = mybir.AluOpType
ACT = mybir.ActivationFunctionType
AX = mybir.AxisListType

P = 128
B, S, D = 2, 1024, 128
T = B * S
NT = T // P
G = 4
GW = T // G
TPG = NT // G
H, HD = 16, 8
NH = B * H
QT = S // P
LAT = 32
PAIRS = 9
CLAMP = 10000.0
DECAY = 0.01 * 0.01
SCALE = 1.0 / (float(np.sqrt(np.float32(D))) + 1e-8)
EPS = 1e-5
NE, EI, TOPK = 160, 64, 8
MT_N = NE * EI // P
ROUTED = 2.5
CH = 64
NCH = S // CH
MAX_LR, MIN_DECAY, MAX_NORM, NORM_EPS = 0.2, 0.5, 30.0, 1e-5
NE2, FI2 = 8, 256
FT_N = NE2 * FI2 // P
RING = 8
BOUND = 40.0
TW = 2 * S - P
CREDIT = 2


class Link:

    def __init__(self, eng, sem):
        self.eng, self.sem, self.n, self.turn = eng, sem, 0, 0

    def sign(self, ins):
        ins.then_inc(self.sem, 1)
        self.n += 1
        return ins

    def wait(self):
        self.eng.wait_ge(self.sem, self.n + self.turn)

    def __call__(self, ins):
        self.sign(ins)
        self.wait()
        return ins

    def end_loop(self, turns, per_turn):
        self.n, self.turn = self.n + (turns - 1) * per_turn, 0


def build(nc, a, out):
    with ExitStack() as ctx:
        def sb(name, shape, dt=F32):
            return ctx.enter_context(nc.sbuf_tensor(name, shape, dt))

        def sem(name):
            return ctx.enter_context(nc.semaphore(name))

        def dram(name, shape, dt):
            return nc.dram_tensor(name, shape, dt, kind="Internal").ap()

        bank01 = ctx.enter_context(nc.psum_tensor("bank01", [P, 1024], F32))
        bank23 = ctx.enter_context(nc.psum_tensor("bank23", [P, 1024], F32))
        bank45 = ctx.enter_context(nc.psum_tensor("bank45", [P, 1024], F32))
        bank67 = ctx.enter_context(nc.psum_tensor("bank67", [P, 1024], F32))
        wide = [bank01, bank23, bank45, bank67]

        def bank(n):
            return wide[n // 2][:, (n % 2) * 512:(n % 2) * 512 + 512]

        x = sb("x", [P, NT, D])
        xn = sb("xn", [P, NT, D])
        xnT = sb("xnT", [P, T])
        stats = sb("stats", [P, NT, 6])
        mv = sb("mv", [P, NT, 2])
        rstd = sb("rstd", [P, NT])
        ident = sb("ident", [P, P])
        half = sb("half", [P, NT])
        wq = sb("wq", [P, D])
        wk = sb("wk", [P, D])
        wv = sb("wv", [P, D])
        wo = sb("wo", [P, D])
        w_down = sb("w_down", [P, LAT])
        w_up = sb("w_up", [LAT, 2 * D])
        big = sb("big", [P, 4 * T])
        kvT = big[:, 0:512]
        latT = big[0:LAT, 512:1024]
        qk_f = big[:, 1024:2048].rearrange("p (w t) -> p w t", w=2)
        folded = big[:, 2048:4096].rearrange("p (s t) -> p s t", s=4)
        qk_sq = big[:, 4096:5120].rearrange("p (w t) -> p w t", w=2)
        distance = big[:, 5120:5120 + TW].bitcast(I32)
        time = big[:, 7104:7104 + S].bitcast(I32)
        v_heads = sb("v_heads", [P, NH, QT, HD])
        v_flat = v_heads[:, :, :, :].rearrange("p n t d -> p (n t d)")
        o_heads = sb("o_heads", [P, QT, NH + 1, HD])
        q_stack = [[sb(f"q_stack{s}{u}", [P, S], BF16) for u in range(2)] for s in range(2)]
        k_stack = [[sb(f"k_stack{s}{u}", [P, S], BF16) for u in range(2)] for s in range(2)]
        v_cur = [sb(f"v_cur{u}", [P, QT, 32]) for u in range(2)]
        ring = sb("ring", [P, RING * S])
        parts = ring[:, 0:6 * S].bitcast(BF16).rearrange("p (s i t) -> p s i t", s=4, i=3)
        fold = sb("fold", [P, 2, S])
        decay = sb("decay", [P, TW])
        unfold = sb("unfold", [P, TW])
        corner = sb("corner", [P, P])
        head_ones = sb("head_ones", [P, H])
        qk_sums = sb("qk_sums", [P, 2 * G])
        sq_max = sb("sq_max", [H, 2 * G])
        bound = sb("bound", [P, 8])
        flag = sb("flag", [1, 1], I32)
        minus_bound = sb("minus_bound", [P, 1])
        evac = [sb(f"evac{u}", [P, GW]) for u in range(2)]
        o_sum = [sb(f"o_sum{u}", [P, QT // 2, 2, HD + 1]) for u in range(2)]
        o_inv = sb("o_inv", [P, 2, QT])
        sc = [ring[:, u * S:(u + 1) * S] for u in range(2)]
        pr = [ring[:, (2 + u) * S:(3 + u) * S] for u in range(2)]
        prT = [ring[:, (4 + u) * S:(5 + u) * S] for u in range(2)]
        row = sb("row", [P, 2, 4])
        oT = big[:, 0:T]


        w_router = sb("w_router", [P, NE])
        b_router = sb("b_router", [P, NE])
        w_shared = sb("w_shared", [P, EI])
        wd_shared = sb("wd_shared", [EI, D])
        gates = big[:, 2 * T:2 * T + NT * NE].rearrange("p (t e) -> p t e", t=NT)
        rest = sb("rest", [P, TPG, NE])
        top = sb("top", [P, NT, 8])
        top_sum = sb("top_sum", [P, NT])
        top_inv = sb("top_inv", [P, NT])
        cT = big[:, 0:2 * T].rearrange("p (a t) -> p a t", a=2)
        c_part = ring[:, 0:3 * GW].bitcast(BF16).rearrange("p (a i t) -> p a i t", a=2, i=3)
        c_dram = dram("c_parts", [NE * 3, T], BF16)
        spread = sb("spread", [P, P], BF16)
        c_rows = [ring[:, (3 + u) * S:(4 + u) * S].bitcast(BF16) for u in range(2)]
        w_exp = [sb(f"w_exp{u}", [P, 2 * D]) for u in range(2)]
        act_out = [ring[:, 5 * S + u * GW:5 * S + (u + 1) * GW] for u in range(2)]
        hid = [ring[:, 6 * S + u * GW:6 * S + (u + 1) * GW] for u in range(2)]
        accT = big[:, 0:T]

        w_tok = sb("w_tok", [P, 3])
        b_tok = sb("b_tok", [1, 3])
        m0 = sb("m0", [P, D])
        vg1T = sb("vg1T", [P, D])
        vg2 = sb("vg2", [P, D])
        vg2T = sb("vg2T", [P, D])
        ones = sb("ones", [P, P])
        root = sb("root", [P, NT])
        state = [sb(f"state{b}", [P, 2 * D]) for b in range(B)]
        kept = [sb(f"kept{b}", [P, 2 * D]) for b in range(B)]
        vg2_cat = sb("vg2_cat", [P, 2 * D])
        tok = big[0:1, 0:2 * T]
        squares = big[:, 2 * T:3 * T]
        inv_norm = sb("inv_norm", [P, NT])
        by_half = sb("by_half", [P, NT, 2])
        x_mean = sb("x_mean", [P, B * NCH])
        k_mean = sb("k_mean", [P, B * NCH])
        one_row = sb("one_row", [1, 6 * B * NCH])
        steps = sb("steps", [P, NCH, B, 3])
        steps_flat = steps[:, :, :, :].rearrange("p n b c -> p (n b c)")
        step = [sb(f"step{u}", [P, B * 3]) for u in range(2)]
        silu_z = [sb(f"silu_z{b}", [P, CH]) for b in range(B)]
        h_sum = [sb(f"h_sum{b}", [P, 1]) for b in range(B)]
        m_sq = sb("m_sq", [P, B, D])
        m_norm = sb("m_norm", [P, 4, B])
        memT = big[:, 3 * T:4 * T]

        def across(ap, n):
            return bass.AP(ap.tensor, ap.offset, [list(ap.ap[0]), [0, n]])

        w_gate2 = sb("w_gate2", [P, NE2])
        r_max = sb("r_max", [P, NT])
        r_sum = sb("r_sum", [P, NT])
        soft = sb("soft", [P, NT, NE2])
        padded = sb("padded", [P, 2, NT, 16])
        best = sb("best", [P, 2, NT, 8])
        taken = sb("taken", [P, 2, NT, 8])
        marked = sb("marked", [P, 2, NT, 16])
        combine2 = sb("combine2", [P, NT, NE2])
        c2T = big[0:NE2, 0:T]
        c2_dram = dram("c2_parts", [NE2 * 3, T], BF16)
        spread2 = sb("spread2", [P, P], BF16)
        w_ffn = [sb(f"w_ffn{u}", [P, 3 * D]) for u in range(2)]
        gated = [ring[:, 7 * S + u * GW:7 * S + (u + 1) * GW] for u in range(2)]

        q_dram = [dram(f"q_parts{s}", [NH, 5, HD, S], BF16) for s in range(2)]
        k_dram = [dram(f"k_parts{s}", [NH, 3, HD, S], BF16) for s in range(2)]

        x_loaded = sem("x_loaded")
        w_loaded = sem("w_loaded")
        consts = sem("consts")
        table = sem("table")
        dve_link = sem("dve_link")
        act_link = sem("act_link")
        pool_link = sem("pool_link")
        var_ready = sem("var_ready")
        rstd_ready = sem("rstd_ready")
        xn_ready = sem("xn_ready")
        xnT_psum = sem("xnT_psum")
        xnT_ready = sem("xnT_ready")
        stored = sem("stored")
        q_psum = sem("q_psum")
        kv_psum = sem("kv_psum")
        kv_ready = sem("kv_ready")
        lat_psum = sem("lat_psum")
        lat_ready = sem("lat_ready")
        k_psum = sem("k_psum")
        v_psum = sem("v_psum")
        q_ready = sem("q_ready")
        k_ready = sem("k_ready")
        v_ready = sem("v_ready")
        parts_ready = sem("parts_ready")
        parts_saved = sem("parts_saved")
        stacks_zero = sem("stacks_zero")
        stacks_loaded = [sem(f"stacks_loaded{u}") for u in range(2)]
        sums_zero = sem("sums_zero")
        sq_psum = sem("sq_psum")
        qk_sq_ready = sem("qk_sq_ready")
        sq_taken = sem("sq_taken")
        pool_set = sem("pool_set")
        bound_psum = sem("bound_psum")
        bound_part = sem("bound_part")
        bound_sq = sem("bound_sq")
        bound_root = sem("bound_root")
        flag_ready = sem("flag_ready")
        first_half = sem("first_half")
        whole = sem("whole")
        corner_done = sem("corner_done")
        exp_done = sem("exp_done")
        pv_done = sem("pv_done")
        v_loaded = sem("v_loaded")
        evac_ready = sem("evac_ready")
        evacT_psum = sem("evacT_psum")
        head_ready = sem("head_ready")
        fast_link = sem("fast_link")
        slow_link = sem("slow_link")
        s_psum = sem("s_psum")
        s_clamped = sem("s_clamped")
        max_ready = sem("max_ready")
        exp_ready = sem("exp_ready")
        prT_psum = sem("prT_psum")
        prT_ready = sem("prT_ready")
        o_psum = sem("o_psum")
        o_ready = sem("o_ready")
        o_all = sem("o_all")
        oT_psum = sem("oT_psum")
        oT_ready = sem("oT_ready")
        y_psum = sem("y_psum")
        x_ready = sem("x_ready")
        w3_loaded = sem("w3_loaded")
        logit2_psum = sem("logit2_psum")
        shifted = sem("shifted")
        exp2_ready = sem("exp2_ready")
        combine2_ready = sem("combine2_ready")
        c2T_psum = sem("c2T_psum")
        c2T_ready = sem("c2T_ready")
        c2_split = sem("c2_split")
        c2_saved = sem("c2_saved")
        ffn_zero = sem("ffn_zero")
        ffn_loaded = [sem(f"ffn_loaded{u}") for u in range(2)]
        gate_z = sem("gate_z")
        up_z = sem("up_z")
        c2_psum = sem("c2_psum")
        silu2_ready = sem("silu2_ready")
        gated_ready = sem("gated_ready")
        hid2_ready = sem("hid2_ready")
        down2_done = sem("down2_done")
        acc2_done = sem("acc2_done")
        accT2_ready = sem("accT2_ready")
        acc2_psum = sem("acc2_psum")
        w2_loaded = sem("w2_loaded")
        tok_psum = sem("tok_psum")
        tok_ready = sem("tok_ready")
        sq_ready = sem("sq_ready")
        root_ready = sem("root_ready")
        by_half_ready = sem("by_half_ready")
        km_psum = sem("km_psum")
        km_ready = sem("km_ready")
        gate_psum = sem("gate_psum")
        gate_row = sem("gate_row")
        scalars_ready = sem("scalars_ready")
        scalars_psum = sem("scalars_psum")
        steps_ready = sem("steps_ready")
        fold_psum = sem("fold_psum")
        fold_ready = sem("fold_ready")
        step_ready = sem("step_ready")
        state_ready = [sem(f"state_ready{b}") for b in range(B)]
        mz_psum = [sem(f"mz_psum{b}") for b in range(B)]
        mz_silu = [sem(f"mz_silu{b}") for b in range(B)]
        err_psum = [sem(f"err_psum{b}") for b in range(B)]
        out_psum = [sem(f"out_psum{b}") for b in range(B)]
        out_taken = [sem(f"out_taken{b}") for b in range(B)]
        rows_ready = sem("rows_ready")
        norm_psum = sem("norm_psum")
        norm_sq = sem("norm_sq")
        norm_ready = sem("norm_ready")
        mem_psum = sem("mem_psum")
        w1_loaded = sem("w1_loaded")
        shared_psum = sem("shared_psum")
        shared_act = sem("shared_act")
        shared_down = sem("shared_down")
        logit_psum = sem("logit_psum")
        logit_ready = sem("logit_ready")
        gate_ready = sem("gate_ready")
        combine_ready = sem("combine_ready")
        cT_psum = sem("cT_psum")
        cT_ready = sem("cT_ready")
        c_split = sem("c_split")
        c_split_b = sem("c_split_b")
        c_saved = sem("c_saved")
        moe_zero = sem("moe_zero")
        exp_loaded = [sem(f"exp_loaded{u}") for u in range(2)]
        z_psum = sem("z_psum")
        silu_ready = sem("silu_ready")
        cb_psum = sem("cb_psum")
        hid_ready = sem("hid_ready")
        down_done = sem("down_done")
        acc_done = sem("acc_done")
        accT_ready = sem("accT_ready")
        acc_psum = sem("acc_psum")

        def x_dram(t):
            return t.rearrange("b (t p) d -> p (b t) d", p=P)

        def ready(eng, s, n):
            eng.wait_ge(s, n + (1 + CREDIT))

        def free(eng, s, n, buffers=2):
            eng.wait_ge(s, n + (1 + CREDIT - buffers))

        block = ctx.enter_context(nc.Block())

        @block.sync
        def _(sp):
            for g in range(G):
                ts = slice(g * TPG, (g + 1) * TPG)
                sp.dma_start(x[:, ts, :], x_dram(a["x"])[:, ts, :]).then_inc(x_loaded, 16)
            for dst, src in ((wq[:], "wq"), (wk[:], "wk"), (wv[:], "wv"), (wo[:], "wo"), (w_down[:], "w_down"),
                             (w_up[:, 0:D], "w_up_k"), (w_up[:, D:2 * D], "w_up_v")):
                sp.dma_start(dst, a[src]).then_inc(w_loaded, 16)
            for dst, src in ((w_router[:], a["w_router"]), (w_shared[:], a["w_shared"]), (wd_shared[:], a["wd_shared"]),
                             (b_router[:], bass.AP(a["b_router"].tensor, 0, [[0, P], [1, NE]]))):
                sp.dma_start(dst, src).then_inc(w1_loaded, 16)
            for dst, src in ((w_tok[:], "w_tok"), (b_tok[:], "b_tok"), (m0[:], "m0"), (state[0][:, 0:D], "m0T"),
                             (state[1][:, 0:D], "m0T"), (vg1T[:], "vg1T"), (vg2[:], "vg2"), (vg2T[:], "vg2T")):
                sp.dma_start(dst, a[src]).then_inc(w2_loaded, 16)
            sp.dma_start(w_gate2[:], a["w_gate2"]).then_inc(w3_loaded, 16)
            for b in range(B):
                sp.wait_ge(parts_ready, 2 * b + 2)
                sp.wait_ge(pool_set, 2 * b + 2)
                for w, drams in ((0, q_dram), (2, k_dram)):
                    for v in range(2):
                        rows = drams[v][b * H:(b + 1) * H]
                        for i in range(rows.shape[1]):
                            sp.dma_start(rows[:, i], parts[:, w + v, i % 3, :]).then_inc(parts_saved, 16)
            sp.wait_ge(parts_saved, B * 16 * 16)
            sp.wait_ge(stacks_zero, 1)

            def load_stacks(n, u):
                for v in range(2):
                    sp.dma_start(q_stack[v][u][0:PAIRS * HD, :], bass.AP(q_dram[v].tensor, n * (5 * HD * S),
                                                                         [[HD * S, 3], [S, 3 * HD], [1, S]]))\
                        .then_inc(stacks_loaded[u], 16)
                    sp.dma_start(k_stack[v][u][0:PAIRS * HD, :], bass.AP(k_dram[v].tensor, n * (3 * HD * S),
                                                                         [[0, 3], [S, 3 * HD], [1, S]]))\
                        .then_inc(stacks_loaded[u], 16)

            load_stacks(0, 0)
            load_stacks(1, 1)
            sp.wait_ge(flag_ready, 1)
            fast = sp.value_load(flag[0:1, 0:1], min_val=0, max_val=1)
            with sp.If(fast == 1):
                with sp.Fori(0, NH // 2 - 1) as i:
                    for u in range(2):
                        ready(sp, whole, i * (2 * QT) + ((u + 1) * QT - 1))
                        load_stacks(i * 2 + (2 + u), u)
            with sp.Else():
                with sp.Fori(0, NH // 2 - 1) as i:
                    for u in range(2):
                        ready(sp, s_psum, i * (2 * QT) + ((u + 1) * QT - 1))
                        load_stacks(i * 2 + (2 + u), u)

            for g in range(G):
                cols = slice(g * GW, (g + 1) * GW)
                sp.wait_ge(c_split, g + 1)
                sp.dma_start(bass.AP(c_dram.tensor, g * GW, [[3 * T, P], [T, 3], [1, GW]]), c_part[:, 0, :, :])\
                    .then_inc(c_saved, 16)
                sp.wait_ge(c_split_b, g + 1)
                sp.dma_start(bass.AP(c_dram.tensor, P * 3 * T + g * GW, [[3 * T, NE - P], [T, 3], [1, GW]]),
                             c_part[0:NE - P, 1, :, :]).then_inc(c_saved, 16)
            sp.wait_ge(c_saved, G * 32)
            sp.wait_ge(moe_zero, 1)

            def load_experts(m, u):
                sp.dma_start(w_exp[u][:], a["w_exp"][bass.ds(m, 1), :, :].rearrange("m p n -> p (m n)")).then_inc(exp_loaded[u], 16)
                sp.dma_start(c_rows[u][0:6, :], c_dram[bass.ds(m * 6, 6), :]).then_inc(exp_loaded[u], 16)

            load_experts(0, 0)
            sp.wait_ge(down_done, 1 + CREDIT)
            load_experts(1, 1)
            with sp.Fori(0, MT_N // 2 - 1) as i:
                for u in range(2):
                    sp.wait_ge(down_done, i * 8 + (4 * (2 + u) - 3 + CREDIT))
                    load_experts(i * 2 + (2 + u), u)
            for g in range(G):
                sp.wait_ge(c2_split, g + 1)
                sp.dma_start(bass.AP(c2_dram.tensor, g * GW, [[3 * T, NE2], [T, 3], [1, GW]]), c_part[0:NE2, 0, :, :])\
                    .then_inc(c2_saved, 16)
            sp.wait_ge(c2_saved, G * 16)
            sp.wait_ge(ffn_zero, 1)

            def load_ffn(m, e, u):
                sp.dma_start(w_ffn[u][:], a["w_ffn"][bass.ds(m, 1), :, :].rearrange("m p n -> p (m n)")).then_inc(ffn_loaded[u], 16)
                sp.dma_start(c_rows[u][0:3, :], c2_dram[bass.ds(e * 3, 3), :]).then_inc(ffn_loaded[u], 16)

            load_ffn(0, 0, 0)
            sp.wait_ge(down2_done, 1 + CREDIT)
            load_ffn(1, 0, 1)
            with sp.Fori(0, NE2 - 1) as i:
                for u in range(2):
                    sp.wait_ge(down2_done, i * 8 + (4 * (2 + u) - 3 + CREDIT))
                    load_ffn(i * 2 + (2 + u), i + 1, u)
            for g in range(G):
                ts = slice(g * TPG, (g + 1) * TPG)
                sp.wait_ge(x_ready, G * 3 + g + 1)
                sp.dma_start(x_dram(out)[:, ts, :], x[:, ts, :]).then_inc(stored, 16)
            sp.wait_ge(stored, 16 * G)

        @block.gpsimd
        def _(pool):
            link = Link(pool, pool_link)
            link(pool.memset(ident[:], 0.0))
            pool.affine_select(out=ident[:], in_=ident[:], compare_op=ALU.not_equal, fill=1.0, base=0,
                               pattern=[[-1, P]], channel_multiplier=1).then_inc(consts, 1)
            link(pool.memset(half[:], -0.5))
            link(pool.memset(root[:], 0.5))
            link(pool.memset(ones[:], 1.0))
            link(pool.memset(by_half[:], 0.0))
            pool.iota(distance, [[1, TW]], base=-(S - P), channel_multiplier=-1).then_inc(table, 1)
            pool.iota(time, [[1, S]], base=-(S // 2), channel_multiplier=0).then_inc(table, 1)
            link(pool.memset(head_ones[:], 1.0))
            link(pool.affine_select(out=head_ones[:], in_=head_ones[:], compare_op=ALU.is_ge, fill=0.0, base=0,
                                    pattern=[[-HD, H]], channel_multiplier=1))
            link(pool.affine_select(out=head_ones[:], in_=head_ones[:], compare_op=ALU.is_ge, fill=0.0, base=HD - 1,
                                    pattern=[[HD, H]], channel_multiplier=-1))
            for u in range(2):
                for v in range(2):
                    link.sign(pool.memset(q_stack[v][u][:], 0.0))
                    link.sign(pool.memset(k_stack[v][u][:], 0.0))
                link(pool.memset(v_cur[u][:], 0.0))
                link.sign(pool.memset(v_cur[u][:, :, HD:HD + 1], 1.0))
            link.sign(pool.memset(evac[1][:], 1.0))
            link.sign(pool.memset(ring[:, 6 * S:8 * S], 0.0))
            link.wait()
            pool.sem_inc(stacks_zero, 1)

            def norm(k):
                for g in range(G):
                    ts = slice(g * TPG, (g + 1) * TPG)
                    pool.wait_ge(var_ready, G * k + g + 1)
                    link(pool.tensor_scalar(rstd[:, ts], mv[:, ts, 1], EPS, None, ALU.add))
                    pool.tensor_tensor(rstd[:, ts], rstd[:, ts], half[:, ts], ALU.pow).then_inc(rstd_ready, 1)

            norm(0)
            for g in range(G):
                o = (g % 2) * GW
                pool.wait_ge(k_ready, g + 1)
                pool.wait_ge(table, 5)
                if g == 2:
                    pool.wait_ge(parts_saved, 16 * 16)
                link(pool.tensor_tensor(folded[:, 3, :], qk_f[:, 1, :], fold[:, 1, o:o + GW], ALU.mult))
                for i in range(3):
                    ins = pool.tensor_copy(parts[:, 3, i, o:o + GW], folded[:, 3, :])
                    if i < 2:
                        link(ins)
                        link(pool.tensor_tensor(folded[:, 3, :], folded[:, 3, :], parts[:, 3, i, o:o + GW], ALU.subtract))
                ins.then_inc(pool_set, 1)
            pool.wait_ge(bound_sq, 1)
            pool.tensor_tensor(bound[0:1, 1:2], bound[0:1, 0:1], root[0:1, 0:1], ALU.pow).then_inc(bound_root, 1)
            pool.wait_ge(flag_ready, 1)
            pool.wait_ge(v_ready, G)
            fast = pool.value_load(flag[0:1, 0:1], min_val=0, max_val=1)

            def take_values(n, u):
                pool.tensor_copy(v_cur[u][:, :, 0:HD], v_flat[:, bass.ds(n * (QT * HD), QT * HD)].rearrange("p (t d) -> p t d", t=QT))\
                    .then_inc(v_loaded, 1)

            with pool.If(fast == 1):
                take_values(0, 0)
                take_values(1, 1)
                with pool.Fori(0, NH // 2 - 1) as i:
                    for u in range(2):
                        pool.wait_ge(pv_done, i * (2 * QT) + ((u + 1) * QT + RING))
                        take_values(i * 2 + (2 + u), u)
            with pool.Else():
                take_values(0, 0)
                take_values(1, 1)
                with pool.Fori(0, NH // 2 - 1) as i:
                    for u in range(2):
                        ready(pool, o_psum, i * (2 * QT) + ((u + 1) * QT - 1))
                        take_values(i * 2 + (2 + u), u)

            for e in range(2):
                half_cols = spread[:, e * EI:(e + 1) * EI]
                link(pool.memset(half_cols, 1.0))
                link(pool.affine_select(out=half_cols, in_=half_cols, compare_op=ALU.is_ge, fill=0.0, base=-3 * e,
                                        pattern=[[0, EI]], channel_multiplier=1))
                link(pool.affine_select(out=half_cols, in_=half_cols, compare_op=ALU.is_ge, fill=0.0, base=3 * e + 2,
                                        pattern=[[0, EI]], channel_multiplier=-1))
            pool.wait_ge(o_all, 1)
            for u in range(2):
                link.sign(pool.memset(c_rows[u], 0.0))
            link.sign(pool.memset(w_exp[1][:, D:2 * D], 0.0))
            link.sign(pool.memset(hid[1], 0.0))
            link.wait()
            pool.sem_inc(moe_zero, 1)
            norm(1)
            for g in range(G):
                v = cT[0:NE - P, 1, g * GW:(g + 1) * GW]
                left = c_part[0:NE - P, 1]
                pool.wait_ge(cT_ready, 2 * g + 2)
                if g:
                    pool.wait_ge(c_saved, 32 * g)
                link(pool.tensor_copy(left[:, 0, :], v))
                link(pool.tensor_tensor(v, v, left[:, 0, :], ALU.subtract))
                link(pool.tensor_copy(left[:, 1, :], v))
                link(pool.tensor_tensor(v, v, left[:, 1, :], ALU.subtract))
                pool.tensor_copy(left[:, 2, :], v).then_inc(c_split_b, 1)

            norm(2)
            pool.wait_ge(sq_ready, 1)
            pool.tensor_tensor(inv_norm[:], inv_norm[:], root[:], ALU.pow).then_inc(root_ready, 1)
            pool.wait_ge(steps_ready, 1)
            pool.sem_inc(step_ready, CREDIT)
            pool.sem_inc(norm_ready, CREDIT)
            with pool.Fori(0, NCH // 2) as i:
                for u in range(2):
                    n = i * 2 + u
                    free(pool, norm_psum, n)
                    pool.tensor_copy(step[u][:], steps_flat[:, bass.ds(i * (2 * B * 3) + u * (B * 3), B * 3)])\
                        .then_inc(step_ready, 1)
                    ready(pool, norm_sq, n)
                    pool.tensor_tensor(m_norm[:, 2, :], m_norm[:, 1, :], root[:, 0:B], ALU.pow).then_inc(norm_ready, 1)

            link(pool.memset(spread2[:], 1.0))
            link(pool.affine_select(out=spread2[:], in_=spread2[:], compare_op=ALU.is_ge, fill=0.0, base=2,
                                    pattern=[[0, P]], channel_multiplier=-1))
            link.sign(pool.memset(padded[:], -1.0))
            link.sign(pool.memset(taken[:], -1.0))
            link.sign(pool.memset(w_ffn[1][:, 2 * D:3 * D], 0.0))
            pool.wait_ge(acc_done, 1)
            link.sign(pool.memset(hid[1], 0.0))
            link.wait()
            pool.sem_inc(ffn_zero, 1)
            norm(3)

        @block.scalar
        def _(act):
            link = Link(act, act_link)
            act.wait_ge(table, 2)
            link(act.activation(decay[:], distance, ACT.Abs))
            act.activation(decay[:], decay[:], ACT.Exp, scale=-DECAY).then_inc(table, 1)
            act.activation(unfold[:], distance, ACT.Exp, scale=-DECAY).then_inc(table, 1)
            link(act.activation(fold[:, 0, :], time, ACT.Exp, scale=-DECAY))
            act.activation(fold[:, 1, :], time, ACT.Exp, scale=DECAY).then_inc(table, 1)

            def norm(k):
                for g in range(G):
                    n = G * k + g
                    act.wait_ge(xnT_psum, n + 1)
                    act.activation(xnT[:, g * GW:(g + 1) * GW], bank(n % 2), ACT.Copy).then_inc(xnT_ready, 1)

            norm(0)
            for g in range(G):
                act.wait_ge(kv_psum, g + 1)
                act.activation(kvT, bank(3), ACT.Copy).then_inc(kv_ready, 1)
                act.wait_ge(q_psum, g + 1)
                if g:
                    act.wait_ge(parts_ready, g)
                    act.wait_ge(pool_set, g)
                act.activation(qk_f[:, 0, :], bank(2), ACT.Copy, scale=SCALE).then_inc(q_ready, 1)
                act.wait_ge(lat_psum, g + 1)
                act.activation(latT, bank(4)[0:LAT, :], ACT.Copy).then_inc(lat_ready, 1)
                act.wait_ge(k_psum, g + 1)
                act.activation(qk_f[:, 1, :], bank(5), ACT.Copy).then_inc(k_ready, 1)
                act.wait_ge(v_psum, g + 1)
                b, t0 = g // 2, (g % 2) * TPG
                for t in range(TPG):
                    ins = act.activation(v_heads[:, b * H:(b + 1) * H, t0 + t, :],
                                         bank(6)[:, t * P:(t + 1) * P].rearrange("p (h d) -> p h d", h=H), ACT.Copy)
                ins.then_inc(v_ready, 1)
                act.wait_ge(k_ready, g + 1)
                if g:
                    act.wait_ge(sq_psum, 2 * g)
                for w in range(2):
                    act.activation(qk_sq[:, w, :], qk_f[:, w, :], ACT.Square,
                                   accum_out=qk_sums[:, w * G + g:w * G + g + 1]).then_inc(qk_sq_ready, 1)

            act.wait_ge(flag_ready, 1)
            fast = act.value_load(flag[0:1, 0:1], min_val=0, max_val=1)
            with act.If(fast == 1):
                act.sem_inc(exp_done, CREDIT)
                with act.Fori(0, NH // 2) as i:
                    for c in range(2 * QT):
                        n = i * (2 * QT) + c
                        ready(act, corner_done, n)
                        ready(act, whole, n)
                        act.wait_ge(pv_done, n + 1)
                        act.activation(ring[:, c % RING * S:(c % RING + 1) * S], wide[c % 2][:], ACT.Exp,
                                       bias=minus_bound[:]).then_inc(exp_done, 1)
            with act.Else():
                act.sem_inc(exp_ready, CREDIT)
                act.sem_inc(prT_ready, CREDIT)
                with act.Fori(0, NH // 2) as i:
                    for c in range(2 * QT + 1):
                        if c < 2 * QT:
                            n = i * (2 * QT) + c
                            ready(act, max_ready, n)
                            free(act, prT_psum, n)
                            free(act, o_ready, n)
                            act.activation(pr[c % 2], sc[c % 2], ACT.Exp, bias=row[:, c % 2, 1:2],
                                           accum_out=row[:, c % 2, 2:3]).then_inc(exp_ready, 1)
                        if c >= 1:
                            n = i * (2 * QT) + (c - 1)
                            ready(act, prT_psum, n)
                            free(act, o_psum, n)
                            act.activation(prT[(c - 1) % 2], wide[2][:], ACT.Copy).then_inc(prT_ready, 1)

            for g in range(G):
                act.wait_ge(oT_psum, g + 1)
                act.activation(oT[:, g * GW:(g + 1) * GW], bank(g % 2), ACT.Copy).then_inc(oT_ready, 1)

            norm(1)
            for g in range(G):
                act.wait_ge(shared_psum, g + 1)
                if g >= 2:
                    act.wait_ge(shared_down, g - 1)
                act.activation(act_out[g % 2][0:EI], bank(4 + g % 2)[0:EI, :], ACT.Silu).then_inc(shared_act, 1)
            for t in range(NT):
                act.wait_ge(logit_ready, t + 1)
                act.activation(gates[:, t, :], gates[:, t, :], ACT.Sigmoid).then_inc(gate_ready, 1)
            for g in range(G):
                cols = slice(g * GW, (g + 1) * GW)
                act.wait_ge(cT_psum, g + 1)
                act.activation(cT[:, 0, cols], bank(4), ACT.Copy).then_inc(cT_ready, 1)
                act.activation(cT[0:NE - P, 1, cols], bank(5)[0:NE - P, :], ACT.Copy).then_inc(cT_ready, 1)
            act.sem_inc(silu_ready, CREDIT)
            with act.Fori(0, MT_N // 2) as i:
                for c in range(2 * G):
                    n = i * (2 * G) + c
                    ready(act, z_psum, n)
                    free(act, hid_ready, n)
                    act.activation(act_out[c % 2], bank(4 + c % 2), ACT.Silu).then_inc(silu_ready, 1)
            for g in range(G):
                act.wait_ge(acc_done, 1)
                act.activation(accT[:, g * GW:(g + 1) * GW], bank(g), ACT.Copy).then_inc(accT_ready, 1)

            norm(2)
            act.wait_ge(w2_loaded, 8 * 16)
            for g in range(G):
                for k in range(2):
                    act.wait_ge(tok_psum, 2 * g + k + 1)
                    act.activation(tok[:, k * T + g * GW:k * T + (g + 1) * GW], bank(2 + k)[0:1, :], ACT.Sigmoid,
                                   bias=b_tok[:, k:k + 1]).then_inc(tok_ready, 1)
            act.wait_ge(gate_psum, 1)
            act.activation(one_row[:, 0:B * NCH], bank(5)[0:1, 0:B * NCH], ACT.Sigmoid, bias=b_tok[:, 2:3]).then_inc(gate_row, 1)
            act.wait_ge(fold_psum, 1)
            link(act.activation(vg2_cat[:, 0:D], vg2T[:], ACT.Copy, scale=1.0 / CH))
            act.activation(vg2_cat[:, D:2 * D], bank(7)[:, 0:D], ACT.Copy, scale=1.0 / CH).then_inc(fold_ready, 1)
            for b in range(B):
                act.activation(state[b][:, D:2 * D], bank(7)[:, D:2 * D], ACT.Copy).then_inc(fold_ready, 1)
            for b in range(B):
                act.sem_inc(mz_silu[b], CREDIT)
                act.sem_inc(out_taken[b], CREDIT)
            with act.Fori(0, NCH // 2) as i:
                for u in range(2):
                    n = i * 2 + u
                    for b in range(B):
                        ready(act, mz_psum[b], n)
                        act.activation(silu_z[b][:], bank(b)[:, 0:CH], ACT.Silu, accum_out=h_sum[b][:]).then_inc(mz_silu[b], 1)
                    for b in range(B):
                        ready(act, out_psum[b], n)
                        act.activation(memT[:, bass.ds(i * (2 * CH) + (b * S + u * CH), CH)], bank(4 + b)[:, 0:CH],
                                       ACT.Copy).then_inc(out_taken[b], 1)

            norm(3)
            act.wait_ge(shifted, 1)
            act.activation(soft[:], soft[:], ACT.Exp).then_inc(exp2_ready, 1)
            for g in range(G):
                act.wait_ge(c2T_psum, g + 1)
                act.activation(c2T[:, g * GW:(g + 1) * GW], bank(g)[0:NE2, :], ACT.Copy).then_inc(c2T_ready, 1)
            act.sem_inc(silu2_ready, CREDIT)
            with act.Fori(0, NE2) as i:
                for c in range(2 * G):
                    n = i * (2 * G) + c
                    ready(act, gate_z, n)
                    free(act, gated_ready, n)
                    act.activation(act_out[c % 2], bank(4), ACT.Silu).then_inc(silu2_ready, 1)
            for g in range(G):
                act.wait_ge(acc2_done, 1)
                act.activation(accT[:, g * GW:(g + 1) * GW], bank(g), ACT.Copy).then_inc(accT2_ready, 1)

        @block.tensor
        def _(pe):
            pe.wait_ge(consts, 1)

            def norm(k):
                for g in range(G):
                    n = G * k + g
                    pe.wait_ge(xn_ready, n + 1)
                    if g >= 2:
                        pe.wait_ge(xnT_ready, n - 1)
                    for t in range(TPG):
                        ins = pe.transpose(bank(n % 2)[:, t * P:(t + 1) * P], xn[:, g * TPG + t, :], ident[:])
                    ins.then_inc(xnT_psum, 1)

            norm(0)
            pe.wait_ge(w_loaded, 7 * 16)
            for g in range(G):
                cols = xnT[:, g * GW:(g + 1) * GW]
                pe.wait_ge(xnT_ready, g + 1)
                if g:
                    pe.wait_ge(kv_ready, g)
                pe.matmul(bank(3), wk[:], cols, start=True, stop=False)
                pe.matmul(bank(3), wv[:], cols, start=False, stop=True).then_inc(kv_psum, 1)
                if g:
                    pe.wait_ge(q_ready, g)
                pe.matmul(bank(2), wq[:], cols, start=True, stop=True).then_inc(q_psum, 1)
                pe.wait_ge(kv_ready, g + 1)
                if g:
                    pe.wait_ge(lat_ready, g)
                pe.matmul(bank(4)[0:LAT, :], w_down[:], kvT, start=True, stop=True).then_inc(lat_psum, 1)
                pe.wait_ge(lat_ready, g + 1)
                if g:
                    pe.wait_ge(k_ready, g)
                pe.matmul(bank(5), w_up[:, 0:D], latT, start=True, stop=True).then_inc(k_psum, 1)
                if g:
                    pe.wait_ge(v_ready, g)
                for t in range(TPG):
                    ins = pe.matmul(bank(6)[:, t * P:(t + 1) * P], latT[:, t * P:(t + 1) * P], w_up[:, D:2 * D],
                                    start=True, stop=True)
                ins.then_inc(v_psum, 1)
                for w in range(2):
                    pe.wait_ge(qk_sq_ready, 2 * g + w + 1)
                    if g:
                        pe.wait_ge(sq_taken, 2 * (g - 1) + w + 1)
                    pe.matmul(bank(7 * w)[0:H, :], head_ones[:], qk_sq[:, w, :], start=True, stop=True).then_inc(sq_psum, 1)

            pe.matmul(bank(6)[0:1, 0:2 * G], ones[:, 0:1], qk_sums[:], start=True, stop=True).then_inc(bound_psum, 1)
            pe.wait_ge(bound_part, 1)
            pe.transpose(bank(5)[0:1, 0:H], bound[0:H, 4:5], ident[0:H, 0:H]).then_inc(bound_psum, 1)
            pe.wait_ge(bound_root, 1)
            pe.matmul(bank(4)[:, 0:1], ones[0:1, :], bound[0:1, 1:2], start=True, stop=True).then_inc(bound_psum, 1)

            pe.wait_ge(stacks_zero, 1)
            pe.wait_ge(flag_ready, 1)
            fast = pe.value_load(flag[0:1, 0:1], min_val=0, max_val=1)
            with pe.If(fast == 1):
                pe.sem_inc(first_half, CREDIT)
                pe.sem_inc(whole, CREDIT)
                pe.sem_inc(pv_done, RING)
                pe.sem_inc(evacT_psum, CREDIT)

                def scores(i, c):
                    n, u, k = i * (2 * QT) + c, c // QT % 2, c % QT
                    free(pe, exp_done, n)
                    keys = slice(k * P, (k + 1) * P)
                    if k == 0:
                        pe.wait_ge(stacks_loaded[u], i * 64 + 64 * (1 + c // (2 * QT)))
                    for j, h in enumerate((k // 4, 1 - k // 4)):
                        lo, hi, mid = h * 512, (h + 1) * 512, min(max(k * P, h * 512), (h + 1) * 512)
                        if mid > lo:
                            ins = pe.matmul(wide[c % 2][:, lo:mid], k_stack[0][u][:, keys], q_stack[1][u][:, lo:mid],
                                            start=True, stop=True)
                        if hi > mid:
                            ins = pe.matmul(wide[c % 2][:, mid:hi], k_stack[1][u][:, keys], q_stack[0][u][:, mid:hi],
                                            start=True, stop=True)
                        ins.then_inc((first_half, whole)[j], 1)

                def products(i, c):
                    u = c // QT
                    ready(pe, exp_done, i * (2 * QT) + c)
                    if c % QT == 1:
                        ready(pe, v_loaded, i * 2 + (u - CREDIT))
                        ready(pe, evac_ready, i * 2 + (u - 1))
                    for s_ in (c - 1, c):
                        for h in range(2):
                            at = 32 * (2 * (s_ % 2) + h)
                            ins = pe.matmul(bank(4 + u)[at:at + 32, :], v_cur[u][:, s_ % QT, :],
                                            ring[:, s_ % RING * S + h * 512:s_ % RING * S + (h + 1) * 512],
                                            start=(s_ % QT < 2), stop=(s_ % QT >= QT - 2), skip_group_check=True)
                        ins.then_inc(pv_done, 1)

                def turn(n, u):
                    ready(pe, evac_ready, n)
                    free(pe, head_ready, n)
                    for t in range(4):
                        ins = pe.transpose(bank(6 + u)[:, t * P:(t + 1) * P], evac[1 - u][:, t * P:(t + 1) * P], ident[:])
                    ins.then_inc(evacT_psum, 1)

                def body(i, last):
                    for c in range(2 * QT):
                        if not last or c + 2 < 2 * QT:
                            scores(i, c + 2)
                        if c % 2:
                            products(i, c)
                        if c % QT == 1:
                            turn(i * 2 + c // QT, c // QT)

                scores(0, 0)
                scores(0, 1)
                with pe.Fori(0, NH // 2 - 1) as i:
                    body(i, False)
                body(NH // 2 - 1, True)
                turn(NH, 0)
            with pe.Else():
                pe.sem_inc(s_psum, CREDIT)
                pe.sem_inc(prT_psum, CREDIT)
                pe.sem_inc(o_psum, CREDIT)
                with pe.Fori(0, NH // 2) as i:
                    for c in range(2 * QT + 2):
                        if c < 2 * QT:
                            n, u, q = i * (2 * QT) + c, c // QT, c % QT
                            if q == 0:
                                pe.wait_ge(stacks_loaded[u], i * 64 + 64)
                            free(pe, s_clamped, n)
                            for k in range(S // 512):
                                ins = pe.matmul(wide[c % 2][:, k * 512:(k + 1) * 512], q_stack[0][u][:, q * P:(q + 1) * P],
                                                k_stack[1][u][:, k * 512:(k + 1) * 512], start=True, stop=True)
                            ins.then_inc(s_psum, 1)
                        if 1 <= c < 2 * QT + 1:
                            n = i * (2 * QT) + (c - 1)
                            ready(pe, exp_ready, n)
                            free(pe, prT_ready, n, 1)
                            for k in range(QT):
                                ins = pe.transpose(wide[2][:, k * P:(k + 1) * P], pr[(c - 1) % 2][:, k * P:(k + 1) * P], ident[:])
                            ins.then_inc(prT_psum, 1)
                        if c >= 2:
                            n, u = i * (2 * QT) + (c - 2), (c - 2) // QT
                            if c % QT == 2:
                                pe.wait_ge(v_loaded, i * 2 + (u + 1))
                            ready(pe, prT_ready, n)
                            free(pe, o_ready, n)
                            for k in range(QT):
                                ins = pe.matmul(bank(6 + c % 2)[:, 0:HD], prT[c % 2][:, k * P:(k + 1) * P],
                                                v_cur[u][:, k, 0:HD], start=(k == 0), stop=(k == QT - 1))
                            ins.then_inc(o_psum, 1)
            pe.wait_ge(o_all, 1)
            for g in range(G):
                b, q0 = g // 2, (g % 2) * TPG
                if g >= 2:
                    pe.wait_ge(oT_ready, g - 1)
                for t in range(TPG):
                    ins = pe.transpose(bank(g % 2)[:, t * P:(t + 1) * P],
                                       o_heads[:, q0 + t, 1 + b * H:1 + (b + 1) * H, :].rearrange("p n d -> p (n d)"), ident[:])
                ins.then_inc(oT_psum, 1)
            for g in range(G):
                pe.wait_ge(oT_ready, g + 1)
                if g >= 2:
                    pe.wait_ge(x_ready, g - 1)
                for t in range(TPG):
                    ins = pe.matmul(bank(2 + g % 2)[:, t * P:(t + 1) * P], oT[:, g * GW + t * P:g * GW + (t + 1) * P], wo[:],
                                    start=True, stop=True)
                ins.then_inc(y_psum, 1)

            norm(1)
            pe.wait_ge(w1_loaded, 4 * 16)
            pe.wait_ge(xnT_ready, 2 * G)
            for g in range(G):
                if g >= 2:
                    pe.wait_ge(shared_act, g - 1)
                pe.matmul(bank(4 + g % 2)[0:EI, :], w_shared[:], xnT[:, g * GW:(g + 1) * GW], start=True, stop=True)\
                    .then_inc(shared_psum, 1)
                pe.wait_ge(shared_act, g + 1)
                pe.matmul(bank(g), wd_shared[:], act_out[g % 2][0:EI], start=True, stop=False, skip_group_check=True)\
                    .then_inc(shared_down, 1)
            for t in range(NT):
                if t >= 2:
                    pe.wait_ge(logit_ready, t - 1)
                pe.matmul(bank(6 + t % 2)[:, 0:NE], xnT[:, t * P:(t + 1) * P], w_router[:], start=True, stop=True)\
                    .then_inc(logit_psum, 1)
            for g in range(G):
                pe.wait_ge(combine_ready, g + 1)
                if g:
                    pe.wait_ge(cT_ready, 2 * g)
                for t in range(TPG):
                    pe.transpose(bank(4)[:, t * P:(t + 1) * P], rest[:, t, 0:P], ident[:])
                    ins = pe.transpose(bank(5)[0:NE - P, t * P:(t + 1) * P], rest[:, t, P:NE], ident[:])
                ins.then_inc(cT_psum, 1)
            pe.wait_ge(moe_zero, 1)
            pe.wait_ge(cT_ready, 2 * G)
            for s_ in (z_psum, cb_psum, down_done):
                pe.sem_inc(s_, CREDIT)

            def down(u, c):
                return pe.matmul(bank(c % G), w_exp[u][:, D:2 * D], hid[c % 2], start=False, stop=False,
                                 skip_group_check=True)

            with pe.Fori(0, MT_N // 2) as i:
                for c in range(2 * G):
                    n, u, g = i * (2 * G) + c, c // G, c % G
                    cols = slice(g * GW, (g + 1) * GW)
                    if g == 0:
                        pe.wait_ge(exp_loaded[u], i * 32 + 32)
                    free(pe, silu_ready, n)
                    pe.matmul(bank(4 + c % 2), w_exp[u][:, 0:D], xnT[:, cols], start=True, stop=True).then_inc(z_psum, 1)
                    free(pe, hid_ready, n)
                    pe.matmul(bank(6 + c % 2), spread[:], c_rows[u][:, cols], start=True, stop=True).then_inc(cb_psum, 1)
                    ready(pe, hid_ready, n - 1)
                    down((c - 1) // G % 2, (c - 1) % (2 * G)).then_inc(down_done, 1)
            ready(pe, hid_ready, MT_N * G - 1)
            down(1, 2 * G - 1).then_inc(acc_done, 1)
            for g in range(G):
                pe.wait_ge(accT_ready, g + 1)
                for t in range(TPG):
                    ins = pe.transpose(bank(4 + g)[:, t * P:(t + 1) * P], accT[:, g * GW + t * P:g * GW + (t + 1) * P], ident[:])
                ins.then_inc(acc_psum, 1)

            norm(2)
            pe.wait_ge(w2_loaded, 8 * 16)
            pe.wait_ge(xnT_ready, 3 * G)
            pe.matmul(bank(7)[:, 0:D], vg2[:], vg1T[:], start=True, stop=True)
            pe.matmul(bank(7)[:, D:2 * D], m0[:], vg1T[:], start=True, stop=True).then_inc(fold_psum, 1)
            for g in range(G):
                for k in range(2):
                    if g:
                        pe.wait_ge(tok_ready, 2 * g + k - 1)
                    pe.matmul(bank(2 + k)[0:1, :], w_tok[:, k:k + 1], xnT[:, g * GW:(g + 1) * GW], start=True, stop=True)\
                        .then_inc(tok_psum, 1)
            pe.wait_ge(by_half_ready, 1)
            for t in range(NT):
                ins = pe.matmul(bank(4)[:, 2 * t:2 * t + 2], xn[:, t, :], by_half[:, t, :], start=True, stop=True)
            ins.then_inc(km_psum, 1)
            pe.wait_ge(km_ready, 1)
            pe.matmul(bank(5)[0:1, 0:B * NCH], w_tok[:, 2:3], k_mean[:], start=True, stop=True).then_inc(gate_psum, 1)
            pe.wait_ge(scalars_ready, 1)
            pe.matmul(bank(6)[:, 0:2 * B * NCH], ones[0:1, :], one_row[:, 4 * B * NCH:6 * B * NCH], start=True, stop=True)\
                .then_inc(scalars_psum, 1)
            pe.wait_ge(steps_ready, 1)
            pe.wait_ge(fold_ready, 1 + B)
            for b in range(B):
                pe.sem_inc(mz_psum[b], CREDIT)
                pe.sem_inc(err_psum[b], CREDIT)
                pe.sem_inc(out_psum[b], CREDIT)
            pe.sem_inc(norm_psum, CREDIT)
            with pe.Fori(0, NCH // 2) as i:
                for u in range(2):
                    n = i * 2 + u
                    for b in range(B):
                        chunk = xnT[:, bass.ds(i * (2 * CH) + (b * S + u * CH), CH)]
                        free(pe, state_ready[b], n, 1)
                        pe.matmul(bank(b)[:, 0:CH], state[b][:, D:2 * D], chunk, start=True, stop=True).then_inc(mz_psum[b], 1)
                        ready(pe, step_ready, n)
                        pe.matmul(bank(2 + b)[:, 0:2 * D], across(step[u][:, 3 * b + 2:3 * b + 3], P), state[b][:],
                                  start=True, stop=False)
                        free(pe, out_taken[b], n, 1)
                        pe.matmul(bank(4 + b)[:, 0:CH], state[b][:, 0:D], chunk, start=True, stop=False)
                    for b in range(B):
                        ready(pe, mz_silu[b], n)
                        pe.matmul(bank(2 + b)[:, 0:2 * D], across(h_sum[b][:], P), vg2_cat[:], start=False, stop=True)\
                            .then_inc(err_psum[b], 1)
                        pe.matmul(bank(4 + b)[:, 0:CH], vg2T[:], silu_z[b][:], start=False, stop=True).then_inc(out_psum[b], 1)
                    ready(pe, rows_ready, n)
                    pe.matmul(bank(6)[:, 0:B], ones[:], m_norm[:, 0, :], start=True, stop=True).then_inc(norm_psum, 1)
            for b in range(B):
                ready(pe, out_taken[b], NCH - 1)
            for g in range(G):
                for t in range(TPG):
                    ins = pe.transpose(bank(g)[:, t * P:(t + 1) * P], memT[:, g * GW + t * P:g * GW + (t + 1) * P], ident[:])
                ins.then_inc(mem_psum, 1)

            norm(3)
            pe.wait_ge(w3_loaded, 16)
            pe.wait_ge(xnT_ready, 4 * G)
            for t in range(NT):
                ins = pe.matmul(bank(4)[:, t * NE2:(t + 1) * NE2], xnT[:, t * P:(t + 1) * P], w_gate2[:], start=True, stop=True)
            ins.then_inc(logit2_psum, 1)
            pe.wait_ge(combine2_ready, 1)
            for g in range(G):
                for t in range(TPG):
                    ins = pe.transpose(bank(g)[0:NE2, t * P:(t + 1) * P], combine2[:, g * TPG + t, :], ident[:])
                ins.then_inc(c2T_psum, 1)
            pe.wait_ge(ffn_zero, 1)
            pe.wait_ge(c2T_ready, G)
            for s_ in (gate_z, up_z, c2_psum, down2_done):
                pe.sem_inc(s_, CREDIT)
            for g in range(G):
                pe.matmul(bank(g), w_ffn[1][:, 2 * D:3 * D], hid[1], start=True, stop=False, skip_group_check=True)

            def down2(u, c):
                return pe.matmul(bank(c % G), w_ffn[u][:, 2 * D:3 * D], hid[c % 2], start=False, stop=False,
                                 skip_group_check=True)

            with pe.Fori(0, NE2) as i:
                for c in range(2 * G):
                    n, u, g = i * (2 * G) + c, c // G, c % G
                    cols = slice(g * GW, (g + 1) * GW)
                    if g == 0:
                        pe.wait_ge(ffn_loaded[u], i * 32 + 32)
                    free(pe, silu2_ready, n, 1)
                    pe.matmul(bank(4), w_ffn[u][:, 0:D], xnT[:, cols], start=True, stop=True).then_inc(gate_z, 1)
                    free(pe, gated_ready, n, 1)
                    pe.matmul(bank(5), w_ffn[u][:, D:2 * D], xnT[:, cols], start=True, stop=True).then_inc(up_z, 1)
                    free(pe, hid2_ready, n, 1)
                    pe.matmul(bank(6), spread2[:], c_rows[u][:, cols], start=True, stop=True).then_inc(c2_psum, 1)
                    ready(pe, hid2_ready, n - 1)
                    down2((c - 1) // G % 2, (c - 1) % (2 * G)).then_inc(down2_done, 1)
            ready(pe, hid2_ready, FT_N * G - 1)
            down2(1, 2 * G - 1).then_inc(acc2_done, 1)
            for g in range(G):
                pe.wait_ge(accT2_ready, g + 1)
                for t in range(TPG):
                    ins = pe.transpose(bank(4 + g)[:, t * P:(t + 1) * P], accT[:, g * GW + t * P:g * GW + (t + 1) * P], ident[:])
                ins.then_inc(acc2_psum, 1)

        @block.vector
        def _(dve):
            link = Link(dve, dve_link)

            def norm(k):
                for g in range(G):
                    n = G * k + g
                    tiles = range(g * TPG, (g + 1) * TPG)
                    if k == 0:
                        dve.wait_ge(x_loaded, 16 * G)
                    else:
                        dve.wait_ge(x_ready, G * (k - 1) + g + 1)
                    for t in tiles:
                        link.sign(dve.bn_stats(stats[:, t, :], x[:, t, :]))
                    link.wait()
                    for t in tiles:
                        ins = dve.bn_aggr(mv[:, t, :], stats[:, t, :])
                        if t < tiles[-1]:
                            link.sign(ins)
                    link.wait()
                    ins.then_inc(var_ready, 1)
                    dve.wait_ge(rstd_ready, n + 1)
                    for t in tiles:
                        ins = dve.tensor_scalar(xn[:, t, :], x[:, t, :], mv[:, t, 0:1], rstd[:, t:t + 1], ALU.subtract, ALU.mult)
                        if t < tiles[-1]:
                            link.sign(ins)
                    link.wait()
                    ins.then_inc(xn_ready, 1)

            norm(0)
            dve.wait_ge(table, 5)
            for g in range(G):
                o = (g % 2) * GW
                if g == 2:
                    dve.wait_ge(parts_saved, 16 * 16)
                for w, src, f in ((0, 0, 0), (1, 0, 1), (2, 1, 0)):
                    dve.wait_ge((q_ready, k_ready)[src], g + 1)
                    link(dve.tensor_tensor(folded[:, w, :], qk_f[:, src, :], fold[:, f, o:o + GW], ALU.mult))
                    for i in range(3):
                        ins = dve.tensor_copy(parts[:, w, i, o:o + GW], folded[:, w, :])
                        if i < 2:
                            link(ins)
                            link(dve.tensor_tensor(folded[:, w, :], folded[:, w, :], parts[:, w, i, o:o + GW], ALU.subtract))
                    if w < 2:
                        link.sign(ins)
                ins.then_inc(parts_ready, 1)
                for w in range(2):
                    dve.wait_ge(sq_psum, 2 * g + w + 1)
                    dve.tensor_reduce(sq_max[:, w * G + g:w * G + g + 1], bank(7 * w)[0:H, :], AX.X, ALU.max).then_inc(sq_taken, 1)
            dve.wait_ge(sq_taken, 2 * G)
            link(dve.tensor_reduce(bound[0:H, 2:4], sq_max[:].rearrange("p (w g) -> p w g", w=2), AX.X, ALU.max))
            dve.tensor_tensor(bound[0:H, 4:5], bound[0:H, 2:3], bound[0:H, 3:4], ALU.mult).then_inc(bound_part, 1)
            dve.wait_ge(bound_psum, 2)
            link(dve.tensor_reduce(bound[0:1, 5:6], bank(6)[0:1, 0:2 * G], AX.X, ALU.add))
            link(dve.tensor_reduce(bound[0:1, 6:7], bank(5)[0:1, 0:H], AX.X, ALU.max))
            dve.scalar_tensor_tensor(bound[0:1, 0:1], bound[0:1, 5:6], 0.0, bound[0:1, 6:7], ALU.mult, ALU.add).then_inc(bound_sq, 1)
            dve.wait_ge(bound_psum, 3)
            link(dve.tensor_scalar(minus_bound[:], bank(4)[:, 0:1], -1.0, None, ALU.mult))
            diagonal = slice(S - P, S)
            link(dve.reciprocal(corner[:], unfold[:, diagonal]))
            link(dve.memset(bank(5), 1.0))
            link(dve.tensor_tensor(corner[:], decay[:, diagonal], corner[:], ALU.mult))
            dve.tensor_scalar(flag[:], bound[0:1, 1:2], BOUND, None, ALU.is_le).then_inc(flag_ready, 1)

            dve.wait_ge(flag_ready, 1)
            fast = dve.value_load(flag[0:1, 0:1], min_val=0, max_val=1)
            with dve.If(fast == 1):
                flink = Link(dve, fast_link)
                dve.sem_inc(corner_done, CREDIT)
                dve.sem_inc(evac_ready, CREDIT)
                dve.sem_inc(head_ready, CREDIT)

                def diagonal_tile(i, c):
                    n, k = i * (2 * QT) + c, c % QT
                    ready(dve, first_half, n)
                    tile = wide[c % 2][:, k * P:(k + 1) * P]
                    dve.tensor_tensor(tile, tile, corner[:], ALU.mult).then_inc(corner_done, 1)

                def evacuate(i, c):
                    u = c // QT
                    n = i * 2 + u
                    dve.wait_ge(pv_done, i * (2 * QT) + (c + RING))
                    free(dve, evacT_psum, n)
                    dve.tensor_copy(evac[1 - u][:], bank(4 + 1 - u)).then_inc(evac_ready, 1)

                def finish(n, u):
                    ready(dve, evacT_psum, n)
                    t = bank(6 + u).rearrange("p (t g d) -> p t g d", t=4, g=4)
                    flink(dve.tensor_copy(o_sum[u][:], t[:, :, 0:2, 0:HD + 1]))
                    flink(dve.tensor_tensor(o_sum[u][:], o_sum[u][:], t[:, :, 2:4, 0:HD + 1], ALU.add))
                    flink(dve.reciprocal(o_inv[:, u, :].rearrange("p (t h) -> p t h", t=4), o_sum[u][:, :, :, HD]))
                    for h in range(2):
                        inv = o_inv[:, u, h:QT:2]
                        ins = dve.tensor_tensor(o_heads[:, h * 4:(h + 1) * 4, :, :].rearrange("p t n d -> p t (n d)")[:, :, bass.ds(n * HD, HD)],
                                                o_sum[u][:, :, h, 0:HD],
                                                bass.AP(inv.tensor, inv.offset, [list(inv.ap[0]), list(inv.ap[1]), [0, HD]]), ALU.mult)
                        if h == 0:
                            flink.sign(ins)
                    flink.wait()
                    ins.then_inc(head_ready, 1)

                def body(i, last):
                    for c in range(2 * QT):
                        if not last or c + 2 < 2 * QT:
                            diagonal_tile(i, c + 2)
                        if c % QT == 0:
                            evacuate(i, c)
                        if c % QT == 2:
                            finish(i * 2 + c // QT, c // QT)

                diagonal_tile(0, 0)
                diagonal_tile(0, 1)
                with dve.Fori(0, NH // 2 - 1) as i:
                    flink.turn = i * 8
                    body(i, False)
                assert flink.n == 8
                flink.end_loop(NH // 2 - 1, 8)
                body(NH // 2 - 1, True)
                evacuate(NH // 2, 0)
                finish(NH, 0)
                ready(dve, head_ready, NH)
                dve.sem_inc(o_all, 1)
            with dve.Else():
                slink = Link(dve, slow_link)
                dve.sem_inc(s_clamped, CREDIT)
                dve.sem_inc(max_ready, CREDIT)
                dve.sem_inc(o_ready, CREDIT)
                with dve.Fori(0, NH // 2) as i:
                    per_turn = 2 * QT * 4
                    slink.turn = i * per_turn
                    for c in range(2 * QT + 2):
                        if c < 2 * QT:
                            n, q = i * (2 * QT) + c, c % QT
                            at = S - P - q * P
                            ready(dve, s_psum, n)
                            free(dve, exp_ready, n)
                            dve.tensor_tensor(sc[c % 2], wide[c % 2][:], unfold[:, at:at + S], ALU.mult).then_inc(s_clamped, 1)
                            ready(dve, s_clamped, n)
                            slink(dve.tensor_scalar(sc[c % 2], sc[c % 2], -CLAMP, CLAMP, ALU.max, ALU.min))
                            slink(dve.tensor_tensor(sc[c % 2], sc[c % 2], decay[:, at:at + S], ALU.mult))
                            slink(dve.tensor_reduce(row[:, c % 2, 0:1], sc[c % 2], AX.X, ALU.max))
                            dve.tensor_scalar(row[:, c % 2, 1:2], row[:, c % 2, 0:1], -1.0, None, ALU.mult).then_inc(max_ready, 1)
                        if c >= 2:
                            n, u, q = i * (2 * QT) + (c - 2), (c - 2) // QT, (c - 2) % QT
                            ready(dve, exp_ready, n)
                            slink(dve.reciprocal(row[:, c % 2, 3:4], row[:, c % 2, 2:3]))
                            ready(dve, o_psum, n)
                            dve.tensor_scalar(o_heads[:, q, :, :].rearrange("p n d -> p (n d)")[:, bass.ds((i * 2 + (u + 1)) * HD, HD)], bank(6 + c % 2)[:, 0:HD],
                                              row[:, c % 2, 3:4], None, ALU.mult).then_inc(o_ready, 1)
                    assert slink.n == per_turn
                ready(dve, o_ready, NH * QT - 1)
                dve.sem_inc(o_all, 1)
            for g in range(G):
                ts = slice(g * TPG, (g + 1) * TPG)
                dve.wait_ge(y_psum, g + 1)
                dve.tensor_tensor(x[:, ts, :], x[:, ts, :], bank(2 + g % 2).rearrange("p (t d) -> p t d", t=TPG), ALU.add)\
                    .then_inc(x_ready, 1)

            norm(1)
            dve.wait_ge(w1_loaded, 4 * 16)
            for t in range(NT):
                dve.wait_ge(logit_psum, t + 1)
                dve.tensor_tensor(gates[:, t, :], bank(6 + t % 2)[:, 0:NE], b_router[:], ALU.add).then_inc(logit_ready, 1)
            for g in range(G):
                tiles = range(g * TPG, (g + 1) * TPG)
                ts = slice(g * TPG, (g + 1) * TPG)
                dve.wait_ge(gate_ready, (g + 1) * TPG)
                for t in tiles:
                    link.sign(dve.max(top[:, t, :], gates[:, t, :]))
                link.wait()
                if g:
                    dve.wait_ge(cT_psum, g)
                for t in tiles:
                    link.sign(dve.match_replace(rest[:, t % TPG, :], top[:, t, :], gates[:, t, :], -1.0))
                link(dve.tensor_reduce(top_sum[:, ts], top[:, ts, :], AX.X, ALU.add))
                link(dve.tensor_scalar(top_sum[:, ts], top_sum[:, ts], 1e-9, None, ALU.add))
                link(dve.reciprocal(top_inv[:, ts], top_sum[:, ts]))
                for t in tiles:
                    link.sign(dve.scalar_tensor_tensor(rest[:, t % TPG, :], rest[:, t % TPG, :], 0.0, gates[:, t, :],
                                                       ALU.max, ALU.subtract))
                link.wait()
                for t in tiles:
                    ins = dve.tensor_scalar(rest[:, t % TPG, :], rest[:, t % TPG, :], top_inv[:, t:t + 1], -ROUTED,
                                            ALU.mult, ALU.mult)
                    if t < tiles[-1]:
                        link.sign(ins)
                link.wait()
                ins.then_inc(combine_ready, 1)
            for g in range(G):
                v = cT[:, 0, g * GW:(g + 1) * GW]
                dve.wait_ge(cT_ready, 2 * g + 1)
                if g:
                    dve.wait_ge(c_saved, 32 * g)
                link(dve.tensor_copy(c_part[:, 0, 0, :], v))
                link(dve.tensor_tensor(v, v, c_part[:, 0, 0, :], ALU.subtract))
                link(dve.tensor_copy(c_part[:, 0, 1, :], v))
                link(dve.tensor_tensor(v, v, c_part[:, 0, 1, :], ALU.subtract))
                dve.tensor_copy(c_part[:, 0, 2, :], v).then_inc(c_split, 1)
            dve.sem_inc(hid_ready, CREDIT)
            with dve.Fori(0, MT_N // 2) as i:
                for c in range(2 * G):
                    n = i * (2 * G) + c
                    ready(dve, silu_ready, n)
                    ready(dve, cb_psum, n)
                    dve.wait_ge(down_done, n + CREDIT)
                    dve.tensor_tensor(hid[c % 2], act_out[c % 2], bank(6 + c % 2), ALU.mult).then_inc(hid_ready, 1)
            for g in range(G):
                ts = slice(g * TPG, (g + 1) * TPG)
                dve.wait_ge(acc_psum, g + 1)
                dve.tensor_tensor(x[:, ts, :], x[:, ts, :], bank(4 + g).rearrange("p (t d) -> p t d", t=TPG), ALU.add)\
                    .then_inc(x_ready, 1)

            norm(2)
            C2 = B * NCH
            dve.wait_ge(xn_ready, 3 * G)
            link(dve.tensor_tensor(squares, xn[:, :, :].rearrange("p t d -> p (t d)"), xn[:, :, :].rearrange("p t d -> p (t d)"),
                                   ALU.mult))
            dve.tensor_reduce(inv_norm[:], squares.rearrange("p (t d) -> p t d", t=NT), AX.X, ALU.add).then_inc(sq_ready, 1)
            dve.wait_ge(xnT_ready, 3 * G)
            link(dve.tensor_reduce(x_mean[:], xnT[:, :].rearrange("p (c t) -> p c t", t=CH), AX.X, ALU.add))
            dve.wait_ge(root_ready, 1)
            link(dve.tensor_scalar(inv_norm[:], inv_norm[:], NORM_EPS, float(CH), ALU.max, ALU.mult))
            link(dve.reciprocal(inv_norm[:], inv_norm[:]))
            link(dve.tensor_copy(by_half[0:CH, :, 0], inv_norm[0:CH, :]))
            dve.tensor_copy(by_half[CH:P, :, 1], inv_norm[CH:P, :]).then_inc(by_half_ready, 1)
            dve.wait_ge(km_psum, 1)
            dve.tensor_copy(k_mean[:], bank(4)[:, 0:C2]).then_inc(km_ready, 1)
            dve.wait_ge(km_ready, 1)
            by_step = [steps[:, :, :, k].rearrange("p n b -> p b n") for k in range(3)]
            by_batch = lambda ap: ap.rearrange("p (b n) -> p b n", b=B)
            link(dve.scalar_tensor_tensor(by_step[2], by_batch(x_mean[:]), 1.0 / CH, by_batch(k_mean[:]), ALU.mult, ALU.subtract))
            dve.wait_ge(tok_ready, 2 * G)
            rows = [one_row[:, k * C2:(k + 1) * C2] for k in range(6)]
            link(dve.tensor_reduce(one_row[:, C2:3 * C2], tok.rearrange("p (c t) -> p c t", t=CH), AX.X, ALU.add))
            link(dve.tensor_scalar(rows[3], rows[2], -(1.0 - MIN_DECAY) / CH, 1.0 - MIN_DECAY, ALU.mult, ALU.add))
            dve.wait_ge(gate_row, 1)
            link(dve.tensor_tensor(rows[3], rows[3], rows[0], ALU.mult))
            link(dve.tensor_scalar(rows[4], rows[3], -1.0, 1.0, ALU.mult, ALU.add))
            dve.scalar_tensor_tensor(rows[5], rows[1], MAX_LR / CH, rows[0], ALU.mult, ALU.mult).then_inc(scalars_ready, 1)
            dve.wait_ge(scalars_psum, 1)
            link(dve.tensor_copy(by_step[0], by_batch(bank(6)[:, 0:C2])))
            dve.tensor_tensor(by_step[1], by_batch(k_mean[:]), by_batch(bank(6)[:, C2:2 * C2]), ALU.mult).then_inc(steps_ready, 1)
            for b in range(B):
                dve.sem_inc(state_ready[b], CREDIT)
            dve.sem_inc(rows_ready, CREDIT)
            dve.sem_inc(norm_sq, CREDIT)
            dve.wait_ge(fold_ready, 1 + B)
            first, per_turn = link.n, 2 * (2 * B + 1 + 3)
            with dve.Fori(0, NCH // 2) as i:
                link.turn = i * per_turn
                for u in range(2):
                    n = i * 2 + u
                    ready(dve, step_ready, n)
                    for b in range(B):
                        free(dve, state_ready[b], n, 1)
                        link.sign(dve.tensor_scalar(kept[b][:], state[b][:], step[u][:, 3 * b:3 * b + 1], None, ALU.mult))
                    link.wait()
                    for b in range(B):
                        ready(dve, err_psum[b], n)
                        link(dve.scalar_tensor_tensor(state[b][:], bank(2 + b)[:, 0:2 * D], step[u][:, 3 * b + 1:3 * b + 2],
                                                      kept[b][:], ALU.mult, ALU.add))
                        ins = dve.tensor_tensor_reduce(m_sq[:, b, :], state[b][:, 0:D], state[b][:, 0:D], 1.0, 0.0,
                                                       ALU.mult, ALU.add, m_norm[:, 0, b:b + 1])
                        if b == 0:
                            link.sign(ins)
                    ins.then_inc(rows_ready, 1)
                    ready(dve, norm_psum, n)
                    dve.tensor_copy(m_norm[:, 1, :], bank(6)[:, 0:B]).then_inc(norm_sq, 1)
                    ready(dve, norm_ready, n)
                    link(dve.tensor_scalar(m_norm[:, 3, :], m_norm[:, 2, :], 1e-6, None, ALU.add))
                    link(dve.reciprocal(m_norm[:, 3, :], m_norm[:, 3, :]))
                    link(dve.tensor_scalar(m_norm[:, 3, :], m_norm[:, 3, :], MAX_NORM, 1.0, ALU.mult, ALU.min))
                    for b in range(B):
                        dve.tensor_scalar(state[b][:], state[b][:], m_norm[:, 3, b:b + 1], None, ALU.mult)\
                            .then_inc(state_ready[b], 1)
                assert link.n - first == per_turn, (link.n - first, per_turn)
            link.end_loop(NCH // 2, per_turn)
            for g in range(G):
                ts = slice(g * TPG, (g + 1) * TPG)
                dve.wait_ge(mem_psum, g + 1)
                dve.tensor_tensor(x[:, ts, :], x[:, ts, :], bank(g).rearrange("p (t d) -> p t d", t=TPG), ALU.add)\
                    .then_inc(x_ready, 1)

            norm(3)

            def by_row(ap, n):
                return bass.AP(ap.tensor, ap.offset, [list(ap.ap[0]), list(ap.ap[1]), [0, n]])

            logits = bank(4)[:, 0:NT * NE2].rearrange("p (t e) -> p t e", t=NT)
            dve.wait_ge(logit2_psum, 1)
            link(dve.tensor_reduce(r_max[:], logits, AX.X, ALU.max))
            dve.tensor_tensor(soft[:], logits, by_row(r_max[:], NE2), ALU.subtract).then_inc(shifted, 1)
            dve.wait_ge(exp2_ready, 1)
            link(dve.tensor_reduce(r_sum[:], soft[:], AX.X, ALU.add))
            link(dve.reciprocal(r_sum[:], r_sum[:]))
            link(dve.tensor_tensor(soft[:], soft[:], by_row(r_sum[:], NE2), ALU.mult))
            dve.wait_ge(ffn_zero, 1)
            pairs = soft[:].rearrange("p t (g k) -> p t g k", k=2)
            link(dve.tensor_reduce(padded[:, 0, :, 0:4], pairs, AX.X, ALU.max))

            def mark_two(k):
                for t in range(NT):
                    link.sign(dve.max(best[:, k, t, :], padded[:, k, t, :]))
                link.wait()
                link(dve.tensor_copy(taken[:, k, :, 0:2], best[:, k, :, 0:2]))
                for t in range(NT):
                    link.sign(dve.match_replace(marked[:, k, t, :], taken[:, k, t, :], padded[:, k, t, :], -2.0))
                link.wait()

            mark_two(0)
            link(dve.tensor_scalar(marked[:, 0, :, :], marked[:, 0, :, :], -2.0, None, ALU.is_equal))
            for k in range(2):
                link.sign(dve.tensor_tensor(padded[:, 1, :, k:8:2], soft[:, :, k:8:2], marked[:, 0, :, 0:4], ALU.mult))
            link.wait()
            mark_two(1)
            link(dve.tensor_scalar(marked[:, 1, :, :], marked[:, 1, :, :], -2.0, None, ALU.is_equal))
            link(dve.tensor_tensor(combine2[:], padded[:, 1, :, 0:8], marked[:, 1, :, 0:8], ALU.mult))
            link(dve.tensor_reduce(r_sum[:], best[:, 1, :, 0:2], AX.X, ALU.add))
            link(dve.reciprocal(r_sum[:], r_sum[:]))
            dve.tensor_tensor(combine2[:], combine2[:], by_row(r_sum[:], NE2), ALU.mult).then_inc(combine2_ready, 1)
            for g in range(G):
                v = c2T[:, g * GW:(g + 1) * GW]
                left = c_part[0:NE2, 0]
                dve.wait_ge(c2T_ready, g + 1)
                if g:
                    dve.wait_ge(c2_saved, 16 * g)
                link(dve.tensor_copy(left[:, 0, :], v))
                link(dve.tensor_tensor(v, v, left[:, 0, :], ALU.subtract))
                link(dve.tensor_copy(left[:, 1, :], v))
                link(dve.tensor_tensor(v, v, left[:, 1, :], ALU.subtract))
                dve.tensor_copy(left[:, 2, :], v).then_inc(c2_split, 1)
            dve.sem_inc(gated_ready, CREDIT)
            dve.sem_inc(hid2_ready, CREDIT)
            with dve.Fori(0, NE2) as i:
                for c in range(2 * G):
                    n = i * (2 * G) + c
                    ready(dve, silu2_ready, n)
                    ready(dve, up_z, n)
                    free(dve, hid2_ready, n)
                    dve.tensor_tensor(gated[c % 2], act_out[c % 2], bank(5), ALU.mult).then_inc(gated_ready, 1)
                    ready(dve, gated_ready, n)
                    ready(dve, c2_psum, n)
                    dve.wait_ge(down2_done, n + CREDIT)
                    dve.tensor_tensor(hid[c % 2], gated[c % 2], bank(6), ALU.mult).then_inc(hid2_ready, 1)
            for g in range(G):
                ts = slice(g * TPG, (g + 1) * TPG)
                dve.wait_ge(acc2_psum, g + 1)
                dve.tensor_tensor(x[:, ts, :], x[:, ts, :], bank(4 + g).rearrange("p (t d) -> p t d", t=TPG), ALU.add)\
                    .then_inc(x_ready, 1)


def kernel(**inputs):
    import concourse.bacc as bacc
    from concourse.bass_utils import run_bass_kernel_spmd as run

    w = {k: np.asarray(v) for k, v in inputs.items()}
    arrays = {
        "x": w["L0_attn_x"], "wq": w["L0_attn_Wq"], "wk": w["L0_attn_Wk"], "wv": w["L0_attn_Wv"], "wo": w["L0_attn_Wo"],
        "w_down": w["L0_attn_W_down_kv"], "w_up_k": w["L0_attn_W_up_k"], "w_up_v": w["L0_attn_W_up_v"],
        "w_router": w["L0_ffn_router_w"].T, "b_router": w["L0_ffn_expert_bias"],
        "w_shared": w["L0_ffn_w_gate_shared"].T, "wd_shared": w["L0_ffn_w_down_shared"].T,
        "w_exp": np.concatenate([w["L0_ffn_w_gate"].reshape(MT_N, P, D).transpose(0, 2, 1),
                                 w["L0_ffn_w_down"].transpose(0, 2, 1).reshape(MT_N, P, D)], axis=2),
        "w_tok": np.stack([w["L1_attn_eta_w"], w["L1_attn_alpha_w"], w["L1_attn_gate_w"]], axis=1),
        "b_tok": np.stack([w["L1_attn_eta_b"], w["L1_attn_alpha_b"], w["L1_attn_gate_b"]], axis=1),
        "m0": w["L1_attn_M_init"], "m0T": w["L1_attn_M_init"].T, "vg1T": w["L1_attn_vg_w1"].T,
        "vg2": w["L1_attn_vg_w2"], "vg2T": w["L1_attn_vg_w2"].T,
        "w_gate2": w["L1_ffn_gate_w"].T,
        "w_ffn": np.concatenate([w["L1_ffn_w13_weight"].reshape(NE2, 2, FI2 // P, P, D)[:, 0].reshape(FT_N, P, D).transpose(0, 2, 1),
                                 w["L1_ffn_w13_weight"].reshape(NE2, 2, FI2 // P, P, D)[:, 1].reshape(FT_N, P, D).transpose(0, 2, 1),
                                 w["L1_ffn_w2_weight"].transpose(0, 2, 1).reshape(FT_N, P, D)], axis=2),
    }
    arrays = {"in_" + k: np.ascontiguousarray(v) for k, v in arrays.items()}
    nc = bacc.Bacc("TRN2", target_bir_lowering=False, num_devices=1)
    a = {k[3:]: nc.dram_tensor(k, v.shape, mybir.dt.from_np(v.dtype), kind="ExternalInput").ap() for k, v in arrays.items()}
    out = nc.dram_tensor("out", (B, S, D), F32, kind="ExternalOutput").ap()
    build(nc, a, out)
    return run(nc, [arrays], core_ids=[0]).results[0]["out"]
```

```python
from contextlib import ExitStack

import concourse.bass as bass
import numpy as np
from concourse import mybir

F32 = mybir.dt.float32
BF16 = mybir.dt.bfloat16
F32R = mybir.dt.float32r
I32 = mybir.dt.int32
ALU = mybir.AluOpType
ACT = mybir.ActivationFunctionType
AX = mybir.AxisListType

P = 128
B, S, D = 2, 1024, 128
T = B * S
NT = T // P
G = 4
GW = T // G
TPG = NT // G
H, HD = 16, 8
NH = B * H
QT = S // P
LAT = 32
PAIRS = 9
CLAMP = 10000.0
DECAY = 0.01 * 0.01
SCALE = 1.0 / (float(np.sqrt(np.float32(D))) + 1e-8)
EPS = 1e-5
NE, EI, TOPK = 160, 64, 8
MT_N = NE * EI // P
ROUTED = 2.5
NCHUNK = 4
CE = NE // NCHUNK
PAIRS_C = CE // 2
CH = 64
NCH = S // CH
MAX_LR, MIN_DECAY, MAX_NORM, NORM_EPS = 0.2, 0.5, 30.0, 1e-5
NE2, FI2 = 8, 256
FT_N = NE2 * FI2 // P
RING = 8
BOUND = 40.0
TW = 2 * S - P
CREDIT = 2


class Link:

    def __init__(self, eng, sem):
        self.eng, self.sem, self.n, self.turn = eng, sem, 0, 0

    def sign(self, ins):
        ins.then_inc(self.sem, 1)
        self.n += 1
        return ins

    def wait(self):
        self.eng.wait_ge(self.sem, self.n + self.turn)

    def __call__(self, ins):
        self.sign(ins)
        self.wait()
        return ins

    def end_loop(self, turns, per_turn):
        self.n, self.turn = self.n + (turns - 1) * per_turn, 0


def build(nc, a, out):
    with ExitStack() as ctx:
        def sb(name, shape, dt=F32):
            return ctx.enter_context(nc.sbuf_tensor(name, shape, dt))

        def sem(name):
            return ctx.enter_context(nc.semaphore(name))

        def dram(name, shape, dt):
            return nc.dram_tensor(name, shape, dt, kind="Internal").ap()

        bank01 = ctx.enter_context(nc.psum_tensor("bank01", [P, 1024], F32))
        bank23 = ctx.enter_context(nc.psum_tensor("bank23", [P, 1024], F32))
        bank45 = ctx.enter_context(nc.psum_tensor("bank45", [P, 1024], F32))
        bank67 = ctx.enter_context(nc.psum_tensor("bank67", [P, 1024], F32))
        wide = [bank01, bank23, bank45, bank67]

        def bank(n):
            return wide[n // 2][:, (n % 2) * 512:(n % 2) * 512 + 512]

        x = sb("x", [P, NT, D])
        xn = sb("xn", [P, NT, D])
        xnT = sb("xnT", [P, T])
        stats = sb("stats", [P, NT, 6])
        mv = sb("mv", [P, NT, 2])
        rstd = sb("rstd", [P, NT])
        ident = sb("ident", [P, P])
        half = sb("half", [P, NT])
        wq = sb("wq", [P, D])
        wk = sb("wk", [P, D])
        wv = sb("wv", [P, D])
        wo = sb("wo", [P, D])
        w_down = sb("w_down", [P, LAT])
        w_up = sb("w_up", [LAT, 2 * D])
        big = sb("big", [P, 4 * T])
        kvT = big[:, 0:512]
        latT = big[0:LAT, 512:1024]
        qk_f = [big[:, 1024 + u * 1024:2048 + u * 1024].rearrange("p (w t) -> p w t", w=2) for u in range(2)]
        distance = big[:, 5120:5120 + TW].bitcast(I32)
        time = big[:, 7104:7104 + S].bitcast(I32)
        v_heads = sb("v_heads", [P, NH, QT, HD])
        v_flat = v_heads[:, :, :, :].rearrange("p n t d -> p (n t d)")
        o_heads = sb("o_heads", [P, QT, NH + 1, HD])
        q_stack = [[sb(f"q_stack{s}{u}", [P, S], BF16) for u in range(2)] for s in range(2)]
        k_stack = [[sb(f"k_stack{s}{u}", [P, S], BF16) for u in range(2)] for s in range(2)]
        v_cur = [sb(f"v_cur{u}", [P, QT, 32]) for u in range(2)]
        ring = sb("ring", [P, RING * S])
        parts = [t.bitcast(BF16).rearrange("p (s i t) -> p s i t", s=4, i=3) for t in (ring[:, 0:3 * S], big[:, 5 * S:8 * S])]
        qk_sq = ring[:, 3 * S:4 * S].rearrange("p (w t) -> p w t", w=2)
        folded = ring[:, 4 * S:6 * S].rearrange("p (s t) -> p s t", s=4)
        fold = sb("fold", [P, 2, S])
        decay = sb("decay", [P, TW])
        unfold = sb("unfold", [P, TW])
        corner = sb("corner", [P, P])
        head_ones = sb("head_ones", [P, H])
        qk_sums = sb("qk_sums", [P, 2 * G])
        sq_max = sb("sq_max", [H, 2 * G])
        bound = sb("bound", [P, 8])
        flag = sb("flag", [1, 1], I32)
        minus_bound = sb("minus_bound", [P, 1])
        evac = [sb(f"evac{u}", [P, GW]) for u in range(2)]
        o_sum = [sb(f"o_sum{u}", [P, QT // 2, 2, HD + 1]) for u in range(2)]
        o_inv = sb("o_inv", [P, 2, QT])
        sc = [ring[:, u * S:(u + 1) * S] for u in range(2)]
        pr = [ring[:, (2 + u) * S:(3 + u) * S] for u in range(2)]
        prT = [ring[:, (4 + u) * S:(5 + u) * S] for u in range(2)]
        row = sb("row", [P, 2, 4])
        oT = big[:, 0:T]

        w_router = sb("w_router", [P, NE])
        b_router = sb("b_router", [P, NE])
        w_shared = sb("w_shared", [P, EI])
        wd_shared = sb("wd_shared", [EI, D])
        gates = big[:, 2 * T:2 * T + NT * NE].rearrange("p (t e) -> p t e", t=NT)
        rest = [ring[:, (5 + u) * S:(5 + u) * S + TPG * NE].rearrange("p (t e) -> p t e", t=TPG) for u in range(2)]
        top = sb("top", [P, NT, 8])
        top_sum = sb("top_sum", [P, NT])
        top_inv = sb("top_inv", [P, NT])
        c_tok = [ring[:, at:at + TPG * 3 * NE // 2].bitcast(BF16).rearrange("p (t e) -> p t e", t=TPG) for at in (4 * S, 7 * S)]
        c_tok_parts = [t.rearrange("p t (e i) -> p t e i", i=3) for t in c_tok]
        c_rows = ring[:, 0:4 * S].bitcast(BF16)
        spread = sb("spread", [P, PAIRS_C * P], BF16)
        ident_b = sb("ident_b", [P, P], BF16)
        xh = sb("xh", [P, T], F32R)
        xl = sb("xl", [P, T], F32R)
        w_raw = [sb(f"w_raw{u}", [P, 3 * D]) for u in range(2)]
        wh = [sb(f"wh{u}", [P, 3 * D], F32R) for u in range(2)]
        wl = [sb(f"wl{u}", [P, 3 * D], F32R) for u in range(2)]
        act_out = [q_stack[0][u][:].bitcast(F32) for u in range(2)]
        hid = [q_stack[1][u][:].bitcast(F32) for u in range(2)]
        hh = [sb(f"hh{u}", [P, GW], F32R) for u in range(2)]
        hl = [sb(f"hl{u}", [P, GW], F32R) for u in range(2)]
        accT = big[:, 0:T]

        w_tok = sb("w_tok", [P, 3])
        b_tok = sb("b_tok", [P, 3])
        m0 = sb("m0", [P, D])
        vg1T = sb("vg1T", [P, D])
        vg2 = sb("vg2", [P, D])
        vg2T = sb("vg2T", [P, D])
        ones = sb("ones", [P, P])
        root = sb("root", [P, NT])
        state = [sb(f"state{b}", [P, 2 * D]) for b in range(B)]
        kept = [ring[:, 7 * S + b * 2 * D:7 * S + (b + 1) * 2 * D] for b in range(B)]
        vg2_cat = sb("vg2_cat", [P, 2 * D])
        tok = sb("tok", [P, NT, 2])
        squares = big[:, 2 * T:3 * T]
        inv_norm = sb("inv_norm", [P, NT])
        by_half = sb("by_half", [P, NT, 2])
        x_mean = sb("x_mean", [P, B * NCH])
        k_mean = sb("k_mean", [P, B * NCH])
        by_chunk = sb("by_chunk", [P, 4, B * NCH])
        first_half_ones = sb("first_half_ones", [P, P])
        steps = sb("steps", [P, NCH, B, 3])
        steps_flat = steps[:, :, :, :].rearrange("p n b c -> p (n b c)")
        step = [sb(f"step{u}", [P, B * 3]) for u in range(2)]
        silu_z = [sb(f"silu_z{b}", [P, CH]) for b in range(B)]
        h_sum = [sb(f"h_sum{b}", [P, 1]) for b in range(B)]
        m_sq = sb("m_sq", [P, B, D])
        m_norm = sb("m_norm", [P, 4, B])
        out_sum = [sb(f"out_sum{b}", [P, CH]) for b in range(B)]
        memT = big[:, 3 * T:4 * T]

        def across(ap, n):
            return bass.AP(ap.tensor, ap.offset, [list(ap.ap[0]), [0, n]])

        w_gate2 = sb("w_gate2", [P, NE2])
        r_max = sb("r_max", [P, NT])
        r_sum = sb("r_sum", [P, NT])
        soft = sb("soft", [P, NT, NE2])

        def choice(at, width):
            start = 4 * S + 2 * NT * at
            return ring[:, start:start + 2 * NT * width].rearrange("p (k t e) -> p k t e", k=2, t=NT)

        padded = choice(0, 16)
        best = choice(16, 8)
        taken = choice(24, 8)
        marked = choice(32, 16)
        combine2 = sb("combine2", [P, NT, NE2])
        c2_tok = ring[:, 7 * S + 512:7 * S + 512 + NT * 3 * NE2 // 2].bitcast(BF16).rearrange("p (t e) -> p t e", t=NT)
        c2_tok_parts = c2_tok[:, :, :].rearrange("p t (e i) -> p t e i", i=3)
        c2_rows = c_rows[:, 0:T]
        spread2 = fold[:, 0, 0:NE2 * P // 2].bitcast(BF16)
        gated = [evac[u][:] for u in range(2)]

        q_dram = [dram(f"q_parts{s}", [NH, 5, HD, S], BF16) for s in range(2)]
        k_dram = [dram(f"k_parts{s}", [NH, 3, HD, S], BF16) for s in range(2)]

        x_loaded = sem("x_loaded")
        w_loaded = sem("w_loaded")
        consts = sem("consts")
        table = sem("table")
        dve_link = sem("dve_link")
        act_link = sem("act_link")
        pool_link = sem("pool_link")
        var_ready = sem("var_ready")
        rstd_ready = sem("rstd_ready")
        xn_ready = sem("xn_ready")
        xnT_psum = sem("xnT_psum")
        xnT_ready = sem("xnT_ready")
        stored = sem("stored")
        q_psum = sem("q_psum")
        kv_psum = sem("kv_psum")
        kv_ready = sem("kv_ready")
        lat_psum = sem("lat_psum")
        lat_ready = sem("lat_ready")
        k_psum = sem("k_psum")
        v_psum = sem("v_psum")
        q_ready = sem("q_ready")
        k_ready = sem("k_ready")
        v_ready = sem("v_ready")
        parts_ready = sem("parts_ready")
        parts_saved = [sem(f"parts_saved{u}") for u in range(2)]
        stacks_zero = sem("stacks_zero")
        stacks_loaded = [sem(f"stacks_loaded{u}") for u in range(2)]
        sq_psum = sem("sq_psum")
        qk_sq_ready = sem("qk_sq_ready")
        sq_taken = sem("sq_taken")
        folded_ready = sem("folded_ready")
        part_cast = sem("part_cast")
        bound_psum = sem("bound_psum")
        bound_part = sem("bound_part")
        bound_sq = sem("bound_sq")
        bound_root = sem("bound_root")
        flag_ready = sem("flag_ready")
        first_half = sem("first_half")
        whole = sem("whole")
        corner_done = sem("corner_done")
        exp_done = sem("exp_done")
        pv_done = sem("pv_done")
        v_loaded = sem("v_loaded")
        evac_ready = sem("evac_ready")
        evacT_psum = sem("evacT_psum")
        head_ready = sem("head_ready")
        fast_link = sem("fast_link")
        slow_link = sem("slow_link")
        s_psum = sem("s_psum")
        s_clamped = sem("s_clamped")
        max_ready = sem("max_ready")
        exp_ready = sem("exp_ready")
        prT_psum = sem("prT_psum")
        prT_ready = sem("prT_ready")
        o_psum = sem("o_psum")
        o_ready = sem("o_ready")
        o_all = sem("o_all")
        oT_psum = sem("oT_psum")
        oT_ready = sem("oT_ready")
        y_psum = sem("y_psum")
        x_ready = sem("x_ready")
        w3_loaded = sem("w3_loaded")
        logit2_psum = sem("logit2_psum")
        shifted = sem("shifted")
        exp2_ready = sem("exp2_ready")
        c2_split = sem("c2_split")
        c2T_psum = sem("c2T_psum")
        c2T_ready = sem("c2T_ready")
        w2_split = sem("w2_split")
        hh2_ready = sem("hh2_ready")
        hl2_ready = sem("hl2_ready")
        ffn_zero = sem("ffn_zero")
        ffn_loaded = [sem(f"ffn_loaded{u}") for u in range(2)]
        gate_z = sem("gate_z")
        up_z = sem("up_z")
        c2_psum = sem("c2_psum")
        silu2_ready = sem("silu2_ready")
        gated_ready = sem("gated_ready")
        hid2_ready = sem("hid2_ready")
        down2_done = sem("down2_done")
        low2_used = sem("low2_used")
        acc2_done = sem("acc2_done")
        accT2_ready = sem("accT2_ready")
        acc2_psum = sem("acc2_psum")
        w2_loaded = sem("w2_loaded")
        tok_psum = sem("tok_psum")
        tok_ready = sem("tok_ready")
        sq_ready = sem("sq_ready")
        squares_ready = sem("squares_ready")
        root_ready = sem("root_ready")
        by_half_ready = sem("by_half_ready")
        km_psum = sem("km_psum")
        km_ready = sem("km_ready")
        gate_psum = sem("gate_psum")
        gate_row = sem("gate_row")
        steps_ready = sem("steps_ready")
        fold_psum = sem("fold_psum")
        fold_ready = sem("fold_ready")
        step_ready = sem("step_ready")
        state_ready = [sem(f"state_ready{b}") for b in range(B)]
        mz_psum = [sem(f"mz_psum{b}") for b in range(B)]
        mz_silu = [sem(f"mz_silu{b}") for b in range(B)]
        err_psum = [sem(f"err_psum{b}") for b in range(B)]
        old_psum = [sem(f"old_psum{b}") for b in range(B)]
        scale_ready = sem("scale_ready")
        out_copied = [sem(f"out_copied{b}") for b in range(B)]
        tok_sums = sem("tok_sums")
        out_psum = [sem(f"out_psum{b}") for b in range(B)]
        out_taken = [sem(f"out_taken{b}") for b in range(B)]
        rows_ready = sem("rows_ready")
        norm_psum = sem("norm_psum")
        norm_sq = sem("norm_sq")
        norm_ready = sem("norm_ready")
        mem_psum = sem("mem_psum")
        w1_loaded = sem("w1_loaded")
        shared_psum = sem("shared_psum")
        shared_act = sem("shared_act")
        shared_down = sem("shared_down")
        logit_psum = sem("logit_psum")
        logit_ready = sem("logit_ready")
        gate_ready = sem("gate_ready")
        combine_ready = sem("combine_ready")
        xl_ready = sem("xl_ready")
        spread_ready = sem("spread_ready")
        c_cast = sem("c_cast")
        c_left = sem("c_left")
        c_psum = sem("c_psum")
        c_ready = sem("c_ready")
        w_split = sem("w_split")
        hh_ready = sem("hh_ready")
        hl_ready = sem("hl_ready")
        moe_zero = sem("moe_zero")
        exp_loaded = [sem(f"exp_loaded{u}") for u in range(2)]
        z_psum = sem("z_psum")
        silu_ready = sem("silu_ready")
        cb_psum = sem("cb_psum")
        hid_ready = sem("hid_ready")
        down_done = sem("down_done")
        low_used = sem("low_used")
        acc_done = sem("acc_done")
        accT_ready = sem("accT_ready")
        acc_psum = sem("acc_psum")

        def x_dram(t):
            return t.rearrange("b (t p) d -> p (b t) d", p=P)

        def ready(eng, s, n):
            eng.wait_ge(s, n + (1 + CREDIT))

        def free(eng, s, n, buffers=2):
            eng.wait_ge(s, n + (1 + CREDIT - buffers))

        def casts_done(g, i):
            return (max(1, 3 * g), 3 * g + 2, min(3 * g + 4, 3 * G))[i]

        def logits1(g):
            return wide[2 + g % 2][:].rearrange("p (b e) -> p b e", b=2)[:, :, 0:2 * NE]

        block = ctx.enter_context(nc.Block())

        @block.sync
        def _(sp):
            for g in range(G):
                ts = slice(g * TPG, (g + 1) * TPG)
                sp.dma_start(x[:, ts, :], x_dram(a["x"])[:, ts, :]).then_inc(x_loaded, 16)
            for dst, src in ((wq[:], "wq"), (wk[:], "wk"), (wv[:], "wv"), (wo[:], "wo"), (w_down[:], "w_down"),
                             (w_up[:, 0:D], "w_up_k"), (w_up[:, D:2 * D], "w_up_v")):
                sp.dma_start(dst, a[src]).then_inc(w_loaded, 16)
            for dst, src in ((w_router[:], a["w_router"]), (w_shared[:], a["w_shared"]), (wd_shared[:], a["wd_shared"]),
                             (b_router[:], bass.AP(a["b_router"].tensor, 0, [[0, P], [1, NE]]))):
                sp.dma_start(dst, src).then_inc(w1_loaded, 16)
            sp.dma_start(b_tok[:], bass.AP(a["b_tok"].tensor, 0, [[0, P], [1, 3]])).then_inc(w2_loaded, 16)
            for dst, src in ((w_tok[:], "w_tok"), (m0[:], "m0"), (state[0][:, 0:D], "m0T"),
                             (state[1][:, 0:D], "m0T"), (vg1T[:], "vg1T"), (vg2[:], "vg2"), (vg2T[:], "vg2T")):
                sp.dma_start(dst, a[src]).then_inc(w2_loaded, 16)
            sp.dma_start(w_gate2[:], a["w_gate2"]).then_inc(w3_loaded, 16)

            def load_weights(name, m, u, loaded):
                w = a[name]
                sp.dma_start(w_raw[u][:, 0:w.shape[2]], w[bass.ds(m, 1), :, :].rearrange("m p n -> p (m n)")).then_inc(loaded[u], 16)

            for u in range(2):
                load_weights("w_exp", u, u, exp_loaded)

            def load_stacks(n, u):
                for v in range(2):
                    sp.dma_start(q_stack[v][u][0:PAIRS * HD, :], bass.AP(q_dram[v].tensor, n * (5 * HD * S),
                                                                         [[HD * S, 3], [S, 3 * HD], [1, S]]))\
                        .then_inc(stacks_loaded[u], 16)
                    sp.dma_start(k_stack[v][u][0:PAIRS * HD, :], bass.AP(k_dram[v].tensor, n * (3 * HD * S),
                                                                         [[0, 3], [S, 3 * HD], [1, S]]))\
                        .then_inc(stacks_loaded[u], 16)

            for g in range(G):
                b, o = g // 2, (g % 2) * GW
                if g == 2:
                    sp.wait_ge(parts_saved[0], 16 * 16)
                    sp.wait_ge(parts_saved[1], 16 * 16)
                    sp.wait_ge(stacks_zero, 1)
                    load_stacks(0, 0)
                    load_stacks(1, 1)
                sp.wait_ge(parts_ready, g + 1)
                for w, drams in ((0, q_dram), (2, k_dram)):
                    if w == 2:
                        sp.wait_ge(part_cast, 6 * (g + 1))
                    for v in range(2):
                        rows = drams[v][b * H:(b + 1) * H]
                        for i in range(rows.shape[1]):
                            sp.dma_start(rows[:, i, :, o:o + GW], parts[g % 2][:, w + v, i % 3, :]).then_inc(parts_saved[g % 2], 16)
            for u in range(2):
                sp.wait_ge(parts_saved[u], 2 * 16 * 16)
            sp.wait_ge(flag_ready, 1)
            fast = sp.value_load(flag[0:1, 0:1], min_val=0, max_val=1)
            with sp.If(fast == 1):
                with sp.Fori(0, NH // 2 - 1) as i:
                    for u in range(2):
                        ready(sp, whole, i * (2 * QT) + ((u + 1) * QT - 1))
                        load_stacks(i * 2 + (2 + u), u)
            with sp.Else():
                with sp.Fori(0, NH // 2 - 1) as i:
                    for u in range(2):
                        ready(sp, s_psum, i * (2 * QT) + ((u + 1) * QT - 1))
                        load_stacks(i * 2 + (2 + u), u)

            with sp.Fori(0, MT_N // 2 - 1) as i:
                for u in range(2):
                    sp.wait_ge(w_split, i * 2 + (u + 1))
                    load_weights("w_exp", i * 2 + (2 + u), u, exp_loaded)
            sp.wait_ge(w_split, MT_N)
            for u in range(2):
                load_weights("w_ffn", u, u, ffn_loaded)
            with sp.Fori(0, NE2 - 1) as i:
                for u in range(2):
                    sp.wait_ge(w2_split, i * 2 + (u + 1))
                    load_weights("w_ffn", i * 2 + (2 + u), u, ffn_loaded)
            for g in range(G):
                ts = slice(g * TPG, (g + 1) * TPG)
                sp.wait_ge(x_ready, G * 3 + g + 1)
                sp.dma_start(x_dram(out)[:, ts, :], x[:, ts, :]).then_inc(stored, 16)
            sp.wait_ge(stored, 16 * G)

        @block.gpsimd
        def _(pool):
            link = Link(pool, pool_link)
            link(pool.memset(ident[:], 0.0))
            pool.affine_select(out=ident[:], in_=ident[:], compare_op=ALU.not_equal, fill=1.0, base=0,
                               pattern=[[-1, P]], channel_multiplier=1).then_inc(consts, 1)
            link(pool.memset(half[:], -0.5))
            link(pool.memset(root[:], 0.5))
            link(pool.memset(ones[:], 1.0))
            link(pool.memset(by_half[:], 0.0))
            link.sign(pool.memset(first_half_ones[:], 0.0))
            link(pool.memset(m_norm[:], 0.0))
            link(pool.memset(first_half_ones[0:CH, :], 1.0))
            pool.iota(distance, [[1, TW]], base=-(S - P), channel_multiplier=-1).then_inc(table, 1)
            pool.iota(time, [[1, S]], base=-(S // 2), channel_multiplier=0).then_inc(table, 1)

            def norm(k):
                for g in range(G):
                    ts = slice(g * TPG, (g + 1) * TPG)
                    pool.wait_ge(var_ready, G * k + g + 1)
                    link(pool.tensor_scalar(rstd[:, ts], mv[:, ts, 1], EPS, None, ALU.add))
                    pool.tensor_tensor(rstd[:, ts], rstd[:, ts], half[:, ts], ALU.pow).then_inc(rstd_ready, 1)

            norm(0)
            link(pool.memset(head_ones[:], 1.0))
            link(pool.affine_select(out=head_ones[:], in_=head_ones[:], compare_op=ALU.is_ge, fill=0.0, base=0,
                                    pattern=[[-HD, H]], channel_multiplier=1))
            link(pool.affine_select(out=head_ones[:], in_=head_ones[:], compare_op=ALU.is_ge, fill=0.0, base=HD - 1,
                                    pattern=[[HD, H]], channel_multiplier=-1))
            for u in range(2):
                for v in range(2):
                    link.sign(pool.memset(q_stack[v][u][:], 0.0))
                    link.sign(pool.memset(k_stack[v][u][:], 0.0))
                link(pool.memset(v_cur[u][:], 0.0))
                link.sign(pool.memset(v_cur[u][:, :, HD:HD + 1], 1.0))
            link.sign(pool.memset(evac[1][:], 1.0))
            link.sign(pool.memset(ring[:, 6 * S:8 * S], 0.0))
            link.wait()
            pool.sem_inc(stacks_zero, 1)

            pool.wait_ge(table, 5)
            for g in range(G):
                o = (g % 2) * GW
                pool.wait_ge(k_ready, g + 1)
                for w in range(2):
                    if g:
                        pool.wait_ge(part_cast, 6 * g)
                    pool.tensor_tensor(folded[:, 2 + w, :], qk_f[g % 2][:, 1, :], fold[:, w, o:o + GW], ALU.mult).then_inc(folded_ready, 1)
                for i in range(2):
                    for w in range(2):
                        pool.wait_ge(part_cast, 6 * g + 2 * i + w + 1)
                        pool.tensor_tensor(folded[:, 2 + w, :], folded[:, 2 + w, :], parts[g % 2][:, 2 + w, i, :], ALU.subtract)\
                            .then_inc(folded_ready, 1)
            pool.wait_ge(bound_sq, 1)
            pool.tensor_tensor(bound[0:1, 1:2], bound[0:1, 0:1], root[0:1, 0:1], ALU.pow).then_inc(bound_root, 1)
            pool.wait_ge(flag_ready, 1)
            pool.wait_ge(v_ready, G)
            fast = pool.value_load(flag[0:1, 0:1], min_val=0, max_val=1)

            def take_values(n, u):
                pool.tensor_copy(v_cur[u][:, :, 0:HD], v_flat[:, bass.ds(n * (QT * HD), QT * HD)].rearrange("p (t d) -> p t d", t=QT))\
                    .then_inc(v_loaded, 1)

            with pool.If(fast == 1):
                take_values(0, 0)
                take_values(1, 1)
                with pool.Fori(0, NH // 2 - 1) as i:
                    for u in range(2):
                        pool.wait_ge(pv_done, i * (2 * QT) + ((u + 1) * QT + RING))
                        take_values(i * 2 + (2 + u), u)
            with pool.Else():
                take_values(0, 0)
                take_values(1, 1)
                with pool.Fori(0, NH // 2 - 1) as i:
                    for u in range(2):
                        ready(pool, o_psum, i * (2 * QT) + ((u + 1) * QT - 1))
                        take_values(i * 2 + (2 + u), u)

            link.sign(pool.memset(spread[:], 1.0))
            link.sign(pool.memset(spread2, 1.0))
            link(pool.tensor_copy(ident_b[:], ident[:]))
            for whole_table, e, w in ((spread, 2 * PAIRS_C, EI), (spread2, NE2, P)):
                v = whole_table[:, :].rearrange("p (e w) -> p e w", w=w)
                link(pool.affine_select(out=v, in_=v, compare_op=ALU.is_ge, fill=0.0, base=0,
                                        pattern=[[-3, e], [0, w]], channel_multiplier=1))
                link(pool.affine_select(out=v, in_=v, compare_op=ALU.is_ge, fill=0.0, base=2,
                                        pattern=[[3, e], [0, w]], channel_multiplier=-1))
            pool.sem_inc(spread_ready, 1)

            def split_weights(u, width, done):
                raw = w_raw[u][:, 0:width]
                link(pool.tensor_tensor(wh[u][:, 0:width], raw, across(ones[:, 0:1], width), ALU.mult))
                pool.tensor_tensor(wl[u][:, 0:width], w_raw[u][:, 0:width], wh[u][:, 0:width].bitcast(F32), ALU.subtract)\
                    .then_inc(done, 1)

            pool.wait_ge(o_all, 1)
            link.sign(pool.memset(hid[0], 0.0))
            link(pool.memset(hid[1], 0.0))
            pool.sem_inc(moe_zero, 1)
            norm(1)
            pool.wait_ge(exp_loaded[0], 16)
            split_weights(0, 2 * D, w_split)
            pool.wait_ge(exp_loaded[1], 16)
            pool.wait_ge(low_used, 3 + CREDIT)
            split_weights(1, 2 * D, w_split)
            with pool.Fori(0, MT_N // 2 - 1) as i:
                first = link.n
                link.turn = i * 2
                for u in range(2):
                    pool.wait_ge(exp_loaded[u], i * 16 + 32)
                    pool.wait_ge(low_used, i * (2 * G) + (G * (2 + u) + 1))
                    split_weights(u, 2 * D, w_split)
                assert link.n == first + 2
            link.end_loop(MT_N // 2 - 1, 2)

            norm(2)
            for g in range(G):
                ts = slice(g * TPG, (g + 1) * TPG)
                pool.wait_ge(sq_ready, g + 1)
                pool.tensor_tensor(inv_norm[:, ts], inv_norm[:, ts], root[:, ts], ALU.pow).then_inc(root_ready, 1)
            link.sign(pool.memset(padded[:], -1.0))
            link.sign(pool.memset(taken[:], -1.0))
            pool.wait_ge(acc_done, 1)
            link(pool.memset(c2_rows, 0.0))
            for t in (hh, hl):
                for u in range(2):
                    link.sign(pool.tensor_copy(t[u][:], ring[:, 0:GW]))
            link.wait()
            pool.sem_inc(ffn_zero, 1)
            pool.wait_ge(steps_ready, 1)
            pool.sem_inc(step_ready, CREDIT)
            pool.sem_inc(norm_ready, CREDIT)
            with pool.Fori(0, NCH // 2) as i:
                for u in range(2):
                    n = i * 2 + u
                    free(pool, err_psum[0], n, 1)
                    free(pool, err_psum[1], n, 1)
                    pool.tensor_copy(step[u][:], steps_flat[:, bass.ds(i * (2 * B * 3) + u * (B * 3), B * 3)])\
                        .then_inc(step_ready, 1)
                    ready(pool, norm_sq, n)
                    pool.tensor_tensor(m_norm[:, 2, :], m_norm[:, 1, :], root[:, 0:B], ALU.pow).then_inc(norm_ready, 1)

            norm(3)
            pool.wait_ge(ffn_loaded[0], 16)
            split_weights(0, 3 * D, w2_split)
            pool.wait_ge(ffn_loaded[1], 16)
            pool.wait_ge(low2_used, 3 + CREDIT)
            split_weights(1, 3 * D, w2_split)
            with pool.Fori(0, NE2 - 1) as i:
                first = link.n
                link.turn = i * 2
                for u in range(2):
                    pool.wait_ge(ffn_loaded[u], i * 16 + 32)
                    pool.wait_ge(low2_used, i * (2 * G) + (G * (2 + u) + 1))
                    split_weights(u, 3 * D, w2_split)
                assert link.n == first + 2
            link.end_loop(NE2 - 1, 2)

        @block.scalar
        def _(act):
            link = Link(act, act_link)
            act.wait_ge(table, 2)
            link(act.activation(decay[:], distance, ACT.Abs))
            act.activation(decay[:], decay[:], ACT.Exp, scale=-DECAY).then_inc(table, 1)
            act.activation(unfold[:], distance, ACT.Exp, scale=-DECAY).then_inc(table, 1)
            link(act.activation(fold[:, 0, :], time, ACT.Exp, scale=-DECAY))
            act.activation(fold[:, 1, :], time, ACT.Exp, scale=DECAY).then_inc(table, 1)

            def norm(k):
                for g in range(G):
                    n = G * k + g
                    act.wait_ge(xnT_psum, n + 1)
                    cols = slice(g * GW, (g + 1) * GW)
                    if k % 2:
                        act.activation(xh[:, cols], bank(n % 2), ACT.Copy)
                    act.activation(xnT[:, cols], bank(n % 2), ACT.Copy).then_inc(xnT_ready, 1)
                    if k == 2:
                        act.wait_ge(xn_ready, n + 1)
                        act.activation(squares[:, cols], xn[:, g * TPG:(g + 1) * TPG, :].rearrange("p t d -> p (t d)"), ACT.Square)\
                            .then_inc(squares_ready, 1)

            def cast(g, i):
                if g >= 2 and i == 0:
                    act.wait_ge(parts_saved[g % 2], 16 * 16)
                for w in range(2):
                    act.wait_ge(folded_ready, 6 * g + 2 * i + w + 1)
                    act.activation(parts[g % 2][:, 2 + w, i, :], folded[:, 2 + w, :], ACT.Copy).then_inc(part_cast, 1)

            norm(0)
            for g in range(G):
                act.wait_ge(kv_psum, g + 1)
                act.activation(kvT, bank(3), ACT.Copy).then_inc(kv_ready, 1)
                act.wait_ge(q_psum, g + 1)
                if g >= 2:
                    act.wait_ge(parts_ready, g - 1)
                    act.wait_ge(folded_ready, 6 * (g - 1))
                act.activation(qk_f[g % 2][:, 0, :], bank(2), ACT.Copy, scale=SCALE).then_inc(q_ready, 1)
                if g:
                    cast(g - 1, 0)
                act.wait_ge(lat_psum, g + 1)
                act.activation(latT, bank(4)[0:LAT, :], ACT.Copy).then_inc(lat_ready, 1)
                act.wait_ge(k_psum, g + 1)
                act.activation(qk_f[g % 2][:, 1, :], bank(5), ACT.Copy).then_inc(k_ready, 1)
                if g:
                    cast(g - 1, 1)
                act.wait_ge(v_psum, g + 1)
                b, t0 = g // 2, (g % 2) * TPG
                for t in range(TPG):
                    ins = act.activation(v_heads[:, b * H:(b + 1) * H, t0 + t, :],
                                         bank(6)[:, t * P:(t + 1) * P].rearrange("p (h d) -> p h d", h=H), ACT.Copy)
                ins.then_inc(v_ready, 1)
                act.wait_ge(k_ready, g + 1)
                if g:
                    act.wait_ge(sq_psum, 2 * g)
                for w in range(2):
                    act.activation(qk_sq[:, w, :], qk_f[g % 2][:, w, :], ACT.Square,
                                   accum_out=qk_sums[:, w * G + g:w * G + g + 1]).then_inc(qk_sq_ready, 1)
                if g:
                    cast(g - 1, 2)
            for i in range(3):
                cast(G - 1, i)

            act.wait_ge(parts_saved[0], 2 * 16 * 16)
            act.wait_ge(flag_ready, 1)
            fast = act.value_load(flag[0:1, 0:1], min_val=0, max_val=1)
            with act.If(fast == 1):
                act.sem_inc(exp_done, CREDIT)
                with act.Fori(0, NH // 2) as i:
                    for c in range(2 * QT):
                        n = i * (2 * QT) + c
                        ready(act, corner_done, n)
                        ready(act, whole, n)
                        act.wait_ge(pv_done, n + 1)
                        act.activation(ring[:, c % RING * S:(c % RING + 1) * S], wide[c % 2][:], ACT.Exp,
                                       bias=minus_bound[:]).then_inc(exp_done, 1)
            with act.Else():
                act.sem_inc(exp_ready, CREDIT)
                act.sem_inc(prT_ready, CREDIT)
                with act.Fori(0, NH // 2) as i:
                    for c in range(2 * QT + 1):
                        if c < 2 * QT:
                            n = i * (2 * QT) + c
                            ready(act, max_ready, n)
                            free(act, prT_psum, n)
                            free(act, o_ready, n)
                            act.activation(pr[c % 2], sc[c % 2], ACT.Exp, bias=row[:, c % 2, 1:2],
                                           accum_out=row[:, c % 2, 2:3]).then_inc(exp_ready, 1)
                        if c >= 1:
                            n = i * (2 * QT) + (c - 1)
                            ready(act, prT_psum, n)
                            free(act, o_psum, n)
                            act.activation(prT[(c - 1) % 2], wide[2][:], ACT.Copy).then_inc(prT_ready, 1)

            for g in range(G):
                act.wait_ge(oT_psum, g + 1)
                act.activation(oT[:, g * GW:(g + 1) * GW], bank(g % 2), ACT.Copy).then_inc(oT_ready, 1)

            norm(1)
            for g in range(G):
                ts = slice(g * TPG, (g + 1) * TPG)
                act.wait_ge(logit_ready, g + 1)
                act.activation(gates[:, ts, :], gates[:, ts, :], ACT.Sigmoid).then_inc(gate_ready, 1)
            def cast_weights(g, i):
                if i == 0:
                    act.wait_ge(combine_ready, g + 1)
                    if g >= 2:
                        act.wait_ge(c_psum, g - 1)
                else:
                    act.wait_ge(c_left, 2 * g + i)
                act.activation(c_tok_parts[g % 2][:, :, :, i], rest[g % 2][:, :, :], ACT.Copy).then_inc(c_cast, 1)

            for g in range(G):
                if g == 2:
                    cast_weights(0, 0)
                act.wait_ge(shared_psum, g + 1)
                if g >= 2:
                    act.wait_ge(shared_down, g - 1)
                if g < 2:
                    act.wait_ge(moe_zero, 1)
                act.activation(act_out[g % 2][0:EI], bank(4 + g % 2)[0:EI, :], ACT.Silu).then_inc(shared_act, 1)
            for g in range(G + 1):
                if 1 <= g < G:
                    cast_weights(g, 0)
                    cast_weights(g - 1, 2)
                if g < G:
                    cast_weights(g, 1)
                if g == G - 1:
                    cast_weights(g, 2)
                if g >= 1:
                    for k in range(NCHUNK if g < G - 1 else NCHUNK // 2):
                        act.wait_ge(c_psum, g)
                        act.activation(c_rows[0:3 * CE, k * T + (g - 1) * GW:k * T + g * GW],
                                       bank(4 + k).bitcast(BF16)[0:3 * CE, 0:GW], ACT.Copy).then_inc(c_ready, 1)
            act.sem_inc(silu_ready, CREDIT)
            act.sem_inc(hh_ready, CREDIT - 1)

            def high_part(n, c, weighted, done, split):
                ready(act, weighted, n - 1)
                act.wait_ge(done, n + CREDIT)
                act.activation(hh[(c - 1) % 2][:], hid[(c - 1) % 2], ACT.Copy).then_inc(split, 1)

            with act.Fori(0, MT_N // 2) as i:
                for c in range(2 * G):
                    n = i * (2 * G) + c
                    ready(act, z_psum, n)
                    free(act, hid_ready, n)
                    act.activation(act_out[c % 2], bank(4 + c % 2), ACT.Silu).then_inc(silu_ready, 1)
                    high_part(n, c, hid_ready, down_done, hh_ready)
            high_part(MT_N * G, 0, hid_ready, down_done, hh_ready)
            for g in range(G):
                act.wait_ge(acc_done, 1)
                act.activation(accT[:, g * GW:(g + 1) * GW], bank(g), ACT.Copy).then_inc(accT_ready, 1)

            act.wait_ge(fold_psum, 1)
            link(act.activation(vg2_cat[:, 0:D], vg2T[:], ACT.Copy, scale=1.0 / CH))
            act.activation(vg2_cat[:, D:2 * D], bank(2)[:, 0:D], ACT.Copy, scale=1.0 / CH).then_inc(fold_ready, 1)
            for b in range(B):
                act.activation(state[b][:, D:2 * D], bank(2)[:, D:2 * D], ACT.Copy).then_inc(fold_ready, 1)
            norm(2)
            act.wait_ge(tok_psum, G)
            for k in range(2):
                act.activation(tok[:, :, k], bank(3)[:, 0:2 * NT].rearrange("p (t k) -> p t k", k=2)[:, :, k], ACT.Sigmoid,
                               bias=b_tok[:, k:k + 1]).then_inc(tok_ready, 1)
            act.wait_ge(gate_psum, 1)
            act.activation(by_chunk[:, 0, :], bank(5)[:, 0:B * NCH], ACT.Sigmoid, bias=b_tok[:, 2:3]).then_inc(gate_row, 1)
            for b in range(B):
                act.sem_inc(mz_silu[b], CREDIT)
                act.sem_inc(out_copied[b], CREDIT)
            with act.Fori(0, NCH // 2) as i:
                for u in range(2):
                    n = i * 2 + u
                    ready(act, scale_ready, n)
                    for b in range(B):
                        ready(act, mz_psum[b], n)
                        act.activation(silu_z[b][:], bank(b)[:, 0:CH], ACT.Silu, scale=m_norm[:, 3, b:b + 1],
                                       accum_out=h_sum[b][:]).then_inc(mz_silu[b], 1)
                    for b in range(B):
                        ready(act, out_taken[b], n)
                        act.activation(memT[:, bass.ds(i * (2 * CH) + (b * S + u * CH), CH)], out_sum[b][:],
                                       ACT.Copy).then_inc(out_copied[b], 1)

            norm(3)
            act.wait_ge(shifted, 1)
            act.activation(soft[:], soft[:], ACT.Exp).then_inc(exp2_ready, 1)
            act.wait_ge(c2T_psum, 1)
            act.activation(c2_rows[0:3 * NE2, :], wide[2][:].bitcast(BF16)[0:3 * NE2, :], ACT.Copy).then_inc(c2T_ready, 1)
            act.sem_inc(silu2_ready, CREDIT)
            act.sem_inc(hh2_ready, CREDIT - 1)
            with act.Fori(0, NE2) as i:
                for c in range(2 * G):
                    n = i * (2 * G) + c
                    ready(act, gate_z, n)
                    free(act, gated_ready, n)
                    act.activation(act_out[c % 2], bank(4), ACT.Silu).then_inc(silu2_ready, 1)
                    high_part(n, c, hid2_ready, down2_done, hh2_ready)
            high_part(FT_N * G, 0, hid2_ready, down2_done, hh2_ready)
            for g in range(G):
                act.wait_ge(acc2_done, 1)
                act.activation(accT[:, g * GW:(g + 1) * GW], bank(g), ACT.Copy).then_inc(accT2_ready, 1)

        @block.tensor
        def _(pe):
            pe.wait_ge(consts, 1)

            def norm(k, read_group=None):
                for g in range(G):
                    n = G * k + g
                    pe.wait_ge(xn_ready, n + 1)
                    if g >= 2:
                        pe.wait_ge(xnT_ready, n - 1)
                    for t in range(TPG):
                        ins = pe.transpose(bank(n % 2)[:, t * P:(t + 1) * P], xn[:, g * TPG + t, :], ident[:])
                    ins.then_inc(xnT_psum, 1)
                    if read_group and g:
                        read_group(g - 1)
                if read_group:
                    read_group(G - 1)

            def squares_of(g):
                if g == 0:
                    pe.wait_ge(stacks_zero, 1)
                for w in range(2):
                    pe.wait_ge(qk_sq_ready, 2 * g + w + 1)
                    if g:
                        pe.wait_ge(sq_taken, 2 * (g - 1) + w + 1)
                    pe.matmul(bank(7 * w)[0:H, :], head_ones[:], qk_sq[:, w, :], start=True, stop=True).then_inc(sq_psum, 1)

            norm(0)
            pe.wait_ge(w_loaded, 7 * 16)
            for g in range(G):
                cols = xnT[:, g * GW:(g + 1) * GW]
                pe.wait_ge(xnT_ready, g + 1)
                if g:
                    pe.wait_ge(kv_ready, g)
                pe.matmul(bank(3), wk[:], cols, start=True, stop=False)
                pe.matmul(bank(3), wv[:], cols, start=False, stop=True).then_inc(kv_psum, 1)
                if g:
                    pe.wait_ge(q_ready, g)
                pe.matmul(bank(2), wq[:], cols, start=True, stop=True).then_inc(q_psum, 1)
                if g:
                    squares_of(g - 1)
                pe.wait_ge(kv_ready, g + 1)
                if g:
                    pe.wait_ge(lat_ready, g)
                pe.matmul(bank(4)[0:LAT, :], w_down[:], kvT, start=True, stop=True).then_inc(lat_psum, 1)
                pe.wait_ge(lat_ready, g + 1)
                if g:
                    pe.wait_ge(k_ready, g)
                pe.matmul(bank(5), w_up[:, 0:D], latT, start=True, stop=True).then_inc(k_psum, 1)
                if g:
                    pe.wait_ge(v_ready, g)
                for t in range(TPG):
                    ins = pe.matmul(bank(6)[:, t * P:(t + 1) * P], latT[:, t * P:(t + 1) * P], w_up[:, D:2 * D],
                                    start=True, stop=True)
                ins.then_inc(v_psum, 1)
            squares_of(G - 1)

            pe.matmul(bank(6)[0:1, 0:2 * G], ones[:, 0:1], qk_sums[:], start=True, stop=True).then_inc(bound_psum, 1)
            pe.wait_ge(bound_part, 1)
            pe.transpose(bank(5)[0:1, 0:H], bound[0:H, 4:5], ident[0:H, 0:H]).then_inc(bound_psum, 1)
            pe.wait_ge(bound_root, 1)
            pe.matmul(bank(4)[:, 0:1], ones[0:1, :], bound[0:1, 1:2], start=True, stop=True).then_inc(bound_psum, 1)

            pe.wait_ge(stacks_zero, 1)
            pe.wait_ge(flag_ready, 1)
            fast = pe.value_load(flag[0:1, 0:1], min_val=0, max_val=1)
            with pe.If(fast == 1):
                pe.sem_inc(first_half, CREDIT)
                pe.sem_inc(whole, CREDIT)
                pe.sem_inc(pv_done, RING)
                pe.sem_inc(evacT_psum, CREDIT)

                def scores(i, c):
                    n, u, k = i * (2 * QT) + c, c // QT % 2, c % QT
                    free(pe, exp_done, n)
                    keys = slice(k * P, (k + 1) * P)
                    if k == 0:
                        pe.wait_ge(stacks_loaded[u], i * 64 + 64 * (1 + c // (2 * QT)))
                    for j, h in enumerate((k // 4, 1 - k // 4)):
                        lo, hi, mid = h * 512, (h + 1) * 512, min(max(k * P, h * 512), (h + 1) * 512)
                        if mid > lo:
                            ins = pe.matmul(wide[c % 2][:, lo:mid], k_stack[0][u][:, keys], q_stack[1][u][:, lo:mid],
                                            start=True, stop=True)
                        if hi > mid:
                            ins = pe.matmul(wide[c % 2][:, mid:hi], k_stack[1][u][:, keys], q_stack[0][u][:, mid:hi],
                                            start=True, stop=True)
                        ins.then_inc((first_half, whole)[j], 1)

                def products(i, c):
                    u = c // QT
                    ready(pe, exp_done, i * (2 * QT) + c)
                    if c % QT == 1:
                        ready(pe, v_loaded, i * 2 + (u - CREDIT))
                        ready(pe, evac_ready, i * 2 + (u - 1))
                    for done_step in (c - 1, c):
                        at_ring = done_step % RING * S
                        for h in range(2):
                            at = 32 * (2 * (done_step % 2) + h)
                            ins = pe.matmul(bank(4 + u)[at:at + 32, :], v_cur[u][:, done_step % QT, :],
                                            ring[:, at_ring + h * 512:at_ring + (h + 1) * 512],
                                            start=(done_step % QT < 2), stop=(done_step % QT >= QT - 2), skip_group_check=True)
                        ins.then_inc(pv_done, 1)

                def turn(n, u, half_):
                    if half_ == 0:
                        ready(pe, evac_ready, n)
                        free(pe, head_ready, n)
                    for t in range(2 * half_, 2 * half_ + 2):
                        ins = pe.transpose(bank(6 + u)[:, t * P:(t + 1) * P], evac[1 - u][:, t * P:(t + 1) * P], ident[:])
                    if half_ == 1:
                        ins.then_inc(evacT_psum, 1)

                def body(i, last):
                    for c in range(2 * QT):
                        if not last or c + 2 < 2 * QT:
                            scores(i, c + 2)
                        if c % 2:
                            products(i, c)
                        if c % QT in (2, 4):
                            turn(i * 2 + c // QT, c // QT, c % QT // 2 - 1)

                scores(0, 0)
                scores(0, 1)
                with pe.Fori(0, NH // 2 - 1) as i:
                    body(i, False)
                body(NH // 2 - 1, True)
                for half_ in range(2):
                    turn(NH, 0, half_)
            with pe.Else():
                pe.sem_inc(s_psum, CREDIT)
                pe.sem_inc(prT_psum, CREDIT)
                pe.sem_inc(o_psum, CREDIT)
                with pe.Fori(0, NH // 2) as i:
                    for c in range(2 * QT + 2):
                        if c < 2 * QT:
                            n, u, q = i * (2 * QT) + c, c // QT, c % QT
                            if q == 0:
                                pe.wait_ge(stacks_loaded[u], i * 64 + 64)
                            free(pe, s_clamped, n)
                            for k in range(S // 512):
                                ins = pe.matmul(wide[c % 2][:, k * 512:(k + 1) * 512], q_stack[0][u][:, q * P:(q + 1) * P],
                                                k_stack[1][u][:, k * 512:(k + 1) * 512], start=True, stop=True)
                            ins.then_inc(s_psum, 1)
                        if 1 <= c < 2 * QT + 1:
                            n = i * (2 * QT) + (c - 1)
                            ready(pe, exp_ready, n)
                            free(pe, prT_ready, n, 1)
                            for k in range(QT):
                                ins = pe.transpose(wide[2][:, k * P:(k + 1) * P], pr[(c - 1) % 2][:, k * P:(k + 1) * P], ident[:])
                            ins.then_inc(prT_psum, 1)
                        if c >= 2:
                            n, u = i * (2 * QT) + (c - 2), (c - 2) // QT
                            if c % QT == 2:
                                pe.wait_ge(v_loaded, i * 2 + (u + 1))
                            ready(pe, prT_ready, n)
                            free(pe, o_ready, n)
                            for k in range(QT):
                                ins = pe.matmul(bank(6 + c % 2)[:, 0:HD], prT[c % 2][:, k * P:(k + 1) * P],
                                                v_cur[u][:, k, 0:HD], start=(k == 0), stop=(k == QT - 1))
                            ins.then_inc(o_psum, 1)
            pe.wait_ge(o_all, 1)
            for g in range(G):
                b, q0 = g // 2, (g % 2) * TPG
                if g >= 2:
                    pe.wait_ge(oT_ready, g - 1)
                for t in range(TPG):
                    ins = pe.transpose(bank(g % 2)[:, t * P:(t + 1) * P],
                                       o_heads[:, q0 + t, 1 + b * H:1 + (b + 1) * H, :].rearrange("p n d -> p (n d)"), ident[:])
                ins.then_inc(oT_psum, 1)
            for g in range(G):
                pe.wait_ge(oT_ready, g + 1)
                if g >= 2:
                    pe.wait_ge(x_ready, g - 1)
                for t in range(TPG):
                    ins = pe.matmul(bank(2 + g % 2)[:, t * P:(t + 1) * P], oT[:, g * GW + t * P:g * GW + (t + 1) * P], wo[:],
                                    start=True, stop=True)
                ins.then_inc(y_psum, 1)

            def shared_sum(g):
                pe.wait_ge(shared_act, g + 1)
                pe.matmul(bank(g), wd_shared[:], act_out[g % 2][0:EI], start=True, stop=False, skip_group_check=True)\
                    .then_inc(shared_down, 1)

            pe.wait_ge(w1_loaded, 4 * 16)

            def router_logits(g):
                pe.wait_ge(xnT_ready, G + g + 1)
                if g >= 2:
                    pe.wait_ge(logit_ready, g - 1)
                for t in range(TPG):
                    ins = pe.matmul(logits1(g)[:, t // 2, t % 2 * NE:(t % 2 + 1) * NE], xnT[:, (g * TPG + t) * P:(g * TPG + t + 1) * P],
                                    w_router[:], start=True, stop=True)
                ins.then_inc(logit_psum, 1)

            norm(1, router_logits)
            for g in range(G):
                if g >= 2:
                    pe.wait_ge(shared_act, g - 1)
                if g == 0:
                    pe.wait_ge(logit_ready, G)
                pe.matmul(bank(4 + g % 2)[0:EI, :], w_shared[:], xnT[:, g * GW:(g + 1) * GW], start=True, stop=True)\
                    .then_inc(shared_psum, 1)
                if g:
                    shared_sum(g - 1)
            shared_sum(G - 1)
            for g in range(G):
                pe.wait_ge(c_cast, casts_done(g, 2))
                if g == 0:
                    pe.wait_ge(shared_act, G)
                    pe.wait_ge(logit_ready, G)
                if g:
                    pe.wait_ge(c_ready, NCHUNK * g)
                for t in range(TPG):
                    for k in range(NCHUNK):
                        ins = pe.transpose(bank(4 + k).bitcast(BF16)[0:3 * CE, t * P:(t + 1) * P],
                                           c_tok[g % 2][:, t, k * 3 * CE:(k + 1) * 3 * CE], ident_b[:])
                ins.then_inc(c_psum, 1)
            pe.wait_ge(moe_zero, 1)
            pe.wait_ge(spread_ready, 1)
            pe.wait_ge(c_ready, G * NCHUNK)
            pe.wait_ge(xl_ready, G)
            for opened in (z_psum, cb_psum, down_done, low_used):
                pe.sem_inc(opened, CREDIT)

            def three(out_, w, x_, stop, start=True):
                for k, (i, j) in enumerate(((0, 0), (1, 0), (0, 1))):
                    ins = pe.matmul(out_, w[i], x_[j], start=start and k == 0, stop=stop and k == 2,
                                    skip_group_check=not start)
                return ins

            def down_low(done_step, at, n, ready_low):
                pe.wait_ge(ready_low, n + 4)
                return pe.matmul(bank(done_step % G), wh[done_step // G % 2][:, at:at + D], hl[done_step % 2][:], start=False, stop=False,
                                 skip_group_check=True)

            def down_high(done_step, at, n, ready_high):
                ready(pe, ready_high, n)
                for w in (wh, wl):
                    ins = pe.matmul(bank(done_step % G), w[done_step // G % 2][:, at:at + D], hh[done_step % 2][:], start=False, stop=False,
                                    skip_group_check=True)
                return ins

            with pe.Fori(0, NCHUNK) as j:
                with pe.Fori(0, PAIRS_C // 2) as i:
                    for c in range(2 * G):
                        n, u, g = j * (PAIRS_C * G) + i * (2 * G) + c, c // G, c % G
                        cols = slice(g * GW, (g + 1) * GW)
                        if g == 0:
                            pe.wait_ge(w_split, j * PAIRS_C + i * 2 + (u + 1))
                        free(pe, silu_ready, n)
                        three(bank(4 + c % 2), (wh[u][:, 0:D], wl[u][:, 0:D]), (xh[:, cols], xl[:, cols]), True)\
                            .then_inc(z_psum, 1)
                        down_low((c - 3) % (2 * G), D, n - 3, hl_ready).then_inc(low_used, 1)
                        free(pe, hid_ready, n)
                        pe.matmul(bank(6 + c % 2), spread[0:3 * CE, bass.ds(i * (2 * P) + u * P, P)],
                                  c_rows[0:3 * CE, bass.ds(j * T + g * GW, GW)], start=True, stop=True).then_inc(cb_psum, 1)
                        down_high((c - 2) % (2 * G), D, n - 2, hh_ready).then_inc(down_done, 1)
            for c in range(2):
                down_low(2 * G - 3 + c, D, MT_N * G - 3 + c, hl_ready).then_inc(low_used, 1)
                down_high(2 * G - 2 + c, D, MT_N * G - 2 + c, hh_ready).then_inc(down_done, 1)
            down_low(2 * G - 1, D, MT_N * G - 1, hl_ready).then_inc(acc_done, 1)
            for g in range(G):
                pe.wait_ge(accT_ready, g + 1)
                for t in range(TPG):
                    ins = pe.transpose(bank(4 + g)[:, t * P:(t + 1) * P], accT[:, g * GW + t * P:g * GW + (t + 1) * P], ident[:])
                ins.then_inc(acc_psum, 1)

            pe.wait_ge(w2_loaded, 8 * 16)
            pe.matmul(bank(2)[:, 0:D], vg2[:], vg1T[:], start=True, stop=True)
            pe.matmul(bank(2)[:, D:2 * D], m0[:], vg1T[:], start=True, stop=True).then_inc(fold_psum, 1)

            def token_scalars(g):
                pe.wait_ge(xnT_ready, 2 * G + g + 1)
                for t in range(g * TPG, (g + 1) * TPG):
                    ins = pe.matmul(bank(3)[:, 2 * t:2 * t + 2], xnT[:, t * P:(t + 1) * P], w_tok[:, 0:2], start=True, stop=True)
                ins.then_inc(tok_psum, 1)

            norm(2, token_scalars)
            pe.wait_ge(x_ready, 2 * G)
            for g in range(G):
                pe.wait_ge(by_half_ready, g + 1)
                for t in range(g * TPG, (g + 1) * TPG):
                    ins = pe.matmul(bank(4)[:, 2 * t:2 * t + 2], xn[:, t, :], by_half[:, t, :], start=True, stop=True)
            ins.then_inc(km_psum, 1)
            pe.wait_ge(tok_ready, 2)
            flat = tok[:, :, :].rearrange("p t k -> p (t k)")
            pe.matmul(bank(6)[:, 0:2 * NT], first_half_ones[:], flat, start=True, stop=True)
            pe.matmul(bank(6)[:, 2 * NT:4 * NT], ones[:], flat, start=True, stop=True).then_inc(tok_sums, 1)
            pe.wait_ge(km_ready, 1)
            pe.matmul(bank(5)[:, 0:B * NCH], across(w_tok[:, 2:3], P), k_mean[:], start=True, stop=True).then_inc(gate_psum, 1)
            pe.wait_ge(steps_ready, 1)
            pe.wait_ge(fold_ready, 1 + B)
            for b in range(B):
                pe.sem_inc(mz_psum[b], CREDIT)
                pe.sem_inc(old_psum[b], CREDIT)
                pe.sem_inc(err_psum[b], CREDIT)
                pe.sem_inc(out_psum[b], CREDIT)
            pe.sem_inc(norm_psum, CREDIT)
            with pe.Fori(0, NCH // 2) as i:
                for u in range(2):
                    n = i * 2 + u
                    chunk = [xnT[:, bass.ds(i * (2 * CH) + (b * S + u * CH), CH)] for b in range(B)]
                    for b in range(B):
                        free(pe, state_ready[b], n, 1)
                        pe.matmul(bank(b)[:, 0:CH], state[b][:, D:2 * D], chunk[b], start=True, stop=True).then_inc(mz_psum[b], 1)
                    free(pe, rows_ready, n, 1)
                    pe.matmul(bank(6)[:, 256:256 + B], ones[:], m_norm[:, 0, :], start=True, stop=True).then_inc(norm_psum, 1)
                    ready(pe, step_ready, n)
                    for b in range(B):
                        pe.matmul(bank(2 + b)[:, 0:2 * D], across(step[u][:, 3 * b + 2:3 * b + 3], P), state[b][:],
                                  start=True, stop=True).then_inc(old_psum[b], 1)
                    for b in range(B):
                        free(pe, out_taken[b], n, 1)
                        pe.matmul(bank(4 + b)[:, 0:CH], state[b][:, 0:D], chunk[b], start=True, stop=True)
                    for b in range(B):
                        ready(pe, mz_silu[b], n)
                        pe.matmul(bank(6 + b)[:, 0:2 * D], across(h_sum[b][:], P), vg2_cat[:], start=True, stop=True)\
                            .then_inc(err_psum[b], 1)
                    for b in range(B):
                        pe.matmul(bank(4 + b)[:, CH:2 * CH], vg2T[:], silu_z[b][:], start=True, stop=True).then_inc(out_psum[b], 1)
            for b in range(B):
                ready(pe, out_copied[b], NCH - 1)
            for g in range(G):
                for t in range(TPG):
                    ins = pe.transpose(bank(g)[:, t * P:(t + 1) * P], memT[:, g * GW + t * P:g * GW + (t + 1) * P], ident[:])
                ins.then_inc(mem_psum, 1)

            pe.wait_ge(w3_loaded, 16)

            def router_logits2(g):
                pe.wait_ge(xnT_ready, 3 * G + g + 1)
                for t in range(g * TPG, (g + 1) * TPG):
                    ins = pe.matmul(bank(4)[:, t * NE2:(t + 1) * NE2], xnT[:, t * P:(t + 1) * P], w_gate2[:], start=True, stop=True)
                ins.then_inc(logit2_psum, 1)

            norm(3, router_logits2)
            pe.wait_ge(c2_split, 1)
            for t in range(NT):
                ins = pe.transpose(wide[2][:].bitcast(BF16)[0:3 * NE2, t * P:(t + 1) * P], c2_tok[:, t, :], ident_b[:])
            ins.then_inc(c2T_psum, 1)
            pe.wait_ge(ffn_zero, 1)
            pe.wait_ge(c2T_ready, 1)
            pe.wait_ge(xl_ready, 2 * G)
            for opened in (gate_z, up_z, c2_psum, down2_done, low2_used):
                pe.sem_inc(opened, CREDIT)
            for g in range(G):
                pe.matmul(bank(g), wh[1][:, 2 * D:3 * D], hh[1][:], start=True, stop=False, skip_group_check=True)

            with pe.Fori(0, NE2) as i:
                for c in range(2 * G):
                    n, u, g = i * (2 * G) + c, c // G, c % G
                    cols = slice(g * GW, (g + 1) * GW)
                    if g == 0:
                        pe.wait_ge(w2_split, i * 2 + (u + 1))
                    free(pe, silu2_ready, n, 1)
                    three(bank(4), (wh[u][:, 0:D], wl[u][:, 0:D]), (xh[:, cols], xl[:, cols]), True).then_inc(gate_z, 1)
                    down_low((c - 3) % (2 * G), 2 * D, n - 3, hl2_ready).then_inc(low2_used, 1)
                    free(pe, gated_ready, n, 1)
                    three(bank(5), (wh[u][:, D:2 * D], wl[u][:, D:2 * D]), (xh[:, cols], xl[:, cols]), True).then_inc(up_z, 1)
                    free(pe, hid2_ready, n, 1)
                    pe.matmul(bank(6), spread2[:, bass.ds(i * P, P)], c2_rows[:, cols], start=True, stop=True).then_inc(c2_psum, 1)
                    down_high((c - 2) % (2 * G), 2 * D, n - 2, hh2_ready).then_inc(down2_done, 1)
            for c in range(2):
                down_low(2 * G - 3 + c, 2 * D, FT_N * G - 3 + c, hl2_ready).then_inc(low2_used, 1)
                down_high(2 * G - 2 + c, 2 * D, FT_N * G - 2 + c, hh2_ready).then_inc(down2_done, 1)
            down_low(2 * G - 1, 2 * D, FT_N * G - 1, hl2_ready).then_inc(acc2_done, 1)
            for g in range(G):
                pe.wait_ge(accT2_ready, g + 1)
                for t in range(TPG):
                    ins = pe.transpose(bank(4 + g)[:, t * P:(t + 1) * P], accT[:, g * GW + t * P:g * GW + (t + 1) * P], ident[:])
                ins.then_inc(acc2_psum, 1)

        @block.vector
        def _(dve):
            link = Link(dve, dve_link)

            def norm(k):
                for g in range(G + 1):
                    if g < G:
                        tiles = range(g * TPG, (g + 1) * TPG)
                        if k == 0:
                            dve.wait_ge(x_loaded, 16 * G)
                        else:
                            dve.wait_ge(x_ready, G * (k - 1) + g + 1)
                        for t in tiles:
                            link.sign(dve.bn_stats(stats[:, t, :], x[:, t, :]))
                        link.wait()
                        for t in tiles:
                            ins = dve.bn_aggr(mv[:, t, :], stats[:, t, :])
                            if t < tiles[-1]:
                                link.sign(ins)
                        link.wait()
                        ins.then_inc(var_ready, 1)
                    if g >= 1:
                        tiles = range((g - 1) * TPG, g * TPG)
                        dve.wait_ge(rstd_ready, G * k + g)
                        for t in tiles:
                            ins = dve.tensor_scalar(xn[:, t, :], x[:, t, :], mv[:, t, 0:1], rstd[:, t:t + 1], ALU.subtract, ALU.mult)
                            if t < tiles[-1]:
                                link.sign(ins)
                        link.wait()
                        ins.then_inc(xn_ready, 1)
                if k % 2:
                    for g in range(G):
                        low_x(k, g)

            def low_x(k, g):
                cols = slice(g * GW, (g + 1) * GW)
                dve.wait_ge(xnT_ready, G * k + g + 1)
                dve.tensor_tensor(xl[:, cols], xnT[:, cols], xh[:, cols].bitcast(F32), ALU.subtract).then_inc(xl_ready, 1)

            link(dve.memset(evac[0][:], 0.0))
            for t, width in ((hh, GW), (hl, GW), (wh, 3 * D), (wl, 3 * D)):
                for u in range(2):
                    link.sign(dve.tensor_copy(t[u][:], evac[0][:, 0:width]))
            norm(0)

            def largest_squares(g):
                for w in range(2):
                    dve.wait_ge(sq_psum, 2 * g + w + 1)
                    dve.tensor_reduce(sq_max[:, w * G + g:w * G + g + 1], bank(7 * w)[0:H, :], AX.X, ALU.max).then_inc(sq_taken, 1)

            dve.wait_ge(table, 5)
            for g in range(G):
                o = (g % 2) * GW
                dve.wait_ge(q_ready, g + 1)
                if g:
                    dve.wait_ge(parts_ready, g)
                if g >= 2:
                    dve.wait_ge(parts_saved[g % 2], 16 * 16)
                for w in range(2):
                    link.sign(dve.tensor_tensor(folded[:, w, :], qk_f[g % 2][:, 0, :], fold[:, w, o:o + GW], ALU.mult))
                link.wait()
                for i in range(3):
                    for w in range(2):
                        ins = dve.tensor_copy(parts[g % 2][:, w, i, :], folded[:, w, :])
                        if i < 2 or w == 0:
                            link.sign(ins)
                    link.wait()
                    if i < 2:
                        for w in range(2):
                            link.sign(dve.tensor_tensor(folded[:, w, :], folded[:, w, :], parts[g % 2][:, w, i, :], ALU.subtract))
                        link.wait()
                ins.then_inc(parts_ready, 1)
                if g:
                    largest_squares(g - 1)
            largest_squares(G - 1)
            dve.wait_ge(sq_taken, 2 * G)
            link(dve.tensor_reduce(bound[0:H, 2:4], sq_max[:].rearrange("p (w g) -> p w g", w=2), AX.X, ALU.max))
            dve.tensor_tensor(bound[0:H, 4:5], bound[0:H, 2:3], bound[0:H, 3:4], ALU.mult).then_inc(bound_part, 1)
            dve.wait_ge(bound_psum, 2)
            link(dve.tensor_reduce(bound[0:1, 5:6], bank(6)[0:1, 0:2 * G], AX.X, ALU.add))
            link(dve.tensor_reduce(bound[0:1, 6:7], bank(5)[0:1, 0:H], AX.X, ALU.max))
            dve.scalar_tensor_tensor(bound[0:1, 0:1], bound[0:1, 5:6], 0.0, bound[0:1, 6:7], ALU.mult, ALU.add).then_inc(bound_sq, 1)
            dve.wait_ge(bound_psum, 3)
            link(dve.tensor_scalar(minus_bound[:], bank(4)[:, 0:1], -1.0, None, ALU.mult))
            diagonal = slice(S - P, S)
            link(dve.reciprocal(corner[:], unfold[:, diagonal]))
            link(dve.memset(bank(5), 1.0))
            link(dve.tensor_tensor(corner[:], decay[:, diagonal], corner[:], ALU.mult))
            dve.tensor_scalar(flag[:], bound[0:1, 1:2], BOUND, None, ALU.is_le).then_inc(flag_ready, 1)

            dve.wait_ge(flag_ready, 1)
            fast = dve.value_load(flag[0:1, 0:1], min_val=0, max_val=1)
            with dve.If(fast == 1):
                flink = Link(dve, fast_link)
                dve.sem_inc(corner_done, CREDIT)
                dve.sem_inc(evac_ready, CREDIT)
                dve.sem_inc(head_ready, CREDIT)

                def diagonal_tile(i, c):
                    n, k = i * (2 * QT) + c, c % QT
                    ready(dve, first_half, n)
                    tile = wide[c % 2][:, k * P:(k + 1) * P]
                    dve.tensor_tensor(tile, tile, corner[:], ALU.mult).then_inc(corner_done, 1)

                def evacuate(i, c):
                    u = c // QT
                    n = i * 2 + u
                    dve.wait_ge(pv_done, i * (2 * QT) + (c + RING))
                    free(dve, evacT_psum, n)
                    dve.tensor_copy(evac[1 - u][:], bank(4 + 1 - u)).then_inc(evac_ready, 1)

                def finish(n, u, part):
                    if part == 0:
                        ready(dve, evacT_psum, n)
                        t = bank(6 + u).rearrange("p (t g d) -> p t g d", t=4, g=4)
                        flink(dve.tensor_copy(o_sum[u][:], t[:, :, 0:2, 0:HD + 1]))
                        flink.sign(dve.tensor_tensor(o_sum[u][:], o_sum[u][:], t[:, :, 2:4, 0:HD + 1], ALU.add))
                    elif part == 1:
                        flink.wait()
                        flink.sign(dve.reciprocal(o_inv[:, u, :].rearrange("p (t h) -> p t h", t=4), o_sum[u][:, :, :, HD]))
                    else:
                        flink.wait()
                        for h in range(2):
                            inv = o_inv[:, u, h:QT:2]
                            o_half = o_heads[:, h * 4:(h + 1) * 4, :, :].rearrange("p t n d -> p t (n d)")
                            ins = dve.tensor_tensor(o_half[:, :, bass.ds(n * HD, HD)],
                                                    o_sum[u][:, :, h, 0:HD],
                                                    bass.AP(inv.tensor, inv.offset, [list(inv.ap[0]), list(inv.ap[1]), [0, HD]]), ALU.mult)
                            if h == 0:
                                flink.sign(ins)
                        flink.wait()
                        ins.then_inc(head_ready, 1)

                def body(i, last):
                    for c in range(2 * QT):
                        if not last or c + 2 < 2 * QT:
                            diagonal_tile(i, c + 2)
                        if c % QT == 0:
                            evacuate(i, c)
                        if c % QT >= 5:
                            finish(i * 2 + c // QT, c // QT, c % QT - 5)

                diagonal_tile(0, 0)
                diagonal_tile(0, 1)
                with dve.Fori(0, NH // 2 - 1) as i:
                    flink.turn = i * 8
                    body(i, False)
                assert flink.n == 8
                flink.end_loop(NH // 2 - 1, 8)
                body(NH // 2 - 1, True)
                evacuate(NH // 2, 0)
                for part in range(3):
                    finish(NH, 0, part)
                ready(dve, head_ready, NH)
                dve.sem_inc(o_all, 1)
            with dve.Else():
                slink = Link(dve, slow_link)
                dve.sem_inc(s_clamped, CREDIT)
                dve.sem_inc(max_ready, CREDIT)
                dve.sem_inc(o_ready, CREDIT)
                with dve.Fori(0, NH // 2) as i:
                    per_turn = 2 * QT * 4
                    slink.turn = i * per_turn
                    for c in range(2 * QT + 2):
                        if c < 2 * QT:
                            n, q = i * (2 * QT) + c, c % QT
                            at = S - P - q * P
                            ready(dve, s_psum, n)
                            free(dve, exp_ready, n)
                            dve.tensor_tensor(sc[c % 2], wide[c % 2][:], unfold[:, at:at + S], ALU.mult).then_inc(s_clamped, 1)
                            ready(dve, s_clamped, n)
                            slink(dve.tensor_scalar(sc[c % 2], sc[c % 2], -CLAMP, CLAMP, ALU.max, ALU.min))
                            slink(dve.tensor_tensor(sc[c % 2], sc[c % 2], decay[:, at:at + S], ALU.mult))
                            slink(dve.tensor_reduce(row[:, c % 2, 0:1], sc[c % 2], AX.X, ALU.max))
                            dve.tensor_scalar(row[:, c % 2, 1:2], row[:, c % 2, 0:1], -1.0, None, ALU.mult).then_inc(max_ready, 1)
                        if c >= 2:
                            n, u, q = i * (2 * QT) + (c - 2), (c - 2) // QT, (c - 2) % QT
                            ready(dve, exp_ready, n)
                            slink(dve.reciprocal(row[:, c % 2, 3:4], row[:, c % 2, 2:3]))
                            ready(dve, o_psum, n)
                            o_tile = o_heads[:, q, :, :].rearrange("p n d -> p (n d)")
                            dve.tensor_scalar(o_tile[:, bass.ds((i * 2 + (u + 1)) * HD, HD)], bank(6 + c % 2)[:, 0:HD],
                                              row[:, c % 2, 3:4], None, ALU.mult).then_inc(o_ready, 1)
                    assert slink.n == per_turn
                ready(dve, o_ready, NH * QT - 1)
                dve.sem_inc(o_all, 1)
            for g in range(G):
                ts = slice(g * TPG, (g + 1) * TPG)
                dve.wait_ge(y_psum, g + 1)
                dve.tensor_tensor(x[:, ts, :], x[:, ts, :], bank(2 + g % 2).rearrange("p (t d) -> p t d", t=TPG), ALU.add)\
                    .then_inc(x_ready, 1)

            norm(1)
            dve.wait_ge(w1_loaded, 4 * 16)

            def leave(g, i):
                r = rest[g % 2][:, :, :]
                dve.wait_ge(c_cast, casts_done(g, i))
                dve.tensor_tensor(r, r, c_tok_parts[g % 2][:, :, :, i], ALU.subtract).then_inc(c_left, 1)

            bias4 = bass.AP(b_router[:].tensor, b_router[:].offset, [list(b_router[:].ap[0]), [0, 2], [0, 2], [1, NE]])
            for g in range(G):
                dve.wait_ge(logit_psum, g + 1)
                v = gates[:, g * TPG:(g + 1) * TPG, :].rearrange("p (b t) e -> p b t e", b=2)
                dve.tensor_tensor(v, logits1(g).rearrange("p b (t e) -> p b t e", t=2), bias4, ALU.add).then_inc(logit_ready, 1)
            for g in range(G):
                tiles = range(g * TPG, (g + 1) * TPG)
                ts = slice(g * TPG, (g + 1) * TPG)
                dve.wait_ge(gate_ready, g + 1)
                for t in tiles:
                    link.sign(dve.max(top[:, t, :], gates[:, t, :]))
                link.wait()
                if g >= 2:
                    dve.wait_ge(c_cast, casts_done(g - 2, 2))
                left = rest[g % 2]
                for t in tiles:
                    link.sign(dve.match_replace(left[:, t % TPG, :], top[:, t, :], gates[:, t, :], -1.0))
                if g:
                    leave(g - 1, 0)
                link(dve.tensor_reduce(top_sum[:, ts], top[:, ts, :], AX.X, ALU.add))
                link(dve.tensor_scalar(top_sum[:, ts], top_sum[:, ts], 1e-9, None, ALU.add))
                link(dve.reciprocal(top_inv[:, ts], top_sum[:, ts]))
                link(dve.tensor_scalar(top_inv[:, ts], top_inv[:, ts], -ROUTED, None, ALU.mult))
                link(dve.scalar_tensor_tensor(left[:, :, :], left[:, :, :], 0.0, gates[:, ts, :], ALU.max, ALU.subtract))
                inv = top_inv[:, ts]
                dve.tensor_tensor(left[:, :, :], left[:, :, :],
                                  bass.AP(inv.tensor, inv.offset, [list(inv.ap[0]), list(inv.ap[1]), [0, NE]]), ALU.mult).then_inc(combine_ready, 1)
                if g:
                    leave(g - 1, 1)
            leave(G - 1, 0)
            leave(G - 1, 1)
            for g in range(G - 2, G):
                dve.wait_ge(c_psum, g + 1)
                for k in range(NCHUNK // 2, NCHUNK):
                    dve.tensor_copy(c_rows[0:3 * CE, k * T + g * GW:k * T + (g + 1) * GW],
                                    bank(4 + k).bitcast(BF16)[0:3 * CE, 0:GW]).then_inc(c_ready, 1)
            dve.sem_inc(hid_ready, CREDIT)
            dve.sem_inc(hl_ready, CREDIT)

            def low_part(n, c, high_ready, done, split):
                ready(dve, high_ready, n - 1)
                dve.wait_ge(done, n + (1 + CREDIT))
                dve.tensor_tensor(hl[(c - 1) % 2][:], hid[(c - 1) % 2], hh[(c - 1) % 2][:].bitcast(F32), ALU.subtract).then_inc(split, 1)

            with dve.Fori(0, MT_N // 2) as i:
                for c in range(2 * G):
                    n = i * (2 * G) + c
                    ready(dve, silu_ready, n)
                    ready(dve, cb_psum, n)
                    free(dve, hh_ready, n)
                    dve.wait_ge(hl_ready, n + CREDIT)
                    dve.tensor_tensor(hid[c % 2], act_out[c % 2], bank(6 + c % 2), ALU.mult).then_inc(hid_ready, 1)
                    low_part(n, c, hh_ready, low_used, hl_ready)
            low_part(MT_N * G, 0, hh_ready, low_used, hl_ready)
            for g in range(G):
                ts = slice(g * TPG, (g + 1) * TPG)
                dve.wait_ge(acc_psum, g + 1)
                dve.tensor_tensor(x[:, ts, :], x[:, ts, :], bank(4 + g).rearrange("p (t d) -> p t d", t=TPG), ALU.add)\
                    .then_inc(x_ready, 1)

            norm(2)
            C2 = B * NCH
            for g in range(G):
                ts, cols, cs = slice(g * TPG, (g + 1) * TPG), slice(g * GW, (g + 1) * GW), slice(g * GW // CH, (g + 1) * GW // CH)
                dve.wait_ge(squares_ready, g + 1)
                dve.tensor_reduce(inv_norm[:, ts], squares[:, cols].rearrange("p (t d) -> p t d", t=TPG), AX.X, ALU.add)\
                    .then_inc(sq_ready, 1)
            for g in range(G):
                ts = slice(g * TPG, (g + 1) * TPG)
                dve.wait_ge(root_ready, g + 1)
                link(dve.tensor_scalar(inv_norm[:, ts], inv_norm[:, ts], NORM_EPS, float(CH), ALU.max, ALU.mult))
                link(dve.reciprocal(inv_norm[:, ts], inv_norm[:, ts]))
                link(dve.tensor_copy(by_half[0:CH, ts, 0], inv_norm[0:CH, ts]))
                dve.tensor_copy(by_half[CH:P, ts, 1], inv_norm[CH:P, ts]).then_inc(by_half_ready, 1)
            for g in range(G):
                cols, cs = slice(g * GW, (g + 1) * GW), slice(g * GW // CH, (g + 1) * GW // CH)
                dve.wait_ge(xnT_ready, 2 * G + g + 1)
                link.sign(dve.tensor_reduce(x_mean[:, cs], xnT[:, cols].rearrange("p (c t) -> p c t", t=CH), AX.X, ALU.add))
            dve.wait_ge(tok_sums, 1)
            sums = bank(6)[:, 0:4 * NT].rearrange("p (h t k) -> p h t k", h=2, k=2)
            link(dve.tensor_copy(tok[:, :, :], sums[:, 0, :, :]))
            for r, k in ((1, 0), (2, 1)):
                row_ = by_chunk[:, r, :].rearrange("p (t h) -> p t h", h=2)
                link.sign(dve.tensor_copy(row_[:, :, 0], tok[:, :, k]))
                link.sign(dve.tensor_tensor(row_[:, :, 1], sums[:, 1, :, k], tok[:, :, k], ALU.subtract))
            link.wait()
            rows = [by_chunk[:, k, :] for k in range(4)]
            link(dve.tensor_scalar(rows[2], rows[2], -(1.0 - MIN_DECAY) / CH, 1.0 - MIN_DECAY, ALU.mult, ALU.add))
            dve.wait_ge(km_psum, 1)
            dve.tensor_copy(k_mean[:], bank(4)[:, 0:C2]).then_inc(km_ready, 1)
            dve.wait_ge(km_ready, 1)
            by_step = [steps[:, :, :, k].rearrange("p n b -> p b n") for k in range(3)]
            by_batch = lambda ap: ap.rearrange("p (b n) -> p b n", b=B)
            link(dve.scalar_tensor_tensor(by_step[2], by_batch(x_mean[:]), 1.0 / CH, by_batch(k_mean[:]), ALU.mult, ALU.subtract))
            dve.wait_ge(gate_row, 1)
            link(dve.tensor_tensor(rows[3], rows[2], rows[0], ALU.mult))
            link(dve.tensor_scalar(by_step[0], by_batch(rows[3]), -1.0, 1.0, ALU.mult, ALU.add))
            link(dve.scalar_tensor_tensor(rows[1], rows[1], MAX_LR / CH, rows[0], ALU.mult, ALU.mult))
            dve.tensor_tensor(by_step[1], by_batch(k_mean[:]), by_batch(rows[1]), ALU.mult).then_inc(steps_ready, 1)
            for b in range(B):
                dve.sem_inc(state_ready[b], CREDIT)
                dve.sem_inc(out_taken[b], CREDIT)
            for t in (rows_ready, norm_sq, scale_ready):
                dve.sem_inc(t, CREDIT)
            dve.wait_ge(fold_ready, 1 + B)
            first, per_turn = link.n, 2 * (2 + 4 * B)
            with dve.Fori(0, NCH // 2) as i:
                link.turn = i * per_turn
                for u in range(2):
                    n = i * 2 + u
                    ready(dve, norm_psum, n)
                    dve.tensor_copy(m_norm[:, 1, :], bank(6)[:, 256:256 + B]).then_inc(norm_sq, 1)
                    ready(dve, step_ready, n)
                    for b in range(B):
                        link.sign(dve.tensor_scalar(kept[b], state[b][:], step[u][:, 3 * b:3 * b + 1], None, ALU.mult))
                    link.wait()
                    for b in range(B):
                        ready(dve, old_psum[b], n)
                        link.sign(dve.scalar_tensor_tensor(kept[b], bank(2 + b)[:, 0:2 * D], step[u][:, 3 * b + 1:3 * b + 2],
                                                           kept[b], ALU.mult, ALU.add))
                        if b == 0:
                            ready(dve, norm_ready, n)
                            link(dve.tensor_scalar(m_norm[:, 3, :], m_norm[:, 2, :], 1e-6, None, ALU.add))
                            link(dve.reciprocal(m_norm[:, 3, :], m_norm[:, 3, :]))
                            dve.tensor_scalar(m_norm[:, 3, :], m_norm[:, 3, :], MAX_NORM, 1.0, ALU.mult, ALU.min)\
                                .then_inc(scale_ready, 1)
                    link.wait()
                    ready(dve, scale_ready, n)
                    for b in range(B):
                        link.sign(dve.tensor_scalar(kept[b], kept[b], m_norm[:, 3, b:b + 1], None, ALU.mult))
                    link.wait()
                    for b in range(B):
                        ready(dve, err_psum[b], n)
                        dve.scalar_tensor_tensor(state[b][:], bank(6 + b)[:, 0:2 * D], step[u][:, 3 * b + 1:3 * b + 2],
                                                 kept[b], ALU.mult, ALU.add).then_inc(state_ready[b], 1)
                        ready(dve, state_ready[b], n)
                        ins = dve.tensor_tensor_reduce(m_sq[:, b, :], state[b][:, 0:D], state[b][:, 0:D], 1.0, 0.0,
                                                       ALU.mult, ALU.add, m_norm[:, 0, b:b + 1])
                        if b == B - 1:
                            ins.then_inc(rows_ready, 1)
                    for b in range(B):
                        ready(dve, out_psum[b], n)
                        free(dve, out_copied[b], n, 1)
                        link(dve.tensor_copy(out_sum[b][:], bank(4 + b)[:, CH:2 * CH]))
                        dve.scalar_tensor_tensor(out_sum[b][:], bank(4 + b)[:, 0:CH], m_norm[:, 3, b:b + 1], out_sum[b][:],
                                                 ALU.mult, ALU.add).then_inc(out_taken[b], 1)
                assert link.n - first == per_turn, (link.n - first, per_turn)
            link.end_loop(NCH // 2, per_turn)
            for g in range(G):
                ts = slice(g * TPG, (g + 1) * TPG)
                dve.wait_ge(mem_psum, g + 1)
                dve.tensor_tensor(x[:, ts, :], x[:, ts, :], bank(g).rearrange("p (t d) -> p t d", t=TPG), ALU.add)\
                    .then_inc(x_ready, 1)

            norm(3)

            def by_row(ap, n):
                return bass.AP(ap.tensor, ap.offset, [list(ap.ap[0]), list(ap.ap[1]), [0, n]])

            logits = bank(4)[:, 0:NT * NE2].rearrange("p (t e) -> p t e", t=NT)
            dve.wait_ge(logit2_psum, G)
            link(dve.tensor_reduce(r_max[:], logits, AX.X, ALU.max))
            dve.tensor_tensor(soft[:], logits, by_row(r_max[:], NE2), ALU.subtract).then_inc(shifted, 1)
            dve.wait_ge(exp2_ready, 1)
            link(dve.tensor_reduce(r_sum[:], soft[:], AX.X, ALU.add))
            link(dve.reciprocal(r_sum[:], r_sum[:]))
            link(dve.tensor_tensor(soft[:], soft[:], by_row(r_sum[:], NE2), ALU.mult))
            dve.wait_ge(ffn_zero, 1)
            pairs = soft[:].rearrange("p t (g k) -> p t g k", k=2)
            link(dve.tensor_reduce(padded[:, 0, :, 0:4], pairs, AX.X, ALU.max))

            def mark_two(k):
                for t in range(NT):
                    link.sign(dve.max(best[:, k, t, :], padded[:, k, t, :]))
                link.wait()
                link(dve.tensor_copy(taken[:, k, :, 0:2], best[:, k, :, 0:2]))
                for t in range(NT):
                    link.sign(dve.match_replace(marked[:, k, t, :], taken[:, k, t, :], padded[:, k, t, :], -2.0))
                link.wait()

            mark_two(0)
            link(dve.tensor_scalar(marked[:, 0, :, :], marked[:, 0, :, :], -2.0, None, ALU.is_equal))
            for k in range(2):
                link.sign(dve.tensor_tensor(padded[:, 1, :, k:8:2], soft[:, :, k:8:2], marked[:, 0, :, 0:4], ALU.mult))
            link.wait()
            mark_two(1)
            link(dve.tensor_scalar(marked[:, 1, :, :], marked[:, 1, :, :], -2.0, None, ALU.is_equal))
            link(dve.tensor_tensor(combine2[:], padded[:, 1, :, 0:8], marked[:, 1, :, 0:8], ALU.mult))
            link(dve.tensor_reduce(r_sum[:], best[:, 1, :, 0:2], AX.X, ALU.add))
            link(dve.reciprocal(r_sum[:], r_sum[:]))
            link(dve.tensor_tensor(combine2[:], combine2[:], by_row(r_sum[:], NE2), ALU.mult))
            for k in range(3):
                ins = dve.tensor_copy(c2_tok_parts[:, :, :, k], combine2[:])
                if k < 2:
                    link(ins)
                    link(dve.tensor_tensor(combine2[:], combine2[:], c2_tok_parts[:, :, :, k], ALU.subtract))
            ins.then_inc(c2_split, 1)
            dve.sem_inc(gated_ready, CREDIT)
            dve.sem_inc(hid2_ready, CREDIT)
            dve.sem_inc(hl2_ready, CREDIT)
            with dve.Fori(0, NE2) as i:
                for c in range(2 * G):
                    n = i * (2 * G) + c
                    ready(dve, silu2_ready, n)
                    ready(dve, up_z, n)
                    free(dve, hid2_ready, n)
                    dve.tensor_tensor(gated[c % 2], act_out[c % 2], bank(5), ALU.mult).then_inc(gated_ready, 1)
                    ready(dve, gated_ready, n)
                    ready(dve, c2_psum, n)
                    free(dve, hh2_ready, n)
                    dve.wait_ge(hl2_ready, n + CREDIT)
                    dve.tensor_tensor(hid[c % 2], gated[c % 2], bank(6), ALU.mult).then_inc(hid2_ready, 1)
                    low_part(n, c, hh2_ready, low2_used, hl2_ready)
            low_part(FT_N * G, 0, hh2_ready, low2_used, hl2_ready)
            for g in range(G):
                ts = slice(g * TPG, (g + 1) * TPG)
                dve.wait_ge(acc2_psum, g + 1)
                dve.tensor_tensor(x[:, ts, :], x[:, ts, :], bank(4 + g).rearrange("p (t d) -> p t d", t=TPG), ALU.add)\
                    .then_inc(x_ready, 1)


def kernel(**inputs):
    import concourse.bacc as bacc
    from concourse.bass_utils import run_bass_kernel_spmd as run

    w = {k: np.asarray(v) for k, v in inputs.items()}
    arrays = {
        "x": w["L0_attn_x"], "wq": w["L0_attn_Wq"], "wk": w["L0_attn_Wk"], "wv": w["L0_attn_Wv"], "wo": w["L0_attn_Wo"],
        "w_down": w["L0_attn_W_down_kv"], "w_up_k": w["L0_attn_W_up_k"], "w_up_v": w["L0_attn_W_up_v"],
        "w_router": w["L0_ffn_router_w"].T, "b_router": w["L0_ffn_expert_bias"],
        "w_shared": w["L0_ffn_w_gate_shared"].T, "wd_shared": w["L0_ffn_w_down_shared"].T,
        "w_exp": np.concatenate([w["L0_ffn_w_gate"].reshape(MT_N, P, D).transpose(0, 2, 1),
                                 w["L0_ffn_w_down"].transpose(0, 2, 1).reshape(MT_N, P, D)], axis=2),
        "w_tok": np.stack([w["L1_attn_eta_w"], w["L1_attn_alpha_w"], w["L1_attn_gate_w"]], axis=1),
        "b_tok": np.stack([w["L1_attn_eta_b"], w["L1_attn_alpha_b"], w["L1_attn_gate_b"]], axis=1),
        "m0": w["L1_attn_M_init"], "m0T": w["L1_attn_M_init"].T, "vg1T": w["L1_attn_vg_w1"].T,
        "vg2": w["L1_attn_vg_w2"], "vg2T": w["L1_attn_vg_w2"].T,
        "w_gate2": w["L1_ffn_gate_w"].T,
        "w_ffn": np.concatenate([w["L1_ffn_w13_weight"].reshape(NE2, 2, FI2 // P, P, D)[:, 0].reshape(FT_N, P, D).transpose(0, 2, 1),
                                 w["L1_ffn_w13_weight"].reshape(NE2, 2, FI2 // P, P, D)[:, 1].reshape(FT_N, P, D).transpose(0, 2, 1),
                                 w["L1_ffn_w2_weight"].transpose(0, 2, 1).reshape(FT_N, P, D)], axis=2),
    }
    arrays = {"in_" + k: np.ascontiguousarray(v) for k, v in arrays.items()}
    nc = bacc.Bacc("TRN2", target_bir_lowering=False, num_devices=1)
    a = {k[3:]: nc.dram_tensor(k, v.shape, mybir.dt.from_np(v.dtype), kind="ExternalInput").ap() for k, v in arrays.items()}
    out = nc.dram_tensor("out", (B, S, D), F32, kind="ExternalOutput").ap()
    build(nc, a, out)
    return run(nc, [arrays], core_ids=[0]).results[0]["out"]
```
